# Optimizing a Trainium2 kernel written in Bass

```python
import numpy as np
import jax
import jax.numpy as jnp

def _softmax(x, axis=-1):
    return jax.nn.softmax(x, axis=axis)

def _gelu(x):
    return jax.nn.gelu(x, approximate=True)

def _silu(x):
    return jax.nn.silu(x)

def _sigmoid(x):
    return jax.nn.sigmoid(x)

def _layernorm(x, axis=-1, eps=1e-05):
    m = jnp.mean(x, axis=axis, keepdims=True)
    v = jnp.var(x, axis=axis, keepdims=True)
    return (x - m) / jnp.sqrt(v + eps)

def _scatter_add(tgt, idx, src, axis=0):
    return tgt.at[idx].add(src)

def _segment_sum(src, seg, n):
    return jax.ops.segment_sum(src, seg, n)
kernel_name = 'mk_decoder_postln_d2_seqx_r8_ab7376'

def setup_inputs(seed: int=0):
    np.random.seed(seed)
    _w = jnp.asarray

    def _rec_inputs():
        import jax
        import jax.numpy as jnp
        _rk = jax.random.key(seed)
        x = 0.01048 + 0.1018 * jax.random.normal(jax.random.fold_in(_rk, 1), (4, 256, 256), jnp.float32)
        _lenS = 256 - jax.random.randint(jax.random.fold_in(_rk, 7), (4,), 0, max(1, 256 // 4) + 1, jnp.int32)
        _lenS2 = 256 - jax.random.randint(jax.random.fold_in(_rk, 8), (4,), 0, max(1, 256 // 4) + 1, jnp.int32)
        _ctx_512P = jax.random.normal(jax.random.fold_in(_rk, 11), (4, 16, 64), jnp.float32)
        _ctx_512c = jax.random.dirichlet(jax.random.fold_in(_rk, 511), 0.3 * jnp.ones((16,), jnp.float32), (4, 256))
        _ctx_512t = jnp.einsum('bsk,bkd->bsd', _ctx_512c, _ctx_512P)
        _ctx_512t = _ctx_512t * jax.lax.rsqrt(jnp.mean(jnp.square(_ctx_512t)) + 1e-12) * 0.953939
        ctx_512 = -0.000292821 + 1.00034 * (_ctx_512t + 0.3 * jax.random.normal(jax.random.fold_in(_rk, 611), (4, 256, 64), jnp.float32))
        return (x, ctx_512)
    x, ctx_512 = _rec_inputs()

    def _L0_attn_setup():
        import jax, jax.numpy as jnp
        import numpy as np
        B, T, C, H = (4, 512, 256, 16)
        Dh = C // H

        def _feature_map(x):
            return jax.nn.elu(x) + 1.0
        key = jax.random.key(seed)
        ks = jax.random.split(key, 7)
        s = 0.02
        return {'x': jax.random.normal(ks[0], (B, T, C), dtype=jnp.float32), 'cos': jax.random.uniform(ks[1], (T, Dh), dtype=jnp.float32), 'sin': jax.random.uniform(ks[2], (T, Dh), dtype=jnp.float32), 'Wq': jax.random.normal(ks[3], (C, C), dtype=jnp.float32) * s, 'Wk': jax.random.normal(ks[4], (C, C), dtype=jnp.float32) * s, 'Wv': jax.random.normal(ks[5], (C, C), dtype=jnp.float32) * s, 'Wo': jax.random.normal(ks[6], (C, C), dtype=jnp.float32) * s}
    _L0_attn_all = _L0_attn_setup()
    _L0_attn_in = {k: v for k, v in _L0_attn_all.items() if k in ('cos', 'sin', 'Wq', 'Wk', 'Wv', 'Wo')}
    del _L0_attn_all

    def _L0_xattn_setup():
        import jax, jax.numpy as jnp
        import numpy as np
        LRELU_ALPHA = 0.2
        MASK_VAL = -10000000000.0
        B, N, F_IN = (4, 256, 64)
        H, F_OUT = (8, 32)
        F_HID = H * F_OUT

        def gat_layer(x, adj, W, a_self, a_neigh, b):
            feat = jnp.einsum('nf,hfo->hno', x, W)
            attn_self = jnp.einsum('hno,ho->hn', feat, a_self)
            attn_neigh = jnp.einsum('hno,ho->hn', feat, a_neigh)
            e = attn_self[:, :, None] + attn_neigh[:, None, :]
            e = jax.nn.leaky_relu(e, LRELU_ALPHA)
            e = e + MASK_VAL * (1.0 - adj)[None, :, :]
            alpha = jax.nn.softmax(e, axis=-1)
            out = jnp.einsum('hnm,hmo->hno', alpha, feat) + b[:, None, :]
            out = jnp.transpose(out, (1, 0, 2)).reshape(out.shape[1], -1)
            return jax.nn.elu(out)
        key = jax.random.key(seed)
        ks = jax.random.split(key, 10)
        feats = jax.random.normal(ks[0], (B, N, F_IN), dtype=jnp.float32)
        a = (jax.random.uniform(ks[1], (B, N, N)) < 0.01).astype(jnp.float32)
        adj = jnp.maximum(a, jnp.eye(N, dtype=jnp.float32)[None])
        s0 = 1.0 / np.sqrt(F_IN)
        s1 = 1.0 / np.sqrt(F_HID)
        return {'feats': feats, 'adj': adj, 'W0': jax.random.normal(ks[2], (H, F_IN, F_OUT), dtype=jnp.float32) * s0, 'a_self0': jax.random.normal(ks[3], (H, F_OUT), dtype=jnp.float32) * 0.1, 'a_neigh0': jax.random.normal(ks[4], (H, F_OUT), dtype=jnp.float32) * 0.1, 'b0': jnp.zeros((H, F_OUT), dtype=jnp.float32), 'W1': jax.random.normal(ks[5], (H, F_HID, F_OUT), dtype=jnp.float32) * s1, 'a_self1': jax.random.normal(ks[6], (H, F_OUT), dtype=jnp.float32) * 0.1, 'a_neigh1': jax.random.normal(ks[7], (H, F_OUT), dtype=jnp.float32) * 0.1, 'b1': jnp.zeros((H, F_OUT), dtype=jnp.float32)}
    _L0_xattn_all = _L0_xattn_setup()
    _L0_xattn_in = {k: v for k, v in _L0_xattn_all.items() if k in ('W0', 'a_self0', 'a_neigh0', 'b0', 'W1', 'a_self1', 'a_neigh1', 'b1')}
    del _L0_xattn_all

    def _L0_ffn_setup():
        import jax, jax.numpy as jnp
        import numpy as np
        D_MODEL = 256
        HIDDEN = int(2 * D_MODEL * 4 / 3)

        def ternary_quant(w):
            s = jnp.mean(jnp.abs(w))
            q = jnp.clip(jnp.round(w / s), -1.0, 1.0) * s
            return w + jax.lax.stop_gradient(q - w)
        key = jax.random.key(seed)
        k0, k1, k2, k3 = jax.random.split(key, 4)
        x = jax.random.normal(k0, (4, 512, D_MODEL), dtype=jnp.float32)
        std_in = 1.0 / np.sqrt(D_MODEL)
        std_h = 1.0 / np.sqrt(HIDDEN)
        w1 = jax.random.uniform(k1, (HIDDEN, D_MODEL), jnp.float32, -std_in, std_in)
        w3 = jax.random.uniform(k2, (HIDDEN, D_MODEL), jnp.float32, -std_in, std_in)
        w2 = jax.random.uniform(k3, (D_MODEL, HIDDEN), jnp.float32, -std_h, std_h)
        return {'x': x, 'w1': w1, 'w3': w3, 'w2': w2}
    _L0_ffn_all = _L0_ffn_setup()
    _L0_ffn_in = {k: v for k, v in _L0_ffn_all.items() if k in ('w1', 'w3', 'w2')}
    del _L0_ffn_all

    def _L1_attn_setup():
        import jax, jax.numpy as jnp
        import numpy as np
        import math
        H = 256
        NH = 16
        HD = H // NH
        THETA = 10000.0

        def rotate_half(x):
            x1, x2 = (x[..., :HD // 2], x[..., HD // 2:])
            return jnp.concatenate((-x2, x1), axis=-1)

        def rope_tables(seq_len, dtype):
            inv_freq = 1.0 / THETA ** (np.arange(0, HD, 2, dtype=np.float32) / HD)
            t = np.arange(seq_len, dtype=np.float32)
            freqs = np.einsum('i,j->ij', t, inv_freq)
            emb = np.concatenate((freqs, freqs), axis=-1)
            return (jnp.asarray(np.cos(emb), dtype), jnp.asarray(np.sin(emb), dtype))
        key = jax.random.key(seed)
        ks = jax.random.split(key, 5)
        B, S = (2, 256)
        scale = 1.0 / math.sqrt(H)
        return {'hidden_states': jax.random.normal(ks[0], (B, S, H), jnp.float32), 'Wq': jax.random.normal(ks[1], (H, H), jnp.float32) * scale, 'Wk': jax.random.normal(ks[2], (H, H), jnp.float32) * scale, 'Wv': jax.random.normal(ks[3], (H, H), jnp.float32) * scale, 'Wo': jax.random.normal(ks[4], (H, H), jnp.float32) * scale}
    _L1_attn_all = _L1_attn_setup()
    _L1_attn_in = {k: v for k, v in _L1_attn_all.items() if k in ('Wq', 'Wk', 'Wv', 'Wo')}
    del _L1_attn_all

    def _L1_xattn_setup():
        import jax, jax.numpy as jnp
        import numpy as np
        B, S, L = (2, 128, 128)
        DIM_Q, H, K, D_C, D_CQ, R = (256, 16, 128, 64, 192, 64)

        def _rope_tables(seq_len, dim, dtype):
            inv_freq = 1.0 / 10000.0 ** (jnp.arange(0, dim, 2, dtype=dtype) / dim)
            t = jnp.arange(seq_len, dtype=dtype)
            freqs = t[:, None] * inv_freq[None, :]
            sin = jnp.repeat(jnp.sin(freqs), 2, axis=-1)
            cos = jnp.repeat(jnp.cos(freqs), 2, axis=-1)
            return (sin, cos)

        def _rotate_half(x):
            h = x.shape[-1] // 2
            return jnp.concatenate([-x[..., h:], x[..., :h]], axis=-1)
        key = jax.random.key(seed)
        ks = jax.random.split(key, 8)
        s_in = 1.0 / np.sqrt(DIM_Q)
        s_k = 1.0 / np.sqrt(K)
        s_cq = 1.0 / np.sqrt(D_CQ)
        s_c = 1.0 / np.sqrt(D_C)
        return {'hidden_q': jax.random.normal(ks[0], (B, S, DIM_Q), jnp.float32), 'kv_c': jax.random.normal(ks[1], (B, L, D_C), jnp.float32), 'Wq': jax.random.normal(ks[2], (H * K, DIM_Q), jnp.float32) * s_in, 'w_kc_q': jax.random.normal(ks[3], (H, K, D_CQ), jnp.float32) * s_k, 'w_kc_kv': jax.random.normal(ks[4], (H, K, D_C), jnp.float32) * s_k, 'W_qr': jax.random.normal(ks[5], (H, D_CQ, R), jnp.float32) * s_cq / np.sqrt(R), 'W_kr': jax.random.normal(ks[6], (H, D_C, R), jnp.float32) * s_c, 'Wo': jax.random.normal(ks[7], (DIM_Q, H * K), jnp.float32) * s_k}
    _L1_xattn_all = _L1_xattn_setup()
    _L1_xattn_in = {k: v for k, v in _L1_xattn_all.items() if k in ('Wq', 'w_kc_q', 'w_kc_kv', 'W_qr', 'W_kr', 'Wo')}
    del _L1_xattn_all

    def _L1_ffn_setup():
        import jax, jax.numpy as jnp
        import numpy as np
        TOP_K = 2
        key = jax.random.key(seed)
        ks = jax.random.split(key, 5)
        B, S, D, M, E = (4, 256, 256, 256, 8)
        x = jax.random.normal(ks[0], (B, S, D), dtype=jnp.float32)
        gate_kernel = jax.random.normal(ks[1], (D, E), dtype=jnp.float32) / np.sqrt(D)
        wi_0 = jax.random.normal(ks[2], (E, D, M), dtype=jnp.float32) / np.sqrt(D)
        wi_1 = jax.random.normal(ks[3], (E, D, M), dtype=jnp.float32) / np.sqrt(D)
        wo = jax.random.normal(ks[4], (E, M, D), dtype=jnp.float32) / np.sqrt(M)
        return {'x': x, 'gate_kernel': gate_kernel, 'wi_0': wi_0, 'wi_1': wi_1, 'wo': wo}
    _L1_ffn_all = _L1_ffn_setup()
    _L1_ffn_in = {k: v for k, v in _L1_ffn_all.items() if k in ('gate_kernel', 'wi_0', 'wi_1', 'wo')}
    del _L1_ffn_all
    return {'x': x, 'ctx_512': ctx_512, 'L0_attn_cos': _L0_attn_in['cos'], 'L0_attn_sin': _L0_attn_in['sin'], 'L0_attn_Wq': _L0_attn_in['Wq'], 'L0_attn_Wk': _L0_attn_in['Wk'], 'L0_attn_Wv': _L0_attn_in['Wv'], 'L0_attn_Wo': _L0_attn_in['Wo'], 'L0_xattn_W0': _L0_xattn_in['W0'], 'L0_xattn_a_self0': _L0_xattn_in['a_self0'], 'L0_xattn_a_neigh0': _L0_xattn_in['a_neigh0'], 'L0_xattn_b0': _L0_xattn_in['b0'], 'L0_xattn_W1': _L0_xattn_in['W1'], 'L0_xattn_a_self1': _L0_xattn_in['a_self1'], 'L0_xattn_a_neigh1': _L0_xattn_in['a_neigh1'], 'L0_xattn_b1': _L0_xattn_in['b1'], 'L0_ffn_w1': _L0_ffn_in['w1'], 'L0_ffn_w3': _L0_ffn_in['w3'], 'L0_ffn_w2': _L0_ffn_in['w2'], 'L1_attn_Wq': _L1_attn_in['Wq'], 'L1_attn_Wk': _L1_attn_in['Wk'], 'L1_attn_Wv': _L1_attn_in['Wv'], 'L1_attn_Wo': _L1_attn_in['Wo'], 'L1_xattn_Wq': _L1_xattn_in['Wq'], 'L1_xattn_w_kc_q': _L1_xattn_in['w_kc_q'], 'L1_xattn_w_kc_kv': _L1_xattn_in['w_kc_kv'], 'L1_xattn_W_qr': _L1_xattn_in['W_qr'], 'L1_xattn_W_kr': _L1_xattn_in['W_kr'], 'L1_xattn_Wo': _L1_xattn_in['Wo'], 'L1_ffn_gate_kernel': _L1_ffn_in['gate_kernel'], 'L1_ffn_wi_0': _L1_ffn_in['wi_0'], 'L1_ffn_wi_1': _L1_ffn_in['wi_1'], 'L1_ffn_wo': _L1_ffn_in['wo']}

def reference(x, ctx_512, L0_attn_cos, L0_attn_sin, L0_attn_Wq, L0_attn_Wk, L0_attn_Wv, L0_attn_Wo, L0_xattn_W0, L0_xattn_a_self0, L0_xattn_a_neigh0, L0_xattn_b0, L0_xattn_W1, L0_xattn_a_self1, L0_xattn_a_neigh1, L0_xattn_b1, L0_ffn_w1, L0_ffn_w3, L0_ffn_w2, L1_attn_Wq, L1_attn_Wk, L1_attn_Wv, L1_attn_Wo, L1_xattn_Wq, L1_xattn_w_kc_q, L1_xattn_w_kc_kv, L1_xattn_W_qr, L1_xattn_W_kr, L1_xattn_Wo, L1_ffn_gate_kernel, L1_ffn_wi_0, L1_ffn_wi_1, L1_ffn_wo):
    import jax
    import jax.numpy as jnp

    def _L0_attn_ref(x, cos, sin, Wq, Wk, Wv, Wo):
        import jax, jax.numpy as jnp
        import numpy as np
        B, T, C, H = (4, 512, 256, 16)
        Dh = C // H

        def _feature_map(x):
            return jax.nn.elu(x) + 1.0
        b, t, c = x.shape
        h, dh = (H, c // H)

        def proj(W):
            y = jnp.einsum('btc,oc->bto', x, W)
            return y.reshape(b, t, h, dh).transpose(0, 2, 1, 3)
        q = _feature_map(proj(Wq))
        k = _feature_map(proj(Wk))
        v = proj(Wv)
        kv = jnp.einsum('bhtd,bhte->bhde', k, v)
        z = 1.0 / (jnp.einsum('bhtd,bhd->bht', q, k.sum(axis=2)) + 1e-06)
        out = jnp.einsum('bhtd,bhde,bht->bhte', q, kv, z)
        out = out.transpose(0, 2, 1, 3).reshape(b, t, c)
        return jnp.einsum('btc,oc->bto', out, Wo)

    def _L0_xattn_ref(feats, adj, W0, a_self0, a_neigh0, b0, W1, a_self1, a_neigh1, b1):
        import jax, jax.numpy as jnp
        import numpy as np
        LRELU_ALPHA = 0.2
        MASK_VAL = -10000000000.0
        B, N, F_IN = (4, 256, 64)
        H, F_OUT = (8, 32)
        F_HID = H * F_OUT

        def gat_layer(x, adj, W, a_self, a_neigh, b):
            feat = jnp.einsum('nf,hfo->hno', x, W)
            attn_self = jnp.einsum('hno,ho->hn', feat, a_self)
            attn_neigh = jnp.einsum('hno,ho->hn', feat, a_neigh)
            e = attn_self[:, :, None] + attn_neigh[:, None, :]
            e = jax.nn.leaky_relu(e, LRELU_ALPHA)
            e = e + MASK_VAL * (1.0 - adj)[None, :, :]
            alpha = jax.nn.softmax(e, axis=-1)
            out = jnp.einsum('hnm,hmo->hno', alpha, feat) + b[:, None, :]
            out = jnp.transpose(out, (1, 0, 2)).reshape(out.shape[1], -1)
            return jax.nn.elu(out)

        def per_graph(x, a):
            h = gat_layer(x, a, W0, a_self0, a_neigh0, b0)
            return gat_layer(h, a, W1, a_self1, a_neigh1, b1)
        return jax.vmap(per_graph)(feats, adj)

    def _L0_ffn_ref(x, w1, w3, w2):
        import jax, jax.numpy as jnp
        import numpy as np
        D_MODEL = 256
        HIDDEN = int(2 * D_MODEL * 4 / 3)

        def ternary_quant(w):
            s = jnp.mean(jnp.abs(w))
            q = jnp.clip(jnp.round(w / s), -1.0, 1.0) * s
            return w + jax.lax.stop_gradient(q - w)
        w1q = ternary_quant(w1)
        w3q = ternary_quant(w3)
        w2q = ternary_quant(w2)
        h1 = jnp.einsum('bsd,hd->bsh', x, w1q)
        h3 = jnp.einsum('bsd,hd->bsh', x, w3q)
        g = jax.nn.silu(h1) * h3
        return jnp.einsum('bsh,dh->bsd', g, w2q)

    def _L1_attn_ref(hidden_states, Wq, Wk, Wv, Wo):
        import jax, jax.numpy as jnp
        import numpy as np
        import math
        H = 256
        NH = 16
        HD = H // NH
        THETA = 10000.0

        def rotate_half(x):
            x1, x2 = (x[..., :HD // 2], x[..., HD // 2:])
            return jnp.concatenate((-x2, x1), axis=-1)

        def rope_tables(seq_len, dtype):
            inv_freq = 1.0 / THETA ** (np.arange(0, HD, 2, dtype=np.float32) / HD)
            t = np.arange(seq_len, dtype=np.float32)
            freqs = np.einsum('i,j->ij', t, inv_freq)
            emb = np.concatenate((freqs, freqs), axis=-1)
            return (jnp.asarray(np.cos(emb), dtype), jnp.asarray(np.sin(emb), dtype))
        B, S, _ = hidden_states.shape

        def proj(W):
            y = jnp.einsum('bsh,oh->bso', hidden_states, W)
            return y.reshape(B, S, NH, HD).transpose(0, 2, 1, 3)
        q, k, v = (proj(Wq), proj(Wk), proj(Wv))
        cos, sin = rope_tables(S, hidden_states.dtype)
        cos, sin = (cos[None, None], sin[None, None])
        q = q * cos + rotate_half(q) * sin
        k = k * cos + rotate_half(k) * sin
        scores = jnp.einsum('bhqd,bhkd->bhqk', q, k) / math.sqrt(HD)
        causal = jnp.triu(jnp.ones((S, S), bool), k=1)
        scores = jnp.where(causal, -jnp.inf, scores)
        attn = jax.nn.softmax(scores, axis=-1)
        out = jnp.einsum('bhqk,bhkd->bhqd', attn, v)
        out = out.transpose(0, 2, 1, 3).reshape(B, S, H)
        return jnp.einsum('bsh,oh->bso', out, Wo)

    def _L1_xattn_ref(hidden_q, kv_c, Wq, w_kc_q, w_kc_kv, W_qr, W_kr, Wo):
        import jax, jax.numpy as jnp
        import numpy as np
        B, S, L = (2, 128, 128)
        DIM_Q, H, K, D_C, D_CQ, R = (256, 16, 128, 64, 192, 64)

        def _rope_tables(seq_len, dim, dtype):
            inv_freq = 1.0 / 10000.0 ** (jnp.arange(0, dim, 2, dtype=dtype) / dim)
            t = jnp.arange(seq_len, dtype=dtype)
            freqs = t[:, None] * inv_freq[None, :]
            sin = jnp.repeat(jnp.sin(freqs), 2, axis=-1)
            cos = jnp.repeat(jnp.cos(freqs), 2, axis=-1)
            return (sin, cos)

        def _rotate_half(x):
            h = x.shape[-1] // 2
            return jnp.concatenate([-x[..., h:], x[..., :h]], axis=-1)
        b, s, _ = hidden_q.shape
        l = kv_c.shape[1]
        q_hk = (hidden_q @ Wq.T).reshape(b, s, H, K)
        q_big = jnp.einsum('bshk,hkq->bshq', q_hk, w_kc_q)
        sin, cos = _rope_tables(l, D_C, kv_c.dtype)
        kv_rope = kv_c * cos[None] + _rotate_half(kv_c) * sin[None]
        q_r = jnp.einsum('bshq,hqr->bhsr', q_big, W_qr)
        k_r = jnp.einsum('bld,hdr->bhlr', kv_rope, W_kr)
        scores = jnp.einsum('bhsr,bhlr->bhsl', q_r, k_r)
        attn = jax.nn.softmax(scores, axis=-1)
        ctx_c = jnp.einsum('bhsl,bld->bhsd', attn, kv_rope)
        ctx_lat = jnp.einsum('bhsd,hkd->bshk', ctx_c, w_kc_kv)
        out = ctx_lat.reshape(b, s, H * K) @ Wo.T
        return out

    def _L1_ffn_ref(x, gate_kernel, wi_0, wi_1, wo):
        import jax, jax.numpy as jnp
        import numpy as np
        TOP_K = 2
        E = gate_kernel.shape[-1]
        gate_logits = jnp.einsum('bsd,de->bse', x, gate_kernel)
        top_k_weights, top_k_indices = jax.lax.top_k(gate_logits, TOP_K)
        top_k_weights = jax.nn.softmax(top_k_weights.astype(jnp.float32), axis=-1).astype(x.dtype)
        combine_w = jnp.sum(jax.nn.one_hot(top_k_indices, E, dtype=x.dtype) * top_k_weights[..., None], axis=-2)
        h0 = jnp.einsum('bsd,edm->bsem', x, wi_0)
        h1 = jnp.einsum('bsd,edm->bsem', x, wi_1)
        h = jax.nn.silu(h0) * h1 * combine_w[..., None]
        out = jnp.einsum('bsem,emd->bsd', h, wo)
        return out
    x = _layernorm(x + _L0_attn_ref(x, L0_attn_cos, L0_attn_sin, L0_attn_Wq, L0_attn_Wk, L0_attn_Wv, L0_attn_Wo), axis=-1)
    x = _layernorm(x + _L0_xattn_ref(ctx_512, x, L0_xattn_W0, L0_xattn_a_self0, L0_xattn_a_neigh0, L0_xattn_b0, L0_xattn_W1, L0_xattn_a_self1, L0_xattn_a_neigh1, L0_xattn_b1), axis=-1)
    x = _layernorm(x + _L0_ffn_ref(x, L0_ffn_w1, L0_ffn_w3, L0_ffn_w2), axis=-1)
    x = _layernorm(x + _L1_attn_ref(x, L1_attn_Wq, L1_attn_Wk, L1_attn_Wv, L1_attn_Wo), axis=-1)
    x = _layernorm(x + _L1_xattn_ref(x, ctx_512, L1_xattn_Wq, L1_xattn_w_kc_q, L1_xattn_w_kc_kv, L1_xattn_W_qr, L1_xattn_W_kr, L1_xattn_Wo), axis=-1)
    x = _layernorm(x + _L1_ffn_ref(x, L1_ffn_gate_kernel, L1_ffn_wi_0, L1_ffn_wi_1, L1_ffn_wo), axis=-1)
    return x

_drawn_inputs = setup_inputs


def setup_inputs(seed=0):
    import zlib

    import numpy as np

    out = dict(_drawn_inputs(seed))
    spreads = {'L0_xattn_b0': (0.0, 0.1), 'L0_xattn_b1': (0.0, 0.1)}
    factors = {'L0_attn_Wq': 200.0, 'L0_attn_Wk': 56.2}
    for name, (base, spread) in spreads.items():
        noise = np.random.default_rng([zlib.crc32(name.encode()), seed]).standard_normal(out[name].shape)
        drawn = base * np.exp(spread * noise) if base else spread * noise
        out[name] = jnp.asarray(drawn.astype(out[name].dtype))
    for name, factor in factors.items():
        out[name] = (out[name] * factor).astype(out[name].dtype)
    return out
```

```python
from contextlib import ExitStack

import numpy as np

import concourse.bass as bass
from concourse import mybir

F32 = mybir.dt.float32
BF16 = mybir.dt.bfloat16
U32 = mybir.dt.uint32
ALU = mybir.AluOpType
ACT = mybir.ActivationFunctionType
AX = mybir.AxisListType

P = 128
B, S, D = 4, 256, 256
NPAIR = 2
TILES = B * S // P
TPP = TILES // NPAIR
PT = TPP * P
CTX = 64
GH, GO = 8, 32
HID = 682
HC = 6
HLAST = HID - (HC - 1) * P
AH, AD = 16, 16
MH, MK, MCQ, MR = 16, 128, 192, 64
QCH = MCQ // 2
NE = 8
LN_EPS = 1e-5
NEG = -1e30
BIG = 3e38


def build_decoder(nc, x, x_t, ctx_rows, ctx_t, wa, gat_w0, gat_w1, gat_a, gat_b, ffn1, ffn3, ffn2,
                  wd_qkv, wd_o, m_q, m_kcq, m_qr, m_kr, m_kckv, m_o, gate_w, moe, c_ident, c_block,
                  c_tri, c_rope, c_mrope, c_sel, c_iota, out):
    ctx = ExitStack()
    with ctx:
        def sb(name, shape, dt=F32):
            return ctx.enter_context(nc.sbuf_tensor(name, shape, dt))

        def sem(name):
            return ctx.enter_context(nc.semaphore(name))

        def carve(region, at, *dims, rows=P):
            n = int(np.prod(dims))
            v = region[0:rows, at:at + n]
            if len(dims) == 2:
                v = v.rearrange("p (a b) -> p a b", a=dims[0])
            elif len(dims) == 3:
                v = v.rearrange("p (a b c) -> p a b c", a=dims[0], b=dims[1])
            return v

        X = sb("X", [P, TILES, D])
        XT = sb("XT", [P, 2, NPAIR * PT])
        R = sb("R", [P, TILES, D])
        stat6 = sb("stat6", [P, TILES, 6])
        mean_var = sb("mean_var", [P, TILES, 2])
        veps = sb("veps", [P, TILES])
        rstd = sb("rstd", [P, TILES])
        ident = sb("ident", [P, P])
        ident_b = sb("ident_b", [P, P], BF16)
        tri = sb("tri", [P, P])
        tri_b = sb("tri_b", [P, P], BF16)
        ones = sb("ones", [P, P])
        block_mask = sb("block_mask", [P, 2 * P])
        rope = sb("rope", [P, 2, 2, 2, AD])
        mrope = sb("mrope", [P, 2, 2, CTX])
        sel = sb("sel", [GH, GH, P])
        iota8 = sb("iota8", [P, NE])
        minus_half = sb("minus_half", [P, TPP])
        WA = sb("WA", [P, 2560])
        wa_q, wa_kv, wa_o = carve(WA, 0, 2, D), carve(WA, 512, 2, 2 * D), carve(WA, 1536, 2, D)
        wd_in, wd_out = carve(WA, 0, 2, 3 * D), carve(WA, 1536, 4, D)
        GW = GH * GO + 2 * GH
        wg0 = sb("wg0", [CTX, GW])
        wg1 = sb("wg1", [P, 2, GW])
        gbias = sb("gbias", [P, 4])
        WF = sb("WF", [P, 2 * 2 * HID + HC * D])
        w1s, w3s = carve(WF, 0, 2, HID), carve(WF, 2 * HID, 2, HID)
        w2s = carve(WF, 4 * HID, HC, D)
        ctx_lat_t = carve(WF, 0, 8, PT)
        abs_sum = sb("abs_sum", [P, 3])
        half_scale = sb("half_scale", [P, 3])
        neg_half = sb("neg_half", [P, 3])
        full_scale = sb("full_scale", [P, 3])
        MW = sb("MW", [P, 6144])
        mq, mkcq = carve(MW, 0, 8, D), carve(MW, 2048, 2, 8, P, rows=QCH)
        mqr, mkr = carve(MW, 4096, 8, MCQ, rows=MR), carve(MW, 5632, 8, MR, rows=MR)
        mkckv, mo = carve(MW, 0, MH, CTX), carve(MW, 1024, MH, D)
        WC = sb("WC", [P, 2, MH * CTX])
        WE = sb("WE", [P, MH // 2, D])
        gate_sb = sb("gate_sb", [P, 2, NE])
        CT = sb("CT", [CTX, NPAIR * PT])
        KVR = sb("KVR", [P, TILES, 2, CTX])
        KVT = sb("KVT", [P, NPAIR * PT])
        A0 = sb("A0", [P, 7680])
        fmin, kf = carve(A0, 0, 3, 512), carve(A0, 1536, TPP, D)
        vo, qf = carve(A0, 2560, TPP, 2, 2 * P), carve(A0, 4608, 2, PT)
        kvm, at0 = carve(A0, 5632, 2, 2, 2 * P), carve(A0, 6656, 2, PT)
        hg, silu_c = carve(A0, 0, HC, PT), carve(A0, 3072, 2, PT)
        qc, pe_, pte = carve(A0, 0, 8, PT), carve(A0, 4096, 3, 512), carve(A0, 5632, 2, 512)
        sum_e, rec_e = carve(A0, 6656, 4, 2), carve(A0, 6664, 4, 2)
        nmax_e = carve(A0, 6672, 4, 2)
        A1 = sb("A1", [P, 13312])
        ft, mask = carve(A1, 0, TPP, D), carve(A1, 1024, TPP, D)
        sneg, trow = carve(A1, 2048, TPP, GH), carve(A1, 2080, PT, rows=GH)
        ab, nl = carve(A1, 2592, 3, 512), carve(A1, 4128, 2, 512)
        eb, pb, ptb = carve(A1, 5152, 2, 512), carve(A1, 6176, 2, 512), carve(A1, 7200, 2, 512)
        ht = [carve(A1, 8224, 2, PT), carve(A1, 9248, 2, PT)]
        g_rec, g_o, g_m = carve(A1, 10272, 2, D), carve(A1, 10784, 2, D), carve(A1, 11296, 2, D)
        nmax_b = carve(A1, 11808, 4, 2)
        quant_tmp, prod_tmp = carve(A1, 12000, 768), carve(A1, 12768, D)
        a_bc = carve(A1, 0, 4, D)
        rp, t1, t2 = carve(A1, 0, 2, 1024), carve(A1, 2048, 512), carve(A1, 2560, 512)
        qkt, vp = carve(A1, 3072, 8, PT), carve(A1, 7168, TPP, 512)
        pd, ptd = carve(A1, 9216, 3, 384), carve(A1, 10368, 2, 384)
        atd = carve(A1, 11136, 4, PT)
        nmax_d = carve(A1, 13248, 4, 2)
        gm, silu_m = carve(A1, 0, 4, PT), carve(A1, 2048, 2, PT)
        logits, top8, top_i = carve(A1, 3072, TILES, NE), carve(A1, 3136, TILES, 8), carve(A1, 3200, TILES, 8)
        top_f = carve(A1, 3264, TILES, 8)
        gap, w_first, w_second = carve(A1, 3328, TILES), carve(A1, 3336, TILES), carve(A1, 3344, TILES)
        pick1, pick2 = carve(A1, 3352, TILES, NE), carve(A1, 3416, TILES, NE)
        combine = carve(A1, 3480, TILES, NE)
        rec_d = sb("rec_d", [P, D])
        fold_g, fold_b = carve(A0, 0, 2, 512, rows=QCH), carve(A0, 1024, 512)
        kv_cos, kv_sin = carve(A0, 2048, TILES, CTX), carve(A0, 2560, TILES, CTX)

        bank = [ctx.enter_context(nc.psum_tensor(f"bank{i}", [P, 512], F32)) for i in range(8)]

        names = ("xt0 xt1 x wa ident block wg0 wg1 ga gb ctxt ctxr sel tri rope mrope iota ffn1 ffn3 ffn2 "
                 "wd fold0 fold1 fold2 gate").split()
        ld = {n: sem("ld_" + n) for n in names}
        slot_ld = [sem(f"ld_slot{i}") for i in range(4)]
        stored = sem("stored")
        consts_ready, casts_ready = sem("consts"), sem("casts")
        pool_link, dve_link = sem("pool_link"), sem("dve_link")
        y_ready, r_done, stats_ready, rstd_ready = sem("y_ready"), sem("r_done"), sem("stats"), sem("rstd_s")
        x_ready, xt_ps, xt_ready = sem("x_ready"), sem("xt_ps"), sem("xt_ready")
        q_ps, kv_ps, f_min, f_exp, f_done, v_done = (sem("a_" + n) for n in "q_ps kv_ps min exp feat v".split())
        kva_ps, kvm_done, nd_ps, at_done = (sem("a_" + n) for n in "kva_ps kvm nd_ps at".split())
        wg_done, ft_ps, ft_done, tr_ps, tr_done, tb_ps = (sem("b_" + n) for n in "wg ft_ps ft tr_ps tr tb".split())
        b_a, b_lr, b_e, b_exp, b_pt, b_evd, b_eva, b_av = (sem("b_" + n) for n in "a lr e exp pt evd eva av".split())
        b_o, b_m, b_em, b_h = (sem("b_" + n) for n in "o m em h".split())
        sum_ps, sums_done, abs_done, quant = (sem("c_" + n) for n in "sum_ps sums abs quant".split())
        h1_ps, c_silu, c_g = (sem("c_" + n) for n in "h_ps silu g".split())
        d_zero = sem("d_zero")
        qkv_ps, d_rope, d_v, rp_ps, d_qkt = (sem("d_" + n) for n in "qkv_ps rope v rp_ps qkt".split())
        d_t1, d_s, d_max, d_exp, d_pt, d_evd, d_eva, d_av, d_fin = (
            sem("d_" + n) for n in "t1 s max exp pt evd eva av fin".split())
        fo_g, fo_gs, fo_b, fo_bs, fo_c, fo_cs, fo_e, fo_es = (
            sem("fo_" + n) for n in "g gs b bs c cs e es".split())
        kvr_done, kvt_ps, kvt_done, qc_ps, qc_done = (sem("e_" + n) for n in "kvr kvt_ps kvt qc_ps qc".split())
        e_s, e_max, e_exp, e_norm, e_pt, e_evd, e_eva, e_av, e_ctx = (
            sem("e_" + n) for n in "s max exp norm pt evd eva av ctx".split())
        lg_ps, gap_done, gap_ready, gap_exp = (sem("f_" + n) for n in "lg_ps lg gap gap_exp".split())
        m_h, m_silu, m_g, m_y, m_acc = (sem("m_" + n) for n in "h silu g y acc".split())

        block = ctx.enter_context(nc.Block())

        def wait_moved(eng, by_dve, by_act, n):
            eng.wait_ge(by_act if n % 2 else by_dve, n // 2 + 1)

        def moved(by_dve, by_act, n):
            return (by_act if n % 2 else by_dve), n // 2 + 1

        @block.sync
        def _(sp):
            def load(dst, src, what):
                sp.dma_start(dst, src).then_inc(ld[what], 16)

            load(XT[:, :, 0:PT], x_t[:, :, 0:PT], "xt0")
            load(WA[:, 0:2048], wa, "wa")
            load(ident[:], c_ident, "ident")
            load(XT[:, :, PT:2 * PT], x_t[:, :, PT:2 * PT], "xt1")
            load(block_mask[:], c_block, "block")
            load(tri[:], c_tri, "tri")
            load(X[:], x, "x")
            load(wg0[:, 0:GH * GO], gat_w0, "wg0")
            load(CT[:], ctx_t, "ctxt")
            load(a_bc, gat_a.partition_broadcast(P), "ga")
            load(wg1[:, :, 0:GH * GO], gat_w1, "wg1")
            load(sel[:], c_sel, "sel")
            load(gbias[:], gat_b, "gb")
            load(w1s, ffn1, "ffn1")
            load(w3s, ffn3, "ffn3")
            load(w2s, ffn2, "ffn2")
            load(MW[:, 0:2048], m_q[:, 0:2048], "fold0")
            load(mkcq, m_kcq[:, :, 0:8, :], "fold0")
            load(mqr, m_qr[:, 0:8, :], "fold0")
            load(mkr, m_kr[:, 0:8, :], "fold0")
            load(rope[:], c_rope, "rope")
            load(mrope[:], c_mrope, "mrope")
            load(KVR[:, :, 0, :], ctx_rows, "ctxr")
            load(iota8[:], c_iota, "iota")
            load(gate_sb[:], gate_w, "gate")
            sp.wait_ge(y_ready, TILES)
            sp.dma_start(WA[:, 0:1536], wd_qkv).then_inc(ld["wd"], 16)
            sp.dma_start(WA[:, 1536:2560], wd_o).then_inc(ld["wd"], 16)
            sp.wait_ge(fo_c, 1)
            load(MW[:, 0:2048], m_q[:, 2048:4096], "fold1")
            load(mkcq, m_kcq[:, :, 8:16, :], "fold1")
            load(mqr, m_qr[:, 8:16, :], "fold1")
            load(mkr, m_kr[:, 8:16, :], "fold1")
            sp.wait_ge(fo_c, 2)
            load(mkckv, m_kckv, "fold2")
            load(mo, m_o, "fold2")
            sp.wait_ge(fo_e, 4)
            for e in range(NE):
                if e >= 4:
                    sp.wait_ge(m_y, 2 * 2 * (e - 3))
                sp.dma_start(MW[:, (e % 4) * 1536:(e % 4 + 1) * 1536], moe[:, e, :]).then_inc(slot_ld[e % 4], 16)
            for p in range(NPAIR):
                sp.wait_ge(x_ready, 5 * TILES + TPP * (p + 1))
                sp.dma_start(out[:, TPP * p:TPP * (p + 1), :], X[:, TPP * p:TPP * (p + 1), :]).then_inc(stored, 16)
            sp.wait_ge(stored, 16 * NPAIR)

        @block.tensor
        def _(pe):
            freed = [()] * 8

            def claim(b, *freed_by):
                for s_, v_ in freed[b]:
                    pe.wait_ge(s_, v_)
                freed[b] = freed_by
                return bank[b]

            def transpose(dst, src):
                return pe.transpose(dst, src, ident[:])

            def norm_transposes(L, p):
                pe.wait_ge(x_ready, L * TILES + TPP * (p + 1))
                for c in range(2):
                    n = (2 * (L - 1) + p) * 2 + c
                    ps = claim(6 + c, (xt_ready, n + 1))
                    for tt in range(TPP):
                        last = transpose(ps[:, tt * P:(tt + 1) * P], X[:, TPP * p + tt, c * P:(c + 1) * P])
                    last.then_inc(xt_ps, 1)

            def project_out(L, p, banks, lhs, rhs, chunks):
                for tt in range(TPP):
                    n = L * TILES + TPP * p + tt
                    if tt % 2 == 0:
                        ps = claim(banks[tt // 2], (r_done, n + 2))
                    for k in range(chunks):
                        last = pe.matmul(ps[:, (tt % 2) * D:(tt % 2 + 1) * D], lhs(k, tt), rhs(k),
                                         start=(k == 0), stop=(k == chunks - 1))
                    last.then_inc(y_ready, 1)

            def stage_a(p):
                pe.wait_ge(ld[f"xt{p}"], 16)
                if p == 0:
                    pe.wait_ge(ld["wa"], 16)
                for oc in range(2):
                    ps = claim(oc, (f_done, 6 * p + oc + 1))
                    for c in range(2):
                        last = pe.matmul(ps[:], wa_q[:, c, oc * P:(oc + 1) * P], XT[:, c, p * PT:(p + 1) * PT],
                                         start=(c == 0), stop=(c == 1))
                    last.then_inc(q_ps, 1)
                for tt in range(TPP):
                    ps = claim(2 + tt, (f_done, 6 * p + tt + 3), (v_done, TPP * p + tt + 1))
                    for c in range(2):
                        last = pe.matmul(ps[:], XT[:, c, (TPP * p + tt) * P:(TPP * p + tt + 1) * P], wa_kv[:, c, :],
                                         start=(c == 0), stop=(c == 1))
                    last.then_inc(kv_ps, 1)
                for j in range(2):
                    ps = claim(6 + j, (kvm_done, 2 * p + j + 1))
                    pe.wait_ge(f_done, 6 * p + 2 * j + 4)
                    pe.wait_ge(v_done, TPP * p + 2 * j + 2)
                    for c in range(2):
                        for s in range(2):
                            tt = 2 * j + s
                            last = pe.matmul(ps[:, c * 2 * P:(c + 1) * 2 * P], kf[:, tt, c * P:(c + 1) * P],
                                             vo[:, tt, c, :], start=(s == 0), stop=(s == 1))
                    last.then_inc(kva_ps, 1)
                pe.wait_ge(kvm_done, 2 * p + 2)
                for c in range(2):
                    for part in range(2):
                        ps = claim(2 * part + c, (at_done, 2 * p + c + 1))
                        for j in range(2):
                            last = pe.matmul(ps[:, j * S:(j + 1) * S], kvm[:, j, c, part * P:(part + 1) * P],
                                             qf[:, c, j * S:(j + 1) * S], start=True, stop=True)
                    last.then_inc(nd_ps, 1)
                pe.wait_ge(at_done, 2 * p + 2)
                project_out(0, p, (4, 5), lambda k, tt: at0[:, k, tt * P:(tt + 1) * P], lambda k: wa_o[:, k, :], 2)

            def stage_b(l, p):
                lp = 2 * l + p
                if l == 0:
                    pe.wait_ge(ld["ctxt"], 16)
                    pe.wait_ge(wg_done, 1)
                else:
                    pe.wait_ge(b_h, 4 * p + 4)
                    pe.wait_ge(wg_done, 2)
                nch = 1 if l == 0 else 2

                def weights(c, a, b):
                    return wg0[:, a:b] if l == 0 else wg1[:, c, a:b]

                def nodes(c, a, b):
                    return CT[:, p * PT + a:p * PT + b] if l == 0 else ht[p][:, c, a:b]

                for tt in range(TPP):
                    ps = claim(tt, (ft_done, TPP * lp + tt + 1))
                    for c in range(nch):
                        last = pe.matmul(ps[:, 0:GW], nodes(c, tt * P, (tt + 1) * P), weights(c, 0, GW),
                                         start=(c == 0), stop=(c == nch - 1))
                    last.then_inc(ft_ps, 1)
                ps = claim(4, (tr_done, lp + 1))
                for c in range(nch):
                    last = pe.matmul(ps[0:GH, :], weights(c, GH * GO + GH, GW), nodes(c, 0, PT),
                                     start=(c == 0), stop=(c == nch - 1))
                last.then_inc(tr_ps, 1)

                def neighbour_rows(h):
                    ps = claim(h % 2, (b_a, 16 * lp + 2 * h + 2))
                    pe.matmul(ps[:], sel[:, h, :], trow, start=True, stop=True).then_inc(tb_ps, 1)

                def turn(i):
                    n = 16 * lp + i
                    pe.wait_ge(b_exp, n + 1)
                    ps = claim(2 + i % 2, moved(b_evd, b_eva, n))
                    for mt in range(2):
                        for s in range(2):
                            last = transpose(ps[:, mt * S + s * P:mt * S + (s + 1) * P],
                                             pb[:, i % 2, s * S + mt * P:s * S + (mt + 1) * P])
                    last.then_inc(b_pt, 1)

                def mix(i):
                    n, h, j = 16 * lp + i, i // 2, i % 2
                    b_ = 4 + 2 * (h // 4) + j
                    if h % 4 == 0:
                        claim(b_, (b_o, 4 * lp + 2 * (h // 4) + j + 1))
                    wait_moved(pe, b_evd, b_eva, n)
                    q = 32 * (h % 4)
                    for part in range(2):
                        for mt in range(2):
                            w = ft[:, 2 * j + mt, h * GO:(h + 1) * GO] if part == 0 else ones[:, 0:GO]
                            last = pe.matmul(bank[b_][q:q + GO, part * S:(part + 1) * S], w,
                                             ptb[:, i % 2, mt * S:(mt + 1) * S], start=(mt == 0), stop=(mt == 1))
                    last.then_inc(b_av, 1)

                pe.wait_ge(ld["sel"], 16)
                pe.wait_ge(tr_done, lp + 1)
                pe.wait_ge(ft_done, TPP * lp + TPP)
                neighbour_rows(0)
                neighbour_rows(1)
                for k in range(19):
                    if 1 <= k <= 16:
                        turn(k - 1)
                    if k >= 3:
                        mix(k - 3)
                    if k % 2 == 0 and 2 <= k // 2 + 1 < GH:
                        neighbour_rows(k // 2 + 1)

            def gat_out(p):
                pe.wait_ge(b_h, 8 + 4 * p + 4)
                for tt in range(TPP):
                    n = TILES + TPP * p + tt
                    if tt % 2 == 0:
                        ps = claim(tt // 2, (r_done, n + 2))
                    for c in range(2):
                        last = transpose(ps[:, (tt % 2) * D + c * P:(tt % 2) * D + (c + 1) * P],
                                         ht[p][:, c, tt * P:(tt + 1) * P])
                    last.then_inc(y_ready, 1)

            def weight_sums():
                pe.wait_ge(abs_done, 3)
                ps = claim(5, (sums_done, 1))
                pe.matmul(ps[:, 0:3], ones[:], abs_sum[:], start=True, stop=True).then_inc(sum_ps, 1)

            def stage_c(p):
                pe.wait_ge(quant, 6)
                pe.wait_ge(xt_ready, 2 * (p + 1))
                for k in range(HC):
                    n, m = HC * p + k, (P if k < HC - 1 else HLAST)
                    for part, w in enumerate((w1s, w3s)):
                        ps = claim(2 * part + n % 2, (c_g, n + 1))
                        for c in range(2):
                            last = pe.matmul(ps[0:m, :], w[:, c, k * P:k * P + m], XT[:, c, p * PT:(p + 1) * PT],
                                             start=(c == 0), stop=(c == 1))
                    last.then_inc(h1_ps, 1)
                pe.wait_ge(c_g, HC * (p + 1))

                def rows(k):
                    return P if k < HC - 1 else HLAST
                project_out(2, p, (4, 5), lambda k, tt: hg[0:rows(k), k, tt * P:(tt + 1) * P],
                            lambda k: w2s[0:rows(k), k, :], HC)

            def fold_queries(w):
                pe.wait_ge(ld[f"fold{w}"], 64)
                for half in range(2):
                    ps = claim(half, (fo_gs, 2 * w + half + 1))
                    for h in range(4 * half, 4 * half + 4):
                        for q in range(2):
                            at = (h % 4) * P + q * MR
                            last = pe.matmul(ps[0:QCH, at:at + MR], mqr[:, h, q * QCH:(q + 1) * QCH],
                                             mkr[:, h, :], start=True, stop=True)
                    last.then_inc(fo_g, 1)
                pe.wait_ge(fo_gs, 2 * w + 2)
                ps = claim(2, (fo_bs, w + 1))
                for h in range(8):
                    for q in range(2):
                        last = pe.matmul(ps[:, h * MR:(h + 1) * MR], mkcq[:, q, h, :],
                                         fold_g[:, h // 4, (h % 4) * P + q * MR:(h % 4) * P + (q + 1) * MR],
                                         start=(q == 0), stop=(q == 1))
                last.then_inc(fo_b, 1)
                pe.wait_ge(fo_bs, w + 1)
                for c in range(2):
                    ps = claim(3 + c, (fo_cs, 2 * w + c + 1))
                    for h in range(8):
                        last = pe.matmul(ps[:, h * MR:(h + 1) * MR], mq[:, h, c * P:(c + 1) * P],
                                         fold_b[:, h * MR:(h + 1) * MR], start=True, stop=True)
                last.then_inc(fo_c, 1)

            def fold_outputs():
                pe.wait_ge(ld["fold2"], 32)
                for q in range(4):
                    ps = claim(q, (fo_es, q + 1))
                    for h in range(4 * q, 4 * q + 4):
                        last = pe.matmul(ps[64 * (h % 2):64 * (h % 2) + 64, (h // 2 % 2) * D:(h // 2 % 2 + 1) * D],
                                         mkckv[:, h, :], mo[:, h, :], start=True, stop=True)
                    last.then_inc(fo_e, 1)

            def stage_d(p):
                pe.wait_ge(ld["wd"], 32)
                pe.wait_ge(casts_ready, 1)
                pe.wait_ge(xt_ready, 4 + 2 * (p + 1))
                for tt in range(TPP):
                    n = TPP * p + tt
                    t = (TPP * p + tt) * P
                    ps, ps2 = claim(n % 2, (d_t1, n + 1)), claim(2 + n % 2, (d_v, n + 1))
                    for c in range(2):
                        pe.matmul(ps[:], XT[:, c, t:t + P], wd_in[:, c, 0:512], start=(c == 0), stop=(c == 1))
                    for c in range(2):
                        last = pe.matmul(ps2[:, 0:D], XT[:, c, t:t + P], wd_in[:, c, 512:768],
                                         start=(c == 0), stop=(c == 1))
                    last.then_inc(qkv_ps, 1)
                    if tt >= 1:
                        turn_heads(p, tt - 1)
                turn_heads(p, TPP - 1)
                pe.wait_ge(d_qkt, 2 * TPP * (p + 1))
                pe.wait_ge(d_v, TPP * (p + 1))

                def scores(i):
                    n, j, h = 32 * p + i, i // AH, i % AH
                    ps = claim(i % 3, (d_exp, n + 1))
                    q, hc, t = 32 * (h % 4), h // 4, j * S
                    for s in range(2):
                        o = 0 if s == 0 else P
                        pe.matmul(ps[:, o:o + P * (s + 1)], qkt[q:q + AD, hc, t + s * P:t + (s + 1) * P],
                                  qkt[q:q + AD, 4 + hc, t:t + P * (s + 1)], start=True, stop=True)
                        last = pe.matmul(ps[:, o + s * P:o + (s + 1) * P], ident_b[:], tri_b[:],
                                         start=False, stop=True, skip_group_check=True)
                    last.then_inc(d_s, 1)

                def turn(i):
                    n = 32 * p + i
                    pe.wait_ge(d_exp, n + 1)
                    ps = claim(3 + i % 2, moved(d_evd, d_eva, n))
                    for at, of in ((0, 0), (P, P), (2 * P, 2 * P)):
                        last = transpose(ps[:, at:at + P], pd[:, i % 3, of:of + P])
                    last.then_inc(d_pt, 1)

                def mix(i):
                    n, j, h = 32 * p + i, i // AH, i % AH
                    g = 8 * p + 4 * j + h // 4
                    b_ = 5 + g % 2
                    if h % 4 == 0:
                        claim(b_, (d_fin, g + 1))
                    wait_moved(pe, d_evd, d_eva, n)
                    q = 32 * (h % 4)
                    for part in range(2):
                        for kt in range(2):
                            w = vp[:, 2 * j + kt, h * 32:(h + 1) * 32] if part == 0 else ones[:, 0:32]
                            last = pe.matmul(bank[b_][q:q + 32, part * S + kt * P:(part + 1) * S], w,
                                             ptd[:, i % 2, kt * S:kt * P + S], start=(kt == 0), stop=(kt == 1),
                                             skip_group_check=True)
                    last.then_inc(d_av, 1)

                for k in range(32 + 3):
                    if k < 32:
                        scores(k)
                    if 2 <= k < 34:
                        turn(k - 2)
                    if k >= 3:
                        mix(k - 3)
                pe.wait_ge(d_fin, 8 * (p + 1))
                project_out(3, p, (3, 4), lambda k, tt: atd[:, k, tt * P:(tt + 1) * P], lambda k: wd_out[:, k, :], 4)

            def turn_heads(p, tt):
                n = TPP * p + tt
                pe.wait_ge(d_rope, n + 1)
                for half in range(2):
                    ps = claim(4 + half, (d_qkt, 2 * n + half + 1))
                    for c in range(4):
                        last = transpose(ps[:, c * P:(c + 1) * P], rp[:, n % 2, (4 * half + c) * P:(4 * half + c + 1) * P])
                    last.then_inc(rp_ps, 1)

            def turn_context():
                pe.wait_ge(kvr_done, 1)
                for p in range(NPAIR):
                    ps = claim(6 + p, (kvt_done, p + 1))
                    for tt in range(TPP):
                        last = transpose(ps[:, tt * P:(tt + 1) * P],
                                         KVR[:, TPP * p + tt, :, :].rearrange("p a b -> p (a b)"))
                    last.then_inc(kvt_ps, 1)

            def stage_e(p):
                pe.wait_ge(xt_ready, 8 + 2 * (p + 1))
                pe.wait_ge(fo_cs, 4)
                for m in range(8):
                    ps = claim(m % 4, (qc_done, 8 * p + m + 1))
                    for c in range(2):
                        last = pe.matmul(ps[:], WC[:, c, m * P:(m + 1) * P], XT[:, c, p * PT:(p + 1) * PT],
                                         start=(c == 0), stop=(c == 1))
                    last.then_inc(qc_ps, 1)
                pe.wait_ge(kvt_done, 2)
                pe.wait_ge(qc_done, 8 * (p + 1))

                def scores(i):
                    n, j, h = 32 * p + i, i // MH, i % MH
                    ps = claim(i % 3, (e_exp, n + 1))
                    q = 64 * (h % 2)
                    for s in range(2):
                        last = pe.matmul(ps[:, s * S:(s + 1) * S], qc[q:q + 64, h // 2, j * S + s * P:j * S + (s + 1) * P],
                                         KVT[q:q + 64, p * PT + j * S:p * PT + (j + 1) * S], start=True, stop=True)
                    last.then_inc(e_s, 1)

                def turn(i):
                    n = 32 * p + i
                    pe.wait_ge(e_norm, n + 1)
                    ps = claim(3 + i % 2, moved(e_evd, e_eva, n))
                    for lt in range(2):
                        for s in range(2):
                            last = transpose(ps[:, lt * S + s * P:lt * S + (s + 1) * P],
                                             pe_[:, i % 3, s * S + lt * P:s * S + (lt + 1) * P])
                    last.then_inc(e_pt, 1)

                def mix(i):
                    n, j, h = 32 * p + i, i // MH, i % MH
                    g = 8 * p + 4 * j + h // 4
                    b_ = 5 + g % 2
                    if h % 4 == 0:
                        claim(b_, (e_ctx, g + 1))
                    wait_moved(pe, e_evd, e_eva, n)
                    q = 64 * (h % 2)
                    for lt in range(2):
                        last = pe.matmul(bank[b_][q:q + 64, (h // 2 % 2) * S:(h // 2 % 2 + 1) * S],
                                         KVR[:, TPP * p + 2 * j + lt, 0, :], pte[:, i % 2, lt * S:(lt + 1) * S],
                                         start=(lt == 0), stop=(lt == 1))
                    last.then_inc(e_av, 1)

                for k in range(32 + 4):
                    if k < 32:
                        scores(k)
                    if 2 <= k < 34:
                        turn(k - 2)
                    if k >= 4:
                        mix(k - 4)
                pe.wait_ge(e_ctx, 8 * (p + 1))
                pe.wait_ge(fo_es, 4)
                project_out(4, p, (3, 4), lambda k, tt: ctx_lat_t[:, k, tt * P:(tt + 1) * P], lambda k: WE[:, k, :], 8)

            def gate(p):
                pe.wait_ge(xt_ready, 12 + 2 * (p + 1))
                pe.wait_ge(ld["gate"], 16)
                ps = claim(4, (gap_done, p + 1))
                for tt in range(TPP):
                    t = (TPP * p + tt) * P
                    for c in range(2):
                        last = pe.matmul(ps[:, tt * NE:(tt + 1) * NE], XT[:, c, t:t + P], gate_sb[:, c, :],
                                         start=(c == 0), stop=(c == 1))
                last.then_inc(lg_ps, 1)

            def expert_in(e, p):
                pe.wait_ge(slot_ld[e % 4], 16 * (e // 4 + 1))
                slot = (e % 4) * 1536
                for mc in range(2):
                    n = (2 * e + p) * 2 + mc
                    for part in range(2):
                        w = carve(MW, slot + 512 * part, 2, D)
                        ps = claim(2 * part + n % 2, (m_g, n + 1))
                        for c in range(2):
                            last = pe.matmul(ps[:], w[:, c, mc * P:(mc + 1) * P], XT[:, c, p * PT:(p + 1) * PT],
                                             start=(c == 0), stop=(c == 1))
                    last.then_inc(m_h, 1)

            def expert_out(e, p):
                g = 2 * e + p
                pe.wait_ge(m_g, 2 * g + 2)
                w = carve(MW, (e % 4) * 1536 + 1024, 2, D)
                for tp in range(2):
                    ps = claim(4 + 2 * (g % 2) + tp, (m_acc, TPP * g + 2 * tp + 2))
                    for tt in range(2 * tp, 2 * tp + 2):
                        for mc in range(2):
                            last = pe.matmul(ps[:, (tt % 2) * D:(tt % 2 + 1) * D],
                                             gm[:, (2 * g + mc) % 4, tt * P:(tt + 1) * P], w[:, mc, :],
                                             start=(mc == 0), stop=(mc == 1))
                    last.then_inc(m_y, 1)

            pe.wait_ge(ld["ident"], 16)
            pe.wait_ge(consts_ready, 1)
            stage_a(0)
            stage_a(1)
            stage_b(0, 0)
            weight_sums()
            stage_b(0, 1)
            fold_queries(0)
            stage_b(1, 0)
            gat_out(0)
            stage_b(1, 1)
            gat_out(1)
            fold_queries(1)
            norm_transposes(1, 0)
            stage_c(0)
            turn_context()
            norm_transposes(1, 1)
            stage_c(1)
            fold_outputs()
            norm_transposes(2, 0)
            stage_d(0)
            norm_transposes(2, 1)
            stage_d(1)
            norm_transposes(3, 0)
            stage_e(0)
            norm_transposes(3, 1)
            stage_e(1)
            norm_transposes(4, 0)
            gate(0)
            expert_in(0, 0)
            norm_transposes(4, 1)
            gate(1)
            units = [(e, p) for e in range(NE) for p in range(NPAIR)]
            for u in range(1, len(units)):
                expert_in(*units[u])
                expert_out(*units[u - 1])
            expert_out(*units[-1])

        @block.scalar
        def _(act):
            def copy(dst, src, scale=1.0):
                return act.activation(dst, src, ACT.Copy, scale=scale)

            def norm_moves(L, p):
                for c in range(2):
                    n = (2 * (L - 1) + p) * 2 + c
                    act.wait_ge(xt_ps, n + 1)
                    copy(XT[:, c, p * PT:(p + 1) * PT], bank[6 + c][:]).then_inc(xt_ready, 1)

            def stage_a(p):
                if p == 1:
                    act.wait_ge(kva_ps, 2)
                for i in range(6):
                    n = 6 * p + i
                    if i < TPP:
                        act.wait_ge(kv_ps, TPP * p + i + 1)
                        copy(vo[:, i, :, 0:P], bank[2 + i][:, D:2 * D].rearrange("p (c n) -> p c n", c=2))\
                            .then_inc(v_done, 1)
                    act.wait_ge(f_min, n + 1)
                    w = 512 if i < 2 else D
                    act.activation(fmin[:, n % 3, 0:w], fmin[:, n % 3, 0:w], ACT.Exp).then_inc(f_exp, 1)

            def stage_b(l, p):
                lp = 2 * l + p
                if lp:
                    act.wait_ge(b_a, 16 * lp)
                for tt in range(TPP):
                    act.wait_ge(ft_ps, TPP * lp + tt + 1)
                    copy(ft[:, tt, :], bank[tt][:, 0:GH * GO])
                    copy(sneg[:, tt, :], bank[tt][:, GH * GO:GH * GO + GH], -1.0).then_inc(ft_done, 1)
                act.wait_ge(tr_ps, lp + 1)
                copy(trow, bank[4][0:GH, :]).then_inc(tr_done, 1)
                act.wait_ge(ft_done, TPP * (lp + 1))
                for k in range(21):
                    if k < 16:
                        n, h, j = 16 * lp + k, k // 2, k % 2
                        act.wait_ge(tb_ps, GH * lp + h + 1)
                        if n >= 3:
                            act.wait_ge(b_lr, n - 2)
                        for s in range(2):
                            last = act.activation(ab[:, k % 3, s * S:(s + 1) * S], bank[h % 2][:, j * S:(j + 1) * S],
                                                  ACT.Identity, bias=sneg[:, 2 * j + s, h:h + 1], scale=-1.0)
                        last.then_inc(b_a, 1)
                    if 1 <= k <= 16:
                        i = k - 1
                        n = 16 * lp + i
                        act.wait_ge(b_e, n + 1)
                        if n >= 2:
                            act.wait_ge(b_pt, n - 1)
                        for s in range(2):
                            last = act.activation(pb[:, i % 2, s * S:(s + 1) * S], eb[:, i % 2, s * S:(s + 1) * S],
                                                  ACT.Exp, bias=nmax_b[:, n % 4, s:s + 1], scale=-1.0)
                        last.then_inc(b_exp, 1)
                    if 2 <= k < 18 and k % 2:
                        i = k - 2
                        n = 16 * lp + i
                        act.wait_ge(b_pt, n + 1)
                        if n >= 2:
                            act.wait_ge(b_av, n - 1)
                        copy(ptb[:, i % 2, :], bank[2 + i % 2][:]).then_inc(b_eva, 1)
                    i = k - 4
                    if i >= 0 and i // 2 % 4 == 3:
                        f = 4 * lp + 2 * (i // 8) + i % 2
                        act.wait_ge(b_m, f + 1)
                        act.activation(g_m[:, f % 2, :], g_m[:, f % 2, :], ACT.Exp).then_inc(b_em, 1)

            def fold_queries(w):
                for half in range(2):
                    act.wait_ge(fo_g, 2 * w + half + 1)
                    copy(fold_g[:, half, :], bank[half][0:QCH, :]).then_inc(fo_gs, 1)
                act.wait_ge(fo_b, w + 1)
                copy(fold_b, bank[2][:]).then_inc(fo_bs, 1)
                act.wait_ge(fo_c, w + 1)
                for c in range(2):
                    copy(WC[:, c, w * 512:(w + 1) * 512], bank[3 + c][:]).then_inc(fo_cs, 1)

            def fold_outputs():
                for q in range(4):
                    act.wait_ge(fo_e, q + 1)
                    copy(WE[:, 2 * q:2 * q + 2, :], bank[q][:].rearrange("p (a n) -> p a n", a=2)).then_inc(fo_es, 1)

            def stage_c(p):
                for k in range(HC):
                    n, m = HC * p + k, (P if k < HC - 1 else HLAST)
                    act.wait_ge(h1_ps, n + 1)
                    if n >= 2:
                        act.wait_ge(c_g, n - 1)
                    act.activation(silu_c[0:m, n % 2, :], bank[n % 2][0:m, :], ACT.Silu).then_inc(c_silu, 1)

            def turn_context():
                for p in range(NPAIR):
                    act.wait_ge(kvt_ps, p + 1)
                    copy(KVT[:, p * PT:(p + 1) * PT], bank[6 + p][:]).then_inc(kvt_done, 1)

            def stage_d(p):
                if p == 0:
                    act.wait_ge(d_zero, 1)

                def move_heads(tt):
                    for half in range(2):
                        n = 2 * (TPP * p + tt) + half
                        act.wait_ge(rp_ps, n + 1)
                        copy(qkt[:, 4 * half:4 * half + 4, tt * P:(tt + 1) * P],
                             bank[4 + half][:].rearrange("p (c n) -> p c n", c=4)).then_inc(d_qkt, 1)

                for tt in range(TPP):
                    n = TPP * p + tt
                    act.wait_ge(qkv_ps, n + 1)
                    copy(vp[:, tt, :].rearrange("p (h i) -> p h i", h=AH)[:, :, 0:AD],
                         bank[2 + n % 2][:, 0:D].rearrange("p (h i) -> p h i", h=AH)).then_inc(d_v, 1)
                    if tt >= 1:
                        move_heads(tt - 1)
                move_heads(TPP - 1)
                for k in range(34):
                    if k < 32:
                        n = 32 * p + k
                        act.wait_ge(d_max, n + 1)
                        if n >= 3:
                            act.wait_ge(d_pt, n - 2)
                        for s in range(2):
                            o, w = (0, P) if s == 0 else (P, 2 * P)
                            last = act.activation(pd[:, k % 3, o:o + w], bank[k % 3][:, o:o + w], ACT.Exp,
                                                  bias=nmax_d[:, n % 4, s:s + 1])
                        last.then_inc(d_exp, 1)
                    i = k - 2
                    if i >= 0 and i % 2:
                        n = 32 * p + i
                        act.wait_ge(d_pt, n + 1)
                        if n >= 2:
                            act.wait_ge(d_av, n - 1)
                        copy(ptd[:, i % 2, :], bank[3 + i % 2][:, 0:384]).then_inc(d_eva, 1)

            def stage_e(p):
                for m in range(8):
                    act.wait_ge(qc_ps, 8 * p + m + 1)
                    copy(qc[:, m, :], bank[m % 4][:]).then_inc(qc_done, 1)
                for k in range(37):
                    if k < 32:
                        n = 32 * p + k
                        act.wait_ge(e_max, n + 1)
                        if n >= 3:
                            act.wait_ge(e_pt, n - 2)
                        for s in range(2):
                            last = act.activation(pe_[:, k % 3, s * S:(s + 1) * S], bank[k % 3][:, s * S:(s + 1) * S],
                                                  ACT.Exp, bias=nmax_e[:, n % 4, s:s + 1],
                                                  accum_out=sum_e[:, n % 4, s:s + 1])
                        last.then_inc(e_exp, 1)
                    i = k - 3
                    if 0 <= i < 32 and i % 2:
                        n = 32 * p + i
                        act.wait_ge(e_pt, n + 1)
                        if n >= 2:
                            act.wait_ge(e_av, n - 1)
                        copy(pte[:, i % 2, :], bank[3 + i % 2][:]).then_inc(e_eva, 1)
                    i = k - 5
                    if i >= 0 and i % 4 == 3:
                        n, q = 32 * p + i, i // 4
                        act.wait_ge(e_av, n + 1)
                        copy(ctx_lat_t[:, 2 * (q % 4):2 * (q % 4) + 2, (q // 4) * S:(q // 4 + 1) * S],
                             bank[5 + q % 2][:].rearrange("p (a n) -> p a n", a=2)).then_inc(e_ctx, 1)

            def gate(p):
                act.wait_ge(gap_ready, p + 1)
                g = gap[:, TPP * p:TPP * (p + 1)]
                act.activation(g, g, ACT.Exp).then_inc(gap_exp, 1)

            def expert_in(e, p):
                for mc in range(2):
                    n = (2 * e + p) * 2 + mc
                    act.wait_ge(m_h, n + 1)
                    if n >= 2:
                        act.wait_ge(m_g, n - 1)
                    act.activation(silu_m[:, n % 2, :], bank[n % 2][:], ACT.Silu).then_inc(m_silu, 1)

            stage_a(0)
            stage_a(1)
            stage_b(0, 0)
            stage_b(0, 1)
            fold_queries(0)
            stage_b(1, 0)
            stage_b(1, 1)
            fold_queries(1)
            norm_moves(1, 0)
            stage_c(0)
            turn_context()
            norm_moves(1, 1)
            stage_c(1)
            fold_outputs()
            norm_moves(2, 0)
            stage_d(0)
            norm_moves(2, 1)
            stage_d(1)
            norm_moves(3, 0)
            stage_e(0)
            norm_moves(3, 1)
            stage_e(1)
            norm_moves(4, 0)
            gate(0)
            expert_in(0, 0)
            norm_moves(4, 1)
            gate(1)
            for e, p in [(e, p) for e in range(NE) for p in range(NPAIR)][1:]:
                expert_in(e, p)

        @block.vector
        def _(dve):
            links = [0]

            def link(ins):
                links[0] += 1
                ins.then_inc(dve_link, 1)
                dve.wait_ge(dve_link, links[0])

            def gat_weights():
                dve.wait_ge(ld["ga"], 16)
                dve.wait_ge(ld["wg0"], 16)
                dve.wait_ge(ld["wg1"], 16)
                for step, (w, rows, first) in enumerate(((wg0[:, :], CTX, 0), (wg1[:, 0, :], P, 2), (wg1[:, 1, :], P, 2))):
                    for k in range(2):
                        t = prod_tmp[0:rows, :]
                        link(dve.tensor_tensor(t, w[:, 0:GH * GO], a_bc[0:rows, first + k, :], ALU.mult))
                        o = GH * GO + k * GH
                        last = dve.tensor_reduce(w[:, o:o + GH], t.rearrange("p (h o) -> p h o", h=GH), AX.X, ALU.add)
                        link(last)
                    if rows == CTX or step == 2:
                        dve.sem_inc(wg_done, 1)

            def norm(L, p):
                if L:
                    dve.wait_ge(x_ready, (L - 1) * TILES + TPP * (p + 1))
                for tt in range(TPP):
                    T = TPP * p + tt
                    n = L * TILES + T
                    if L < 5:
                        dve.wait_ge(y_ready, n - tt % 2 + 2)
                        b_ = {0: (4, 5), 1: (0, 1), 2: (4, 5), 3: (3, 4), 4: (3, 4)}[L][tt // 2]
                        y = bank[b_][:, (tt % 2) * D:(tt % 2 + 1) * D]
                        dve.tensor_tensor(R[:, T, :], y, X[:, T, :], ALU.add).then_inc(r_done, 1)
                if L < 5:
                    dve.wait_ge(r_done, L * TILES + TPP * (p + 1))
                for tt in range(TPP):
                    last = dve.bn_stats(stat6[:, TPP * p + tt, :], R[:, TPP * p + tt, :])
                link(last)
                for tt in range(TPP):
                    last = dve.bn_aggr(mean_var[:, TPP * p + tt, :], stat6[:, TPP * p + tt, :])
                last.then_inc(stats_ready, 1)
                dve.wait_ge(rstd_ready, 2 * L + p + 1)
                dve.wait_ge(stats_ready, 2 * L + p + 1)
                for tt in range(TPP):
                    T = TPP * p + tt
                    dve.tensor_scalar(X[:, T, :], R[:, T, :], mean_var[:, T, 0:1], rstd[:, T:T + 1],
                                      ALU.subtract, ALU.mult).then_inc(x_ready, 1)

            def stage_a(p):
                def source(i):
                    return bank[i][:] if i < 2 else bank[i][:, 0:D]

                for k in range(7):
                    if k < 6:
                        n = 6 * p + k
                        dve.wait_ge(q_ps if k < 2 else kv_ps, (2 * p + k + 1) if k < 2 else (TPP * p + k - 1))
                        if k >= 2:
                            dve.wait_ge(v_done, TPP * p + k - 1)
                        if n >= 3:
                            dve.wait_ge(f_done, n - 2)
                        if p == 1 and k < 2:
                            dve.wait_ge(at_done, 2)
                        w = 512 if k < 2 else D
                        dve.tensor_scalar(fmin[:, n % 3, 0:w], source(k), 0.0, None, ALU.min).then_inc(f_min, 1)
                    if k >= 1:
                        i = k - 1
                        n = 6 * p + i
                        dve.wait_ge(f_exp, n + 1)
                        w = 512 if i < 2 else D
                        if p == 1 and i in (0, 2):
                            dve.wait_ge(nd_ps if i == 0 else kva_ps, 2)
                        o = qf[:, i, :] if i < 2 else kf[:, i - 2, :]
                        dve.scalar_tensor_tensor(o, source(i), 0.0, fmin[:, n % 3, 0:w], ALU.max, ALU.add)\
                           .then_inc(f_done, 1)
                if p == 0:
                    dve.wait_ge(ld["block"], 16)
                for j in range(2):
                    dve.wait_ge(kva_ps, 2 * p + j + 1)
                    for c in range(2):
                        last = dve.tensor_tensor(kvm[:, j, c, :], bank[6 + j][:, c * 2 * P:(c + 1) * 2 * P],
                                                 block_mask[:], ALU.mult)
                    last.then_inc(kvm_done, 1)
                dve.wait_ge(f_done, 6 * (p + 1))
                for c in range(2):
                    dve.wait_ge(nd_ps, 2 * p + c + 1)
                    r = fmin[:, c, :]
                    link(dve.tensor_scalar(r, bank[2 + c][:], 1e-6, None, ALU.add))
                    link(dve.reciprocal(r, r))
                    dve.tensor_tensor(at0[:, c, :], bank[c][:], r, ALU.mult).then_inc(at_done, 1)

            def stage_b(l, p):
                lp = 2 * l + p
                dve.wait_ge(x_ready, TPP * (p + 1))
                if lp:
                    dve.wait_ge(b_e, 16 * lp)
                link(dve.tensor_scalar(mask[:, :, :], X[:, TPP * p:TPP * (p + 1), :], 1.0, -1e10,
                                       ALU.subtract, ALU.mult))
                for k in range(22):
                    if k < 16:
                        n, j = 16 * lp + k, k % 2
                        dve.wait_ge(b_a, n + 1)
                        if n >= 2:
                            dve.wait_ge(b_e, n - 1)
                        dve.scalar_tensor_tensor(nl[:, k % 2, :], ab[:, k % 3, :], 0.2, ab[:, k % 3, :],
                                                 ALU.mult, ALU.min).then_inc(b_lr, 1)
                        dve.wait_ge(b_lr, n + 1)
                        if n >= 2:
                            dve.wait_ge(b_exp, n - 1)
                        for s in range(2):
                            last = dve.tensor_tensor_reduce(eb[:, k % 2, s * S:(s + 1) * S], nl[:, k % 2, s * S:(s + 1) * S],
                                                            mask[:, 2 * j + s, :], 1.0, BIG, ALU.add, ALU.min,
                                                            nmax_b[:, n % 4, s:s + 1])
                        last.then_inc(b_e, 1)
                    if 2 <= k < 18 and k % 2 == 0:
                        i = k - 2
                        n = 16 * lp + i
                        dve.wait_ge(b_pt, n + 1)
                        if n >= 2:
                            dve.wait_ge(b_av, n - 1)
                        dve.tensor_copy(ptb[:, i % 2, :], bank[2 + i % 2][:]).then_inc(b_evd, 1)
                    i = k - 4
                    if 0 <= i < 16 and i // 2 % 4 == 3:
                        g, j = i // 8, i % 2
                        f = 4 * lp + 2 * g + j
                        dve.wait_ge(b_av, 16 * lp + i + 1)
                        if f >= 2:
                            dve.wait_ge(b_h, f - 1)
                        ps = bank[4 + 2 * g + j]
                        link(dve.reciprocal(g_rec[:, j, :], ps[:, S:2 * S]))
                        dve.tensor_tensor(g_o[:, j, :], ps[:, 0:S], g_rec[:, j, :], ALU.mult).then_inc(b_o, 1)
                        dve.wait_ge(b_o, f + 1)
                        bias = gbias[:, 2 * l + g:2 * l + g + 1]
                        dve.tensor_scalar(g_m[:, j, :], g_o[:, j, :], bias, 0.0, ALU.add, ALU.min).then_inc(b_m, 1)
                        link(dve.tensor_scalar(g_rec[:, j, :], g_o[:, j, :], bias, 0.0, ALU.add, ALU.max))
                    i = k - 5
                    if 0 <= i < 16 and i // 2 % 4 == 3:
                        g, j = i // 8, i % 2
                        dve.wait_ge(b_em, 4 * lp + 2 * g + j + 1)
                        dve.scalar_tensor_tensor(ht[p][:, g, j * S:(j + 1) * S], g_m[:, j, :], -1.0, g_rec[:, j, :],
                                                 ALU.add, ALU.add).then_inc(b_h, 1)

            def weight_abs():
                for i, (w, what) in enumerate(((w1s, "ffn1"), (w3s, "ffn3"), (w2s, "ffn2"))):
                    dve.wait_ge(ld[what], 16)
                    dve.tensor_reduce(abs_sum[:, i:i + 1], w.rearrange("p a b -> p (a b)"), AX.X, ALU.add,
                                      apply_absolute_value=True).then_inc(abs_done, 1)

            def weight_scales():
                dve.wait_ge(sum_ps, 1)
                for dst, f in ((half_scale, 0.5), (neg_half, -0.5), (full_scale, 1.0)):
                    last = dve.tensor_scalar(dst[:], bank[5][:, 0:3], f / (HID * D), None, ALU.mult)
                last.then_inc(sums_done, 1)

            def context_rope():
                dve.wait_ge(ld["ctxr"], 16)
                dve.wait_ge(ld["mrope"], 16)
                kv, hf = KVR[:, :, 0, :], CTX // 2
                dve.wait_ge(y_ready, TILES)
                for s in range(2):
                    dve.tensor_tensor(kv_cos[:, s::2, :], kv[:, s::2, :],
                                      mrope[:, 0, s, :].unsqueeze(1).broadcast_to([P, B, CTX]), ALU.mult)
                    for a in range(2):
                        last = dve.tensor_tensor(kv_sin[:, s::2, a * hf:(a + 1) * hf], kv[:, s::2, (1 - a) * hf:(2 - a) * hf],
                                                 mrope[:, 1, s, a * hf:(a + 1) * hf].unsqueeze(1).broadcast_to([P, B, hf]),
                                                 ALU.mult)
                link(last)
                for a in range(2):
                    last = dve.tensor_tensor(KVR[:, :, a, :], kv_cos[:, :, :], kv_sin[:, :, :], ALU.add)
                last.then_inc(kvr_done, 1)

            def stage_c(p):
                for k in range(HC):
                    n, m = HC * p + k, (P if k < HC - 1 else HLAST)
                    dve.wait_ge(c_silu, n + 1)
                    dve.tensor_tensor(hg[0:m, k, :], silu_c[0:m, n % 2, :], bank[2 + n % 2][0:m, :], ALU.mult)\
                       .then_inc(c_g, 1)

            def stage_d(p):
                if p == 0:
                    dve.wait_ge(d_zero, 1)
                    dve.wait_ge(ld["rope"], 16)
                for tt in range(TPP):
                    n, s = TPP * p + tt, tt % 2
                    dve.wait_ge(qkv_ps, n + 1)

                    def heads(v):
                        return v.rearrange("p (a h i) -> p a h i", a=2, h=AH)

                    def table(cs, lo, hi):
                        return rope[:, cs, s, :, lo:hi].unsqueeze(2).broadcast_to([P, 2, AH, hi - lo])
                    qk, hf = heads(bank[n % 2][:]), AD // 2
                    if n:
                        dve.wait_ge(d_rope, n)
                    dve.tensor_tensor(heads(t1), qk, table(0, 0, AD), ALU.mult)
                    for a in range(2):
                        last = dve.tensor_tensor(heads(t2)[:, :, :, a * hf:(a + 1) * hf],
                                                 qk[:, :, :, (1 - a) * hf:(2 - a) * hf],
                                                 table(1, a * hf, (a + 1) * hf), ALU.mult)
                    last.then_inc(d_t1, 1)
                    dve.wait_ge(d_t1, n + 1)
                    if n >= 2:
                        dve.wait_ge(rp_ps, 2 * (n - 1))
                    dve.tensor_tensor(rp[:, n % 2, :].rearrange("p (h i) -> p h i", i=32)[:, :, 0:AD],
                                      t1.rearrange("p (h i) -> p h i", i=AD), t2.rearrange("p (h i) -> p h i", i=AD),
                                      ALU.add).then_inc(d_rope, 1)
                for k in range(36):
                    if k < 32:
                        n = 32 * p + k
                        dve.wait_ge(d_s, n + 1)
                        if n >= 4:
                            dve.wait_ge(d_exp, n - 3)
                        for s in range(2):
                            o, w = (0, P) if s == 0 else (P, 2 * P)
                            last = dve.tensor_reduce(nmax_d[:, n % 4, s:s + 1], bank[k % 3][:, o:o + w], AX.X, ALU.max,
                                                     negate=True)
                        last.then_inc(d_max, 1)
                    i = k - 2
                    if 0 <= i < 32 and i % 2 == 0:
                        n = 32 * p + i
                        dve.wait_ge(d_pt, n + 1)
                        if n >= 2:
                            dve.wait_ge(d_av, n - 1)
                        dve.tensor_copy(ptd[:, i % 2, :], bank[3 + i % 2][:, 0:384]).then_inc(d_evd, 1)
                    i = k - 4
                    if i >= 0 and i % 4 == 3:
                        n, q = 32 * p + i, i // 4
                        dve.wait_ge(d_av, n + 1)
                        ps = bank[5 + q % 2]
                        if 8 * p + q:
                            dve.wait_ge(d_fin, 8 * p + q)
                        link(dve.reciprocal(rec_d[:], ps[:, S:2 * S]))
                        dve.tensor_tensor(atd[:, q % 4, (q // 4) * S:(q // 4 + 1) * S], ps[:, 0:S], rec_d[:], ALU.mult)\
                           .then_inc(d_fin, 1)

            def stage_e(p):
                for k in range(36):
                    if k < 32:
                        n = 32 * p + k
                        dve.wait_ge(e_s, n + 1)
                        if n >= 4:
                            dve.wait_ge(e_exp, n - 3)
                        dve.tensor_reduce(nmax_e[:, n % 4, :], bank[k % 3][:].rearrange("p (s n) -> p s n", s=2),
                                          AX.X, ALU.max, negate=True).then_inc(e_max, 1)
                    i = k - 1
                    if 0 <= i < 32:
                        n = 32 * p + i
                        dve.wait_ge(e_exp, n + 1)
                        if n >= 4:
                            dve.wait_ge(e_norm, n - 3)
                        link(dve.reciprocal(rec_e[:, n % 4, :], sum_e[:, n % 4, :]))
                        for s in range(2):
                            w = pe_[:, i % 3, s * S:(s + 1) * S]
                            last = dve.tensor_scalar(w, w, rec_e[:, n % 4, s:s + 1], None, ALU.mult)
                        last.then_inc(e_norm, 1)
                    i = k - 3
                    if 0 <= i < 32 and i % 2 == 0:
                        n = 32 * p + i
                        dve.wait_ge(e_pt, n + 1)
                        if n >= 2:
                            dve.wait_ge(e_av, n - 1)
                        dve.tensor_copy(pte[:, i % 2, :], bank[3 + i % 2][:]).then_inc(e_evd, 1)

            def gate(p):
                a, b = TPP * p, TPP * (p + 1)
                dve.wait_ge(lg_ps, p + 1)
                dve.tensor_copy(logits[:, a:b, :], bank[4][:, 0:TPP * NE].rearrange("p (t e) -> p t e", e=NE))\
                   .then_inc(gap_done, 1)
                dve.wait_ge(gap_done, p + 1)
                for T in range(a, b):
                    last = dve.max(top8[:, T, :], logits[:, T, :])
                link(last)
                dve.tensor_tensor(gap[:, a:b], top8[:, a:b, 1], top8[:, a:b, 0], ALU.subtract).then_inc(gap_ready, 1)
                for T in range(a, b):
                    last = dve.max_index(top_i[:, T, :].bitcast(U32), top8[:, T, :], logits[:, T, :])
                link(last)
                link(dve.tensor_copy(top_f[:, a:b, :], top_i[:, a:b, :].bitcast(U32)))
                dve.wait_ge(gap_exp, p + 1)
                link(dve.tensor_scalar(w_first[:, a:b], gap[:, a:b], 1.0, None, ALU.add))
                link(dve.reciprocal(w_first[:, a:b], w_first[:, a:b]))
                link(dve.tensor_tensor(w_second[:, a:b], w_first[:, a:b], gap[:, a:b], ALU.mult))
                if p == 0:
                    dve.wait_ge(ld["iota"], 16)
                for T in range(a, b):
                    dve.tensor_scalar(pick1[:, T, :], iota8[:], top_f[:, T, 0:1], w_first[:, T:T + 1], ALU.is_equal, ALU.mult)
                    last = dve.tensor_scalar(pick2[:, T, :], iota8[:], top_f[:, T, 1:2], w_second[:, T:T + 1],
                                             ALU.is_equal, ALU.mult)
                link(last)
                link(dve.tensor_tensor(combine[:, a:b, :], pick1[:, a:b, :], pick2[:, a:b, :], ALU.add))

            def expert_gates(e, p):
                g = 2 * e + p
                for mc in range(2):
                    n = 2 * g + mc
                    dve.wait_ge(m_silu, n + 1)
                    if g >= 2:
                        dve.wait_ge(m_y, 2 * (g - 1))
                    dve.tensor_tensor(gm[:, n % 4, :], silu_m[:, n % 2, :], bank[2 + n % 2][:], ALU.mult)\
                       .then_inc(m_g, 1)

            def expert_sum(e, p):
                g = 2 * e + p
                for tt in range(TPP):
                    T, n = TPP * p + tt, TPP * g + tt
                    dve.wait_ge(m_y, 2 * g + tt // 2 + 1)
                    if e:
                        dve.wait_ge(m_acc, n - TILES + 1)
                    else:
                        dve.wait_ge(x_ready, 4 * TILES + T + 1)
                    dve.scalar_tensor_tensor(R[:, T, :], bank[4 + 2 * (g % 2) + tt // 2][:, (tt % 2) * D:(tt % 2 + 1) * D],
                                             combine[:, T, e:e + 1], (R if e else X)[:, T, :], ALU.mult, ALU.add)\
                       .then_inc(m_acc, 1)

            dve.wait_ge(ld["ident"], 16)
            dve.wait_ge(ld["tri"], 16)
            dve.tensor_copy(ident_b[:], ident[:])
            dve.tensor_copy(tri_b[:], tri[:]).then_inc(casts_ready, 1)
            gat_weights()
            stage_a(0)
            dve.wait_ge(ld["x"], 16)
            norm(0, 0)
            stage_a(1)
            norm(0, 1)
            weight_abs()
            dve.wait_ge(ld["gb"], 16)
            stage_b(0, 0)
            weight_scales()
            stage_b(0, 1)
            context_rope()
            stage_b(1, 0)
            norm(1, 0)
            stage_b(1, 1)
            norm(1, 1)
            stage_c(0)
            norm(2, 0)
            stage_c(1)
            norm(2, 1)
            stage_d(0)
            norm(3, 0)
            stage_d(1)
            norm(3, 1)
            stage_e(0)
            norm(4, 0)
            stage_e(1)
            norm(4, 1)
            gate(0)
            expert_gates(0, 0)
            gate(1)
            units = [(e, p) for e in range(NE) for p in range(NPAIR)]
            for u in range(1, len(units)):
                expert_gates(*units[u])
                expert_sum(*units[u - 1])
                if units[u] == (NE - 1, 1):
                    dve.wait_ge(m_acc, TPP * (2 * NE - 1))
                    norm(5, 0)
            expert_sum(*units[-1])
            dve.wait_ge(m_acc, TPP * 2 * NE)
            norm(5, 1)

        @block.gpsimd
        def _(pool):
            links = [0]

            def link(ins):
                links[0] += 1
                ins.then_inc(pool_link, 1)
                pool.wait_ge(pool_link, links[0])

            def inverse_std(L, p):
                a, b = TPP * p, TPP * (p + 1)
                pool.wait_ge(stats_ready, 2 * L + p + 1)
                if L:
                    pool.wait_ge(rstd_ready, 2 * (L - 1) + p + 1)
                link(pool.tensor_scalar(veps[:, a:b], mean_var[:, a:b, 1], LN_EPS, None, ALU.add))
                pool.tensor_tensor(rstd[:, a:b], veps[:, a:b], minus_half[:], ALU.pow).then_inc(rstd_ready, 1)

            pool.memset(vo[:, :, :, P:2 * P], 1.0)
            pool.memset(minus_half[:], -0.5)
            pool.memset(ones[:], 1.0).then_inc(consts_ready, 1)
            for p in range(NPAIR):
                inverse_std(0, p)
            pool.wait_ge(sums_done, 1)
            for i, w in enumerate((w1s, w3s, w2s)):
                w = w.rearrange("p a b -> p (a b)")
                n = w.shape[1] // 2
                for half in range(2):
                    v, t = w[:, half * n:(half + 1) * n], quant_tmp[:, 0:n]
                    full = full_scale[:, i:i + 1]
                    pool_first = pool.tensor_scalar(t, v, half_scale[:, i:i + 1], full, ALU.is_gt, ALU.mult)
                    link(pool_first)
                    link(pool.tensor_scalar(v, v, neg_half[:, i:i + 1], full, ALU.is_lt, ALU.mult))
                    pool.tensor_tensor(v, t, v, ALU.subtract).then_inc(quant, 1)
                    pool.wait_ge(quant, 2 * i + half + 1)
            inverse_std(1, 0)
            inverse_std(1, 1)
            pool.wait_ge(y_ready, 2 * TILES)
            pool.memset(rp, 0.0)
            pool.memset(vp, 0.0).then_inc(d_zero, 1)
            for L in range(2, 6):
                for p in range(NPAIR):
                    inverse_std(L, p)


INPUTS = ("x x_t ctx_rows ctx_t wa gat_w0 gat_w1 gat_a gat_b ffn1 ffn3 ffn2 wd_qkv wd_o m_q m_kcq m_qr m_kr "
          "m_kckv m_o gate_w moe c_ident c_block c_tri c_rope c_mrope c_sel c_iota").split()


def constants():
    ident = np.eye(P, dtype=np.float32)
    blocks = np.kron(np.eye(P // AD), np.ones((AD, AD))).astype(np.float32)
    tri = np.where(np.triu(np.ones((P, P)), 1) > 0, np.float32(NEG), np.float32(0)).astype(np.float32)
    inv = (1.0 / 10000.0 ** (np.arange(0, AD, 2, dtype=np.float32) / AD)).astype(np.float32)
    f = np.einsum("i,j->ij", np.arange(S, dtype=np.float32), inv)
    f = np.concatenate((f, f), axis=-1)
    sign = np.where(np.arange(AD) < AD // 2, -1.0, 1.0).astype(np.float32)
    cs = np.stack([np.cos(f), np.sin(f) * sign]).astype(np.float32).reshape(2, 2, P, AD)
    rope = np.stack([cs * np.float32(AD ** -0.5), cs], axis=3).transpose(2, 0, 1, 3, 4)
    inv = (1.0 / 10000.0 ** (np.arange(0, CTX, 2, dtype=np.float32) / CTX)).astype(np.float32)
    f = (np.arange(S, dtype=np.float32)[:, None] * inv[None, :]).astype(np.float32)
    sign = np.where(np.arange(CTX) < CTX // 2, -1.0, 1.0).astype(np.float32)
    cs = np.stack([np.repeat(np.cos(f), 2, -1), np.repeat(np.sin(f), 2, -1) * sign]).astype(np.float32)
    mrope = cs.reshape(2, 2, P, CTX).transpose(2, 0, 1, 3)
    sel = np.repeat(np.eye(GH, dtype=np.float32)[:, :, None], P, axis=2)
    iota = np.broadcast_to(np.arange(NE, dtype=np.float32), (P, NE))
    return dict(c_ident=ident, c_block=np.concatenate([blocks, blocks], 1), c_tri=tri, c_rope=rope,
                c_mrope=mrope, c_sel=sel, c_iota=iota)


def lay_out(i):
    def chunks(w, rows=P):
        return w.reshape(-1, rows, w.shape[-1]).transpose(1, 0, 2)

    def zeros_like_rows(n, w):
        return np.zeros((n, w.shape[-1]), w.dtype)
    x = i["x"].reshape(B * S, D)
    c = i["ctx_512"].reshape(B * S, CTX)
    a = dict(x=chunks(x), x_t=chunks(x.T), ctx_rows=chunks(c), ctx_t=c.T)
    a["wa"] = np.concatenate([chunks(i["L0_attn_Wq"].T).reshape(P, -1),
                              chunks(np.concatenate([i["L0_attn_Wk"].T, i["L0_attn_Wv"].T], 1)).reshape(P, -1),
                              chunks(i["L0_attn_Wo"].T).reshape(P, -1)], 1)
    a["gat_w0"] = i["L0_xattn_W0"].transpose(1, 0, 2).reshape(CTX, GH * GO)
    a["gat_w1"] = chunks(i["L0_xattn_W1"].transpose(1, 0, 2).reshape(D, GH * GO))
    a["gat_a"] = np.stack([i["L0_xattn_" + n].reshape(-1) for n in ("a_self0", "a_neigh0", "a_self1", "a_neigh1")])
    a["gat_b"] = np.concatenate([i["L0_xattn_b0"].reshape(2, P).T, i["L0_xattn_b1"].reshape(2, P).T], 1)
    a["ffn1"], a["ffn3"] = chunks(i["L0_ffn_w1"].T), chunks(i["L0_ffn_w3"].T)
    w2 = i["L0_ffn_w2"].T
    a["ffn2"] = chunks(np.concatenate([w2, zeros_like_rows(HC * P - HID, w2)], 0))
    a["wd_qkv"] = chunks(np.concatenate([i["L1_attn_" + n].T for n in ("Wq", "Wk", "Wv")], 1)).reshape(P, -1)
    wo = i["L1_attn_Wo"].T.reshape(AH, AD, D)
    wo = np.concatenate([wo, np.zeros((AH, 32 - AD, D), wo.dtype)], 1)
    a["wd_o"] = chunks(wo.reshape(AH * 32, D)).reshape(P, -1)
    a["m_q"] = i["L1_xattn_Wq"].reshape(MH, MK, D).transpose(1, 0, 2).reshape(MK, MH * D)
    a["m_kcq"] = i["L1_xattn_w_kc_q"].transpose(2, 0, 1).reshape(2, QCH, MH, MK).transpose(1, 0, 2, 3)
    a["m_qr"] = i["L1_xattn_W_qr"].transpose(2, 0, 1)
    a["m_kr"] = i["L1_xattn_W_kr"].transpose(2, 0, 1)
    a["m_kckv"] = i["L1_xattn_w_kc_kv"].transpose(1, 0, 2)
    a["m_o"] = i["L1_xattn_Wo"].T.reshape(MH, MK, D).transpose(1, 0, 2)
    a["gate_w"] = chunks(i["L1_ffn_gate_kernel"])
    a["moe"] = np.concatenate([i["L1_ffn_" + n].reshape(NE, 2, P, D).transpose(2, 0, 1, 3).reshape(P, NE, 2 * D)
                               for n in ("wi_0", "wi_1", "wo")], 2)
    return a


def kernel(**inputs):
    import concourse.bacc as _bacc
    from concourse.bass_utils import run_bass_kernel_spmd as _run

    given = {k: np.asarray(v) for k, v in inputs.items()}
    arrays = {**lay_out(given), **constants()}
    nc = _bacc.Bacc("TRN2", target_bir_lowering=False, num_devices=1)
    feed, args = {}, []
    for name in INPUTS:
        a = np.ascontiguousarray(arrays[name])
        feed[name + "_dram"] = a
        args.append(nc.dram_tensor(name + "_dram", a.shape, mybir.dt.from_np(a.dtype), kind="ExternalInput").ap())
    out = nc.dram_tensor("out_dram", (P, TILES, D), F32, kind="ExternalOutput").ap()
    build_decoder(nc, *args, out)
    r = _run(nc, [feed], core_ids=[0])
    y = r.results[0]["out_dram"]
    return y.transpose(1, 0, 2).reshape(B, S, D)
```

```python
from contextlib import ExitStack

import numpy as np

import concourse.bass as bass
from concourse import mybir

F32 = mybir.dt.float32
F32R = mybir.dt.float32r
BF16 = mybir.dt.bfloat16
U32 = mybir.dt.uint32
ALU = mybir.AluOpType
ACT = mybir.ActivationFunctionType
AX = mybir.AxisListType

P = 128
B, S, D = 4, 256, 256
NPAIR = 2
TILES = B * S // P
TPP = TILES // NPAIR
PT = TPP * P
CTX = 64
GH, GO = 8, 32
HID = 682
HC = 6
HP = HC * P
AH, AD = 16, 16
MH, MK, MCQ, MR = 16, 128, 192, 64
QCH = MCQ // 2
NE = 8
TR = 32 + GH
GN = 2 * NPAIR * GH * 2
LN_EPS = 1e-5
FOLDS = {22: (0, "g", 0, 6), 23: (0, "g", 1, 7), 30: (0, "b", 0, 4), 31: (0, "b", 1, 4), 32: (0, "b", 2, 4),
         33: (0, "b", 3, 4), 35: (0, "c", 0, 5), 36: (0, "c", 1, 5), 38: (0, "c", 2, 6), 39: (0, "c", 3, 6),
         46: (1, "g", 0, 4), 47: (1, "g", 1, 5), 48: (1, "b", 0, 4), 49: (1, "b", 1, 4), 50: (1, "b", 2, 4),
         51: (1, "b", 3, 4), 54: (1, "c", 0, 7), 55: (1, "c", 1, 7), 56: (1, "c", 2, 6), 57: (1, "c", 3, 6)}
NEG = -1e30
BIG = 3e38


def build_decoder(nc, x, x_t, ctx_rows, ctx_t, wa, gat_w0, gat_w1, gat_a, gat_b, ffn1, ffn3, ffn2,
                  wd_qkv, wd_o, m_q, m_kcq, m_qr, m_kr, m_kckv, m_o, gate_w, moe, c_ident, c_block,
                  c_tri, c_rope, c_mrope, c_sel, c_iota, out):
    ctx = ExitStack()
    with ctx:
        def sb(name, shape, dt=F32):
            return ctx.enter_context(nc.sbuf_tensor(name, shape, dt))

        def sem(name):
            return ctx.enter_context(nc.semaphore(name))

        def over(*regions):
            at = []
            for name, floats, *dt in regions[1:]:
                with nc.sbuf_tensor(name, [P, floats], *(dt or [F32])) as t:
                    at.append(t)
            return [sb(regions[0][0], [P, regions[0][1]], *(regions[0][2:] or [F32]))] + at

        def carve(region, at, *dims, rows=P):
            n = int(np.prod(dims))
            v = region[0:rows, at:at + n]
            if len(dims) == 2:
                v = v.rearrange("p (a b) -> p a b", a=dims[0])
            elif len(dims) == 3:
                v = v.rearrange("p (a b c) -> p a b c", a=dims[0], b=dims[1])
            return v

        X = sb("X", [P, TILES, D])
        XT = sb("XT", [P, 2, NPAIR * PT])
        R = sb("R", [P, TILES, D])
        stat6 = sb("stat6", [P, TILES, 6])
        mean_var = sb("mean_var", [P, TILES, 2])
        veps = sb("veps", [P, TILES])
        rstd = sb("rstd", [P, TILES])
        ident = sb("ident", [P, P])
        tri = sb("tri", [P, 2 * P])
        ones = sb("ones", [P, P])
        block_mask = sb("block_mask", [P, P + GH])
        rope = sb("rope", [P, 2, 2, 2, AD])
        mrope = sb("mrope", [P, 2, 2, CTX])
        sel_r = sb("sel_r", [TR, GH, P], F32R)
        iota8 = sb("iota8", [P, NE])
        minus_half = sb("minus_half", [P, TPP])
        WA = sb("WA", [P, 2560])
        wa_q, wa_kv, wa_o = carve(WA, 0, 2, D), carve(WA, 512, 2, 2 * D), carve(WA, 1536, 2, D)
        wd_in, wd_out = carve(WA, 0, 2, 3 * D), carve(WA, 1536, 4, D)
        GF = GH * GO + GH
        GW = GF + TR
        wg0 = sb("wg0", [CTX, GW])
        wg1 = sb("wg1", [P, 2, GW])
        gbias = sb("gbias", [P, 4])
        ternary, E1 = over(("ternary", 2 * 2 * HP + HC * D, F32R), ("E1", 8 * PT))
        w1t, w3t = carve(ternary, 0, 2, HP), carve(ternary, 2 * HP, 2, HP)
        w2t = carve(ternary, 4 * HP, HC, D)
        ctx_lat_t = carve(E1, 0, 8, PT)
        abs_sum = sb("abs_sum", [P, 3])
        half_scale = sb("half_scale", [P, 3])
        neg_half = sb("neg_half", [P, 3])
        full_scale = sb("full_scale", [P, 3])
        out_scale = sb("out_scale", [P, 1])
        MW = sb("MW", [P, 6144])
        mq, mkcq = carve(MW, 0, 8, D), carve(MW, 2048, 2, 8, P, rows=QCH)
        mqr, mkr = carve(MW, 4096, 8, MCQ, rows=MR), carve(MW, 5632, 8, MR, rows=MR)
        raw = [carve(MW, a, b) for a, b in ((0, 2 * HP), (2 * HP, 2 * HP), (4 * HP, HC * D))]
        mkckv, mo = carve(MW, 0, MH, CTX), carve(MW, 1024, MH, D)
        WC = sb("WC", [P, 2, MH * CTX])
        WE = sb("WE", [P, MH // 2, D])
        sel = WE[0:TR, 0:4, :].rearrange("p a (b n) -> p (a b) n", b=2)
        gate_sb = sb("gate_sb", [P, 2, NE])
        CT = sb("CT", [CTX, NPAIR * PT])
        KVR = sb("KVR", [P, TILES, 2, CTX])
        KVT = sb("KVT", [P, NPAIR * PT])
        A0, R0, RD = over(("A0", 16 * PT), ("R0", 4096, F32R), ("RD", 16 * PT, F32R))
        NV = P + GH
        kf = [carve(A0, 1024 * p, TPP, D) for p in range(NPAIR)]
        qf = [carve(A0, 2048 + 1024 * p, 2, PT) for p in range(NPAIR)]
        vo = [carve(A0, 4096 + 1088 * p, TPP, 2, NV) for p in range(NPAIR)]
        kvm = carve(A0, 6272, 2, 2, NV)
        ht = [carve(A0, 4096, 2, PT), carve(A0, 5120, 2, PT)]
        prod_tmp = carve(A0, 6912, D)
        xh, xl = ([carve(R0, 2048 * p + 1024 * i, 2, PT) for p in range(NPAIR)] for i in range(2))
        silu_c = carve(A0, 6144, 2, PT)
        qc, pe_, pte = carve(A0, 0, 8, PT), carve(A0, 4096, 4, 512), carve(A0, 6144, 2, 512)
        sum_e, nmax_e = carve(A0, 7168, 4, 2), carve(A0, 7176, 4, 2)
        A1, RA = over(("A1", 12416), ("RA", 4096 + 2 * HC * PT, F32R))
        R1, = over(("R1", 1024, F32R))
        ft = [carve(A1, 1024 * i, TPP, D) for i in range(2)]
        mask = [carve(A1, 2048 + 1024 * i, TPP, D) for i in range(2)]
        sneg = [carve(A1, 4096 + 32 * i, TPP, GH) for i in range(2)]
        tneg, a2, nl = carve(A1, 4160, 2, 512), carve(A1, 5184, 2, 512), carve(A1, 6208, 2, 512)
        eb, pb, ptb = carve(A1, 7232, 2, 512), carve(A1, 8256, 3, 512), carve(A1, 9792, 2, 512)
        g_v, g_m = carve(A1, 10816, 2, D), carve(A1, 11328, 2, D)
        nmax_b, sum_b = carve(A1, 11840, 4, 2), carve(A1, 11848, 4, 2)
        trow = [carve(R1, 512 * i, PT, rows=TR) for i in range(2)]
        below = carve(A1, 2048, HC * D)
        hg_hi, hg_lo = carve(RA, 4096, HC, PT), carve(RA, 4096 + HC * PT, HC, PT)
        hg = carve(A1, 4096 + 2 * HC * PT, 2, PT)
        fmin, a_tok, at0 = carve(A1, 8256, 3, 512), carve(A1, 9792, 2, D), carve(A1, 10816, 2, PT)
        a_den = carve(A1, 11856, TPP, 2, 8)
        a_bc = carve(A1, 0, 4, D)
        vp, t1, t2 = carve(A1, 0, TPP, 512), carve(A1, 2048, 512), carve(A1, 2560, 512)
        roped, rp = carve(A1, 3072, 2, 512), carve(A1, 4096, 2, 2048)
        pd, ns_d = carve(A1, 8192, 4, 384), carve(A1, 9728, 3, 384)
        qkt, atd, ptd = carve(RD, 0, 16, PT), carve(E1, 0, 4, PT), carve(E1, 2048, 2, 384)
        nmin_d, sum_d = sb("nmin_d", [P, 4, 2]), sb("sum_d", [P, 4, 2])
        gm, silu_m = carve(A1, 0, 4, PT), carve(A1, 2048, 2, PT)
        logits, top8, top_i = carve(A1, 3072, TILES, NE), carve(A1, 3136, TILES, 8), carve(A1, 3200, TILES, 8)
        top_f = carve(A1, 3264, TILES, 8)
        gap, w_first, w_second = carve(A1, 3328, TILES), carve(A1, 3336, TILES), carve(A1, 3344, TILES)
        pick1, pick2 = carve(A1, 3352, TILES, NE), carve(A1, 3416, TILES, NE)
        combine = carve(A1, 3480, TILES, NE)
        fold_g, fold_b = carve(A0, 0, 2, 512, rows=QCH), carve(A0, 1024, 512)
        kv_cos, kv_sin = carve(A0, 2048, TILES, CTX), carve(A0, 2560, TILES, CTX)

        bank = [ctx.enter_context(nc.psum_tensor(f"bank{i}", [P, 512], F32)) for i in range(8)]

        names = ("xt0 xt1 x wa ident block wg0 wg1 ga gb ctxt ctxr sel tri rope mrope iota ffn1 ffn3 ffn2 "
                 "wd fold_r0 fold_b0 fold_q0 fold_r1 fold_b1 fold_q1 fold2 gate").split()
        ld = {n: sem("ld_" + n) for n in names}
        slot_ld = [sem(f"ld_slot{i}") for i in range(4)]
        stored = sem("stored")
        consts_ready, casts_ready = sem("consts"), sem("casts")
        pool_link, dve_link = sem("pool_link"), sem("dve_link")
        y_ready, r_done, stats_ready, rstd_ready = sem("y_ready"), sem("r_done"), sem("stats"), sem("rstd_s")
        x_ready, xt_ps, xt_ready, xl_ready = sem("x_ready"), sem("xt_ps"), sem("xt_ready"), sem("xl_ready")
        q_ps, kv_ps, f_min, f_exp, f_done, v_done = (sem("a_" + n) for n in "q_ps kv_ps min exp feat v".split())
        kva_ps, kvm_done, nd_ps, a_tok_done, at_ps, at_done = (sem("a_" + n) for n in "kva_ps kvm nd_ps tok at_ps at".split())
        wg_done, ft_ps, ft_done, tr_ps, tr_done, trow_done, tb_ps = (
            sem("b_" + n) for n in "wg ft_ps ft tr_ps tr trow tb".split())
        b_tc, b_a2, b_lr, b_e, b_exp, b_rec, b_norm = (sem("b_" + n) for n in "tc a2 lr e exp rec norm".split())
        b_pt, b_evd, b_eva, b_av, b_m, b_em, b_h = (sem("b_" + n) for n in "pt evd eva av m em h".split())
        sum_ps, sums_done, abs_done, quant = (sem("c_" + n) for n in "sum_ps sums abs quant".split())
        h1_ps, c_silu, c_g, c_hi, c_lo = (sem("c_" + n) for n in "h_ps silu g hi lo".split())
        d_zero, d_hi, d_lo, d_rec, d_norm = sem("d_zero"), sem("d_hi"), sem("d_lo"), sem("d_rec"), sem("d_norm")
        qkv_ps, d_rope, d_v, rp_ps, d_qkt = (sem("d_" + n) for n in "qkv_ps rope v rp_ps qkt".split())
        d_t1, d_s, d_max, d_exp, d_pt, d_evd, d_eva, d_av, d_fin = (
            sem("d_" + n) for n in "t1 s max exp pt evd eva av fin".split())
        fo_g, fo_gs, fo_b, fo_bs, fo_c, fo_cs, fo_e, fo_es = (
            sem("fo_" + n) for n in "g gs b bs c cs e es".split())
        kvr_done, kvt_ps, kvt_done, qc_ps, qc_done = (sem("e_" + n) for n in "kvr kvt_ps kvt qc_ps qc".split())
        e_s, e_max, e_exp, e_rec, e_norm, e_pt, e_evd, e_eva, e_av, e_ctx = (
            sem("e_" + n) for n in "s max exp rec norm pt evd eva av ctx".split())
        lg_ps, gap_done, gap_ready, gap_exp = (sem("f_" + n) for n in "lg_ps lg gap gap_exp".split())
        m_h, m_silu, m_g, m_y, m_acc = (sem("m_" + n) for n in "h silu g y acc".split())

        block = ctx.enter_context(nc.Block())

        def wait_moved(eng, by_dve, by_act, n):
            eng.wait_ge(by_act if n % 2 else by_dve, n // 2 + 1)

        def moved(by_dve, by_act, n):
            return (by_act if n % 2 else by_dve), n // 2 + 1

        @block.sync
        def _(sp):
            def load(dst, src, what):
                sp.dma_start(dst, src).then_inc(ld[what], 16)

            load(XT[:, :, 0:PT], x_t[:, :, 0:PT], "xt0")
            load(WA[:, 0:2048], wa, "wa")
            load(XT[:, :, PT:2 * PT], x_t[:, :, PT:2 * PT], "xt1")
            load(block_mask[:], c_block, "block")
            load(ident[:], c_ident, "ident")
            load(X[:], x, "x")
            for src, dst, what in zip((ffn1, ffn3, ffn2), raw, ("ffn1", "ffn3", "ffn2")):
                load(dst, src, what)
            load(wg0[:, 0:GH * GO], gat_w0, "wg0")
            load(CT[:], ctx_t, "ctxt")
            load(a_bc, gat_a.partition_broadcast(P), "ga")
            load(wg1[:, :, 0:GH * GO], gat_w1, "wg1")
            load(sel[:], c_sel, "sel")
            load(gbias[:], gat_b, "gb")
            load(tri[:], c_tri, "tri")
            load(rope[:], c_rope, "rope")
            load(mrope[:], c_mrope, "mrope")
            load(KVR[:, :, 0, :], ctx_rows, "ctxr")
            load(iota8[:], c_iota, "iota")
            load(gate_sb[:], gate_w, "gate")
            sp.wait_ge(quant, 3)
            load(mqr, m_qr[:, 0:8, :], "fold_r0")
            load(mkr, m_kr[:, 0:8, :], "fold_r0")
            load(mkcq, m_kcq[:, :, 0:8, :], "fold_b0")
            load(MW[:, 0:2048], m_q[:, 0:2048], "fold_q0")
            sp.wait_ge(y_ready, TILES)
            sp.dma_start(WA[:, 0:1536], wd_qkv).then_inc(ld["wd"], 16)
            sp.dma_start(WA[:, 1536:2560], wd_o).then_inc(ld["wd"], 16)
            sp.wait_ge(fo_g, 2)
            load(mqr, m_qr[:, 8:16, :], "fold_r1")
            load(mkr, m_kr[:, 8:16, :], "fold_r1")
            sp.wait_ge(fo_b, 1)
            load(mkcq, m_kcq[:, :, 8:16, :], "fold_b1")
            sp.wait_ge(fo_c, 2)
            load(MW[:, 0:2048], m_q[:, 2048:4096], "fold_q1")
            sp.wait_ge(fo_c, 4)
            load(mkckv, m_kckv, "fold2")
            load(mo, m_o, "fold2")
            sp.wait_ge(fo_e, 4)
            for e in range(NE):
                if e >= 4:
                    sp.wait_ge(m_y, 2 * 2 * (e - 3))
                sp.dma_start(MW[:, (e % 4) * 1536:(e % 4 + 1) * 1536], moe[:, e, :]).then_inc(slot_ld[e % 4], 16)
            for p in range(NPAIR):
                sp.wait_ge(x_ready, 5 * TILES + TPP * (p + 1))
                sp.dma_start(out[:, TPP * p:TPP * (p + 1), :], X[:, TPP * p:TPP * (p + 1), :]).then_inc(stored, 16)
            sp.wait_ge(stored, 16 * NPAIR)

        @block.tensor
        def _(pe):
            freed = [()] * 8

            def claim(b, *freed_by):
                for s_, v_ in freed[b]:
                    pe.wait_ge(s_, v_)
                freed[b] = freed_by
                return bank[b]

            def transpose(dst, src):
                return pe.transpose(dst, src, ident[:])

            def norm_transposes(L, p):
                pe.wait_ge(x_ready, L * TILES + TPP * (p + 1))
                for c in range(2):
                    n = (2 * (L - 1) + p) * 2 + c
                    ps = claim(6 + c, (xl_ready, n + 1) if L == 1 else (xt_ready, n + 1))
                    for tt in range(TPP):
                        last = transpose(ps[:, tt * P:(tt + 1) * P], X[:, TPP * p + tt, c * P:(c + 1) * P])
                    last.then_inc(xt_ps, 1)

            def project_out(L, p, banks, lhs, rhs, chunks):
                for tt in range(TPP):
                    n = L * TILES + TPP * p + tt
                    if tt % 2 == 0:
                        ps = claim(banks[tt // 2], (r_done, n + 2))
                    for k in range(chunks):
                        last = pe.matmul(ps[:, (tt % 2) * D:(tt % 2 + 1) * D], lhs(k, tt), rhs(k),
                                         start=(k == 0), stop=(k == chunks - 1))
                    last.then_inc(y_ready, 1)

            def project_in(p):
                pe.wait_ge(ld[f"xt{p}"], 16)
                if p == 0:
                    pe.wait_ge(ld["wa"], 16)
                for oc in range(2):
                    ps = claim(oc, (f_done, 6 * p + oc + 1))
                    for c in range(2):
                        last = pe.matmul(ps[:], wa_q[:, c, oc * P:(oc + 1) * P], XT[:, c, p * PT:(p + 1) * PT],
                                         start=(c == 0), stop=(c == 1))
                    last.then_inc(q_ps, 1)
                for tt in range(TPP):
                    ps = claim(2 + tt, (f_done, 6 * p + tt + 3), (v_done, TPP * p + tt + 1))
                    for c in range(2):
                        last = pe.matmul(ps[:], XT[:, c, (TPP * p + tt) * P:(TPP * p + tt + 1) * P], wa_kv[:, c, :],
                                         start=(c == 0), stop=(c == 1))
                    last.then_inc(kv_ps, 1)

            def linear_attention(p):
                for j in range(2):
                    ps = claim(6 + j, (kvm_done, 2 * p + j + 1))
                    pe.wait_ge(f_done, 6 * p + 2 * j + 4)
                    pe.wait_ge(v_done, TPP * p + 2 * j + 2)
                    for c in range(2):
                        for s in range(2):
                            tt = 2 * j + s
                            last = pe.matmul(ps[:, c * NV:(c + 1) * NV], kf[p][:, tt, c * P:(c + 1) * P],
                                             vo[p][:, tt, c, :], start=(s == 0), stop=(s == 1))
                    last.then_inc(kva_ps, 1)
                for tt in range(TPP):
                    ps = claim(tt, (a_tok_done, TPP * p + tt + 1))
                    if tt % 2 == 0:
                        pe.wait_ge(kvm_done, 2 * p + tt // 2 + 1)
                    for c in range(2):
                        last = pe.matmul(ps[:, c * NV:(c + 1) * NV], qf[p][:, c, tt * P:(tt + 1) * P],
                                         kvm[:, tt // 2, c, :], start=True, stop=True)
                    last.then_inc(nd_ps, 1)

            def linear_out(p):
                ps = [claim(4 + c, (at_done, 2 * p + c + 1)) for c in range(2)]
                for tt in range(TPP):
                    pe.wait_ge(a_tok_done, TPP * p + tt + 1)
                    for c in range(2):
                        last = transpose(ps[c][:, tt * P:(tt + 1) * P], a_tok[:, tt % 2, c * P:(c + 1) * P])
                    last.then_inc(at_ps, 1)
                pe.wait_ge(at_done, 2 * p + 2)
                project_out(0, p, (6, 7), lambda k, tt: at0[:, k, tt * P:(tt + 1) * P], lambda k: wa_o[:, k, :], 2)

            def node_features(lp, step):
                l, p = lp // 2, lp % 2
                if step:
                    pass
                elif l == 0:
                    pe.wait_ge(ld["ctxt"], 16)
                    pe.wait_ge(wg_done, 1)
                else:
                    pe.wait_ge(b_h, 4 * p + 4)
                    pe.wait_ge(wg_done, 2)
                nch = 1 if l == 0 else 2

                def weights(c, a, b):
                    return wg0[:, a:b] if l == 0 else wg1[:, c, a:b]

                def nodes(c, a, b):
                    return CT[:, p * PT + a:p * PT + b] if l == 0 else ht[p][:, c, a:b]

                if step < TPP:
                    ps = claim(6 + step % 2, (ft_done, TPP * lp + step + 1))
                    for c in range(nch):
                        last = pe.matmul(ps[:, 0:GF], nodes(c, step * P, (step + 1) * P), weights(c, 0, GF),
                                         start=(c == 0), stop=(c == nch - 1))
                    last.then_inc(ft_ps, 1)
                    return
                ps = claim(6, (trow_done, lp + 1))
                for c in range(nch):
                    last = pe.matmul(ps[0:TR, :], weights(c, GF, GW), nodes(c, 0, PT),
                                     start=(c == 0), stop=(c == nch - 1))
                last.then_inc(tr_ps, 1)

            def neighbour_rows(hh):
                lp, h = hh // GH, hh % GH
                if h == 0:
                    pe.wait_ge(trow_done, lp + 1)
                ps = claim(h % 2, (b_tc, hh + 1))
                pe.matmul(ps[:], sel_r[:, h, :], trow[lp % 2], start=True, stop=True).then_inc(tb_ps, 1)

            def gat_turn(n):
                pe.wait_ge(b_norm, n + 1)
                ps = claim(2 + n % 2, moved(b_evd, b_eva, n))
                for mt in range(2):
                    for s in range(2):
                        last = transpose(ps[:, mt * S + s * P:mt * S + (s + 1) * P],
                                         pb[:, n % 3, s * S + mt * P:s * S + (mt + 1) * P])
                last.then_inc(b_pt, 1)

            def gat_mix(n):
                lp, i = n // 16, n % 16
                h, j = i // 2, i % 2
                b_ = 4 + 2 * (h // 4) + j
                if h % 4 == 0:
                    claim(b_, (b_m, 4 * lp + 2 * (h // 4) + j + 1))
                wait_moved(pe, b_evd, b_eva, n)
                q = 32 * (h % 4)
                for mt in range(2):
                    last = pe.matmul(bank[b_][q:q + GO, 0:S], ft[lp % 2][:, 2 * j + mt, h * GO:(h + 1) * GO],
                                     ptb[:, n % 2, mt * S:(mt + 1) * S], start=(mt == 0), stop=(mt == 1))
                last.then_inc(b_av, 1)

            def gat_out(p):
                pe.wait_ge(b_h, 8 + 4 * p + 4)
                for tt in range(TPP):
                    n = TILES + TPP * p + tt
                    if tt % 2 == 0:
                        ps = claim(6 + tt // 2, (r_done, n + 2))
                    for c in range(2):
                        last = transpose(ps[:, (tt % 2) * D + c * P:(tt % 2) * D + (c + 1) * P],
                                         ht[p][:, c, tt * P:(tt + 1) * P])
                    last.then_inc(y_ready, 1)

            def stage_b():
                for step in range(TPP + 1):
                    node_features(0, step)
                pe.wait_ge(casts_ready, 1)
                neighbour_rows(0)
                neighbour_rows(1)
                for k in range(GN + 6):
                    if k % 2 == 0 and 2 <= k // 2 + 1 < GN // 2:
                        neighbour_rows(k // 2 + 1)
                    if 3 <= k < GN + 3:
                        gat_turn(k - 3)
                    if 5 <= k < GN + 5:
                        gat_mix(k - 5)
                    if 8 <= k % 16 < 13 and k // 16 < 3:
                        node_features(k // 16 + 1, k % 16 - 8)
                    if k in FOLDS:
                        fold_queries(*FOLDS[k])
                    if k == 48 + 10:
                        gat_out(0)
                gat_out(1)

            def weight_sums():
                pe.wait_ge(abs_done, 3)
                ps = claim(5, (sums_done, 1))
                pe.matmul(ps[:, 0:3], ones[:], abs_sum[:], start=True, stop=True).then_inc(sum_ps, 1)

            def stage_c(p):
                pe.wait_ge(quant, 3)
                pe.wait_ge(xl_ready, 2 * (p + 1))
                for k in range(HC):
                    n = HC * p + k
                    for part, w in enumerate((w1t, w3t)):
                        ps = claim(2 * part + n % 2, (c_g, n + 1))
                        for i, (c, x_) in enumerate((c, x_) for c in range(2) for x_ in (xl[p], xh[p])):
                            last = pe.matmul(ps[:], w[:, c, k * P:(k + 1) * P], x_[:, c, :], start=(i == 0), stop=(i == 3))
                    last.then_inc(h1_ps, 1)
                if p == 0:
                    norm_transposes(1, 1)
                    turn_context()
                for tt in range(TPP):
                    n = 2 * TILES + TPP * p + tt
                    if tt % 2 == 0:
                        ps = claim(4 + tt // 2, (r_done, n + 2))
                    for i, (k, g_) in enumerate((k, g_) for k in range(HC) for g_ in (hg_lo, hg_hi)):
                        if tt == 0:
                            pe.wait_ge(c_lo, HC * p + k + 1)
                        last = pe.matmul(ps[:, (tt % 2) * D:(tt % 2 + 1) * D], g_[:, k, tt * P:(tt + 1) * P],
                                         w2t[:, k, :], start=(i == 0), stop=(i == 2 * HC - 1))
                    last.then_inc(y_ready, 1)

            def fold_queries(w, product, i, b_):
                if product == "g":
                    if i == 0:
                        pe.wait_ge(ld[f"fold_r{w}"], 32)
                    ps = claim(b_, (fo_gs, 2 * w + i + 1))
                    for h in range(4 * i, 4 * i + 4):
                        for q in range(2):
                            at = (h % 4) * P + q * MR
                            last = pe.matmul(ps[0:QCH, at:at + MR], mqr[:, h, q * QCH:(q + 1) * QCH],
                                             mkr[:, h, :], start=True, stop=True)
                    last.then_inc(fo_g, 1)
                elif product == "b":
                    ps = bank[b_]
                    if i == 0:
                        pe.wait_ge(fo_gs, 2 * w + 2)
                        pe.wait_ge(ld[f"fold_b{w}"], 16)
                        claim(b_, (fo_bs, w + 1))
                    for h in (2 * i, 2 * i + 1):
                        for q in range(2):
                            last = pe.matmul(ps[:, h * MR:(h + 1) * MR], mkcq[:, q, h, :],
                                             fold_g[:, h // 4, (h % 4) * P + q * MR:(h % 4) * P + (q + 1) * MR],
                                             start=(q == 0), stop=(q == 1))
                    if i == 3:
                        last.then_inc(fo_b, 1)
                else:
                    c, ps = i // 2, bank[b_]
                    if i % 2 == 0:
                        pe.wait_ge(fo_bs, w + 1)
                        pe.wait_ge(ld[f"fold_q{w}"], 16)
                        claim(b_, (fo_cs, 2 * w + c + 1))
                    for h in range(4 * (i % 2), 4 * (i % 2) + 4):
                        last = pe.matmul(ps[:, h * MR:(h + 1) * MR], mq[:, h, c * P:(c + 1) * P],
                                         fold_b[:, h * MR:(h + 1) * MR], start=True, stop=True)
                    if i % 2:
                        last.then_inc(fo_c, 1)

            def fold_outputs():
                pe.wait_ge(ld["fold2"], 32)
                for q in range(4):
                    ps = claim(q, (fo_es, q + 1))
                    for h in range(4 * q, 4 * q + 4):
                        last = pe.matmul(ps[64 * (h % 2):64 * (h % 2) + 64, (h // 2 % 2) * D:(h // 2 % 2 + 1) * D],
                                         mkckv[:, h, :], mo[:, h, :], start=True, stop=True)
                    last.then_inc(fo_e, 1)

            def stage_d(p):
                pe.wait_ge(ld["wd"], 32)
                pe.wait_ge(xt_ready, 4 + 2 * (p + 1))
                for tt in range(TPP):
                    n = TPP * p + tt
                    t = (TPP * p + tt) * P
                    ps, ps2 = claim(n % 2, (d_t1, n + 1)), claim(2 + n % 2, (d_v, n + 1))
                    for c in range(2):
                        pe.matmul(ps[:], XT[:, c, t:t + P], wd_in[:, c, 0:512], start=(c == 0), stop=(c == 1))
                    for c in range(2):
                        last = pe.matmul(ps2[:, 0:D], XT[:, c, t:t + P], wd_in[:, c, 512:768],
                                         start=(c == 0), stop=(c == 1))
                    last.then_inc(qkv_ps, 1)
                    if tt >= 1:
                        turn_heads(p, tt - 1)
                turn_heads(p, TPP - 1)
                pe.wait_ge(d_qkt, 4 * TPP * (p + 1))
                pe.wait_ge(d_v, TPP * (p + 1))

                def scores(i):
                    n, j, h = 32 * p + i, i // AH, i % AH
                    ps = claim(i % 3, (d_max, n + 1))
                    q, hc, t = 64 * (h % 2), h // 2, j * S
                    for s in range(2):
                        last = pe.matmul(ps[:, s * S:(s + 1) * S], qkt[q:q + 64, hc, t + s * P:t + (s + 1) * P],
                                         qkt[q:q + 64, 8 + hc, t:t + S], start=True, stop=True)
                    last.then_inc(d_s, 1)

                def turn(i):
                    n = 32 * p + i
                    pe.wait_ge(d_norm, n + 1)
                    ps = claim(3 + i % 2, moved(d_evd, d_eva, n))
                    for at, of in ((0, 0), (P, P), (2 * P, 2 * P)):
                        last = transpose(ps[:, at:at + P], pd[:, i % 4, of:of + P])
                    last.then_inc(d_pt, 1)

                def mix(i):
                    n, j, h = 32 * p + i, i // AH, i % AH
                    g = 8 * p + 4 * j + h // 4
                    b_ = 5 + g % 2
                    if h % 4 == 0:
                        claim(b_, (d_fin, g + 1))
                    wait_moved(pe, d_evd, d_eva, n)
                    q = 32 * (h % 4)
                    for kt in range(2):
                        last = pe.matmul(bank[b_][q:q + 32, kt * P:S], vp[:, 2 * j + kt, h * 32:(h + 1) * 32],
                                         ptd[:, i % 2, kt * S:kt * P + S], start=(kt == 0), stop=(kt == 1),
                                         skip_group_check=True)
                    last.then_inc(d_av, 1)

                for k in range(32 + 5):
                    if k < 32:
                        scores(k)
                    if 3 <= k < 35:
                        turn(k - 3)
                    if k >= 5:
                        mix(k - 5)
                pe.wait_ge(d_fin, 8 * (p + 1))
                project_out(3, p, (3, 4), lambda k, tt: atd[:, k, tt * P:(tt + 1) * P], lambda k: wd_out[:, k, :], 4)

            def turn_heads(p, tt):
                n = TPP * p + tt
                pe.wait_ge(d_hi, n + 1)
                pe.wait_ge(d_lo, n + 1)
                for part in range(4):
                    ps = claim(4 + part, (d_qkt, 4 * n + part + 1))
                    for c in range(4):
                        last = transpose(ps[:, c * P:(c + 1) * P], rp[:, n % 2, (4 * part + c) * P:(4 * part + c + 1) * P])
                    last.then_inc(rp_ps, 1)

            def turn_context():
                pe.wait_ge(kvr_done, 1)
                for p in range(NPAIR):
                    ps = claim(6 + p, (kvt_done, p + 1))
                    for tt in range(TPP):
                        last = transpose(ps[:, tt * P:(tt + 1) * P],
                                         KVR[:, TPP * p + tt, :, :].rearrange("p a b -> p (a b)"))
                    last.then_inc(kvt_ps, 1)

            def stage_e(p):
                pe.wait_ge(xt_ready, 8 + 2 * (p + 1))
                pe.wait_ge(fo_cs, 4)
                for m in range(8):
                    ps = claim(m % 4, (qc_done, 8 * p + m + 1))
                    for c in range(2):
                        last = pe.matmul(ps[:], WC[:, c, m * P:(m + 1) * P], XT[:, c, p * PT:(p + 1) * PT],
                                         start=(c == 0), stop=(c == 1))
                    last.then_inc(qc_ps, 1)
                pe.wait_ge(kvt_done, 2)
                pe.wait_ge(qc_done, 8 * (p + 1))

                def scores(i):
                    n, j, h = 32 * p + i, i // MH, i % MH
                    ps = claim(i % 3, (e_exp, n + 1))
                    q = 64 * (h % 2)
                    for s in range(2):
                        last = pe.matmul(ps[:, s * S:(s + 1) * S], qc[q:q + 64, h // 2, j * S + s * P:j * S + (s + 1) * P],
                                         KVT[q:q + 64, p * PT + j * S:p * PT + (j + 1) * S], start=True, stop=True)
                    last.then_inc(e_s, 1)

                def turn(i):
                    n = 32 * p + i
                    pe.wait_ge(e_norm, n + 1)
                    ps = claim(3 + i % 2, moved(e_evd, e_eva, n))
                    for lt in range(2):
                        for s in range(2):
                            last = transpose(ps[:, lt * S + s * P:lt * S + (s + 1) * P],
                                             pe_[:, i % 4, s * S + lt * P:s * S + (lt + 1) * P])
                    last.then_inc(e_pt, 1)

                def mix(i):
                    n, j, h = 32 * p + i, i // MH, i % MH
                    g = 8 * p + 4 * j + h // 4
                    b_ = 5 + g % 2
                    if h % 4 == 0:
                        claim(b_, (e_ctx, g + 1))
                    wait_moved(pe, e_evd, e_eva, n)
                    q = 64 * (h % 2)
                    for lt in range(2):
                        last = pe.matmul(bank[b_][q:q + 64, (h // 2 % 2) * S:(h // 2 % 2 + 1) * S],
                                         KVR[:, TPP * p + 2 * j + lt, 0, :], pte[:, i % 2, lt * S:(lt + 1) * S],
                                         start=(lt == 0), stop=(lt == 1))
                    last.then_inc(e_av, 1)

                for k in range(32 + 5):
                    if k < 32:
                        scores(k)
                    if 3 <= k < 35:
                        turn(k - 3)
                    if k >= 5:
                        mix(k - 5)
                pe.wait_ge(e_ctx, 8 * (p + 1))
                pe.wait_ge(fo_es, 4)
                project_out(4, p, (3, 4), lambda k, tt: ctx_lat_t[:, k, tt * P:(tt + 1) * P], lambda k: WE[:, k, :], 8)

            def gate(p):
                pe.wait_ge(xt_ready, 12 + 2 * (p + 1))
                pe.wait_ge(ld["gate"], 16)
                ps = claim(4, (gap_done, p + 1))
                for tt in range(TPP):
                    t = (TPP * p + tt) * P
                    for c in range(2):
                        last = pe.matmul(ps[:, tt * NE:(tt + 1) * NE], XT[:, c, t:t + P], gate_sb[:, c, :],
                                         start=(c == 0), stop=(c == 1))
                last.then_inc(lg_ps, 1)

            def expert_in(e, p):
                pe.wait_ge(slot_ld[e % 4], 16 * (e // 4 + 1))
                slot = (e % 4) * 1536
                for mc in range(2):
                    n = (2 * e + p) * 2 + mc
                    for part in range(2):
                        w = carve(MW, slot + 512 * part, 2, D)
                        ps = claim(2 * part + n % 2, (m_g, n + 1))
                        for c in range(2):
                            last = pe.matmul(ps[:], w[:, c, mc * P:(mc + 1) * P], XT[:, c, p * PT:(p + 1) * PT],
                                             start=(c == 0), stop=(c == 1))
                    last.then_inc(m_h, 1)

            def expert_out(e, p):
                g = 2 * e + p
                pe.wait_ge(m_g, 2 * g + 2)
                w = carve(MW, (e % 4) * 1536 + 1024, 2, D)
                for tp in range(2):
                    ps = claim(4 + 2 * (g % 2) + tp, (m_acc, TPP * g + 2 * tp + 2))
                    for tt in range(2 * tp, 2 * tp + 2):
                        for mc in range(2):
                            last = pe.matmul(ps[:, (tt % 2) * D:(tt % 2 + 1) * D],
                                             gm[:, (2 * g + mc) % 4, tt * P:(tt + 1) * P], w[:, mc, :],
                                             start=(mc == 0), stop=(mc == 1))
                    last.then_inc(m_y, 1)

            pe.wait_ge(consts_ready, 1)
            project_in(0)
            project_in(1)
            linear_attention(0)
            pe.wait_ge(ld["ident"], 16)
            linear_out(0)
            weight_sums()
            linear_attention(1)
            linear_out(1)
            stage_b()
            norm_transposes(1, 0)
            stage_c(0)
            stage_c(1)
            fold_outputs()
            norm_transposes(2, 0)
            stage_d(0)
            norm_transposes(2, 1)
            stage_d(1)
            norm_transposes(3, 0)
            stage_e(0)
            norm_transposes(3, 1)
            stage_e(1)
            norm_transposes(4, 0)
            gate(0)
            expert_in(0, 0)
            norm_transposes(4, 1)
            gate(1)
            units = [(e, p) for e in range(NE) for p in range(NPAIR)]
            for u in range(1, len(units)):
                expert_in(*units[u])
                expert_out(*units[u - 1])
            expert_out(*units[-1])

        @block.scalar
        def _(act):
            def copy(dst, src, scale=1.0):
                return act.activation(dst, src, ACT.Copy, scale=scale)

            def norm_moves(L, p):
                for c in range(2):
                    n = (2 * (L - 1) + p) * 2 + c
                    act.wait_ge(xt_ps, n + 1)
                    if L == 1:
                        copy(xh[p][:, c, :], bank[6 + c][:]).then_inc(xt_ready, 1)
                        continue
                    copy(XT[:, c, p * PT:(p + 1) * PT], bank[6 + c][:]).then_inc(xt_ready, 1)

            def stage_a(p):
                for i in range(6):
                    n = 6 * p + i
                    if i < TPP:
                        act.wait_ge(kv_ps, TPP * p + i + 1)
                        copy(vo[p][:, i, :, 0:P], bank[2 + i][:, D:2 * D].rearrange("p (c n) -> p c n", c=2))\
                            .then_inc(v_done, 1)
                    act.wait_ge(f_min, n + 1)
                    w = 512 if i < 2 else D
                    act.activation(fmin[:, n % 3, 0:w], fmin[:, n % 3, 0:w], ACT.Exp).then_inc(f_exp, 1)

            def linear_out(p):
                act.wait_ge(at_ps, TPP * (p + 1))
                for c in range(2):
                    copy(at0[:, c, :], bank[4 + c][:]).then_inc(at_done, 1)

            def node_features(lp, step):
                u = lp % 2
                if lp >= 2 and step == 0:
                    act.wait_ge(b_e, 16 * (lp - 1))
                    act.wait_ge(b_a2, 16 * (lp - 1))
                if step < TPP:
                    act.wait_ge(ft_ps, TPP * lp + step + 1)
                    copy(ft[u][:, step, :], bank[6 + step % 2][:, 0:GH * GO])
                    copy(sneg[u][:, step, :], bank[6 + step % 2][:, GH * GO:GH * GO + GH], -1.0).then_inc(ft_done, 1)
                else:
                    act.wait_ge(tr_ps, lp + 1)
                    copy(trow[u], bank[6][0:TR, :], -1.0).then_inc(tr_done, 1)

            def neighbour_rows(hh):
                act.wait_ge(tb_ps, hh + 1)
                if hh >= 2:
                    act.wait_ge(b_a2, 2 * hh - 2)
                    act.wait_ge(b_lr, 2 * hh - 2)
                copy(tneg[:, hh % 2, :], bank[hh % 2][:]).then_inc(b_tc, 1)

            def stage_b():
                for step in range(TPP + 1):
                    node_features(0, step)
                neighbour_rows(0)
                for k in range(GN + 8):
                    if k % 2 == 0 and k // 2 + 1 < GN // 2:
                        neighbour_rows(k // 2 + 1)
                    if 1 <= k <= GN:
                        n = k - 1
                        act.wait_ge(b_e, n + 1)
                        if n >= 3:
                            act.wait_ge(b_pt, n - 2)
                        if n >= 4:
                            act.wait_ge(b_norm, n - 3)
                        for s in range(2):
                            last = act.activation(pb[:, n % 3, s * S:(s + 1) * S], eb[:, n % 2, s * S:(s + 1) * S],
                                                  ACT.Exp, bias=nmax_b[:, n % 4, s:s + 1], scale=-1.0,
                                                  accum_out=sum_b[:, n % 4, s:s + 1])
                        last.then_inc(b_exp, 1)
                    n = k - 4
                    if 0 <= n < GN and n % 2:
                        act.wait_ge(b_pt, n + 1)
                        if n >= 2:
                            act.wait_ge(b_av, n - 1)
                        copy(ptb[:, n % 2, :], bank[2 + n % 2][:]).then_inc(b_eva, 1)
                    n = k - 7
                    if 0 <= n < GN and n // 2 % 4 == 3:
                        f = n // 8 * 2 + n % 2
                        act.wait_ge(b_m, f + 1)
                        act.activation(g_m[:, f % 2, :], g_m[:, f % 2, :], ACT.Exp).then_inc(b_em, 1)
                    if k - 1 in FOLDS:
                        fold_queries(*FOLDS[k - 1])
                    if 8 <= k % 16 < 13 and k // 16 < 3:
                        node_features(k // 16 + 1, k % 16 - 8)

            def fold_queries(w, product, i, b_):
                if product == "g":
                    act.wait_ge(fo_g, 2 * w + i + 1)
                    copy(fold_g[:, i, :], bank[b_][0:QCH, :]).then_inc(fo_gs, 1)
                elif product == "b" and i == 3:
                    act.wait_ge(fo_b, w + 1)
                    copy(fold_b, bank[b_][:]).then_inc(fo_bs, 1)
                elif product == "c" and i % 2:
                    c = i // 2
                    act.wait_ge(fo_c, 2 * w + c + 1)
                    copy(WC[:, c, w * 512:(w + 1) * 512], bank[b_][:]).then_inc(fo_cs, 1)

            def fold_outputs():
                for q in range(4):
                    act.wait_ge(fo_e, q + 1)
                    copy(WE[:, 2 * q:2 * q + 2, :], bank[q][:].rearrange("p (a n) -> p a n", a=2)).then_inc(fo_es, 1)

            def stage_c(p):
                if p:
                    act.wait_ge(y_ready, 2 * TILES + TPP)
                for k in range(HC + 1):
                    n = HC * p + k
                    if k < HC:
                        act.wait_ge(h1_ps, n + 1)
                        if n >= 2:
                            act.wait_ge(c_g, n - 1)
                        act.activation(silu_c[:, n % 2, :], bank[n % 2][:], ACT.Silu, scale=full_scale[:, 0:1])\
                           .then_inc(c_silu, 1)
                    if k:
                        act.wait_ge(c_g, n)
                        copy(hg_hi[:, k - 1, :], hg[:, (n - 1) % 2, :]).then_inc(c_hi, 1)

            def turn_context():
                for p in range(NPAIR):
                    act.wait_ge(kvt_ps, p + 1)
                    copy(KVT[:, p * PT:(p + 1) * PT], bank[6 + p][:]).then_inc(kvt_done, 1)

            def stage_d(p):
                if p == 0:
                    act.wait_ge(d_zero, 1)

                def move_heads(tt):
                    for part in range(4):
                        n = 4 * (TPP * p + tt) + part
                        act.wait_ge(rp_ps, n + 1)
                        copy(qkt[:, 4 * part:4 * part + 4, tt * P:(tt + 1) * P],
                             bank[4 + part][:].rearrange("p (c n) -> p c n", c=4)).then_inc(d_qkt, 1)

                for tt in range(TPP):
                    n = TPP * p + tt
                    act.wait_ge(qkv_ps, n + 1)
                    copy(vp[:, tt, :].rearrange("p (h i) -> p h i", h=AH)[:, :, 0:AD],
                         bank[2 + n % 2][:, 0:D].rearrange("p (h i) -> p h i", h=AH)).then_inc(d_v, 1)
                    act.wait_ge(d_rope, n + 1)
                    if n >= 2:
                        act.wait_ge(rp_ps, 4 * (n - 1))
                    slots = rp[:, n % 2, :].bitcast(F32R).rearrange("p (a h d i) -> p a h d i", a=2, h=AH, d=4)
                    v = roped[:, n % 2, :].rearrange("p (a h i) -> p a h i", a=2, h=AH)
                    for a, to in enumerate((slots[:, 0, :, 0:2, :], slots[:, 1, :, 0::2, :])):
                        last = copy(to, v[:, a, :, :].unsqueeze(2).broadcast_to([P, AH, 2, AD]))
                    last.then_inc(d_hi, 1)
                    if tt >= 1:
                        move_heads(tt - 1)
                move_heads(TPP - 1)
                for k in range(36):
                    if k < 32:
                        n = 32 * p + k
                        act.wait_ge(d_max, n + 1)
                        if n >= 4:
                            act.wait_ge(d_pt, n - 3)
                        for s in range(2):
                            o, w = (0, P) if s == 0 else (P, 2 * P)
                            last = act.activation(pd[:, n % 4, o:o + w], ns_d[:, n % 3, o:o + w], ACT.Exp,
                                                  bias=nmin_d[:, n % 4, s:s + 1], scale=-1.0,
                                                  accum_out=sum_d[:, n % 4, s:s + 1])
                        last.then_inc(d_exp, 1)
                    i = k - 4
                    if i >= 0 and i % 2:
                        n = 32 * p + i
                        act.wait_ge(d_pt, n + 1)
                        if n >= 2:
                            act.wait_ge(d_av, n - 1)
                        copy(ptd[:, i % 2, :], bank[3 + i % 2][:, 0:384]).then_inc(d_eva, 1)

            def stage_e(p):
                for m in range(8):
                    act.wait_ge(qc_ps, 8 * p + m + 1)
                    copy(qc[:, m, :], bank[m % 4][:]).then_inc(qc_done, 1)
                for k in range(39):
                    if k < 32:
                        n = 32 * p + k
                        act.wait_ge(e_max, n + 1)
                        if n >= 4:
                            act.wait_ge(e_pt, n - 3)
                        for s in range(2):
                            last = act.activation(pe_[:, k % 4, s * S:(s + 1) * S], bank[k % 3][:, s * S:(s + 1) * S],
                                                  ACT.Exp, bias=nmax_e[:, n % 4, s:s + 1],
                                                  accum_out=sum_e[:, n % 4, s:s + 1])
                        last.then_inc(e_exp, 1)
                    i = k - 4
                    if 0 <= i < 32 and i % 2:
                        n = 32 * p + i
                        act.wait_ge(e_pt, n + 1)
                        if n >= 2:
                            act.wait_ge(e_av, n - 1)
                        copy(pte[:, i % 2, :], bank[3 + i % 2][:]).then_inc(e_eva, 1)
                    i = k - 6
                    if i >= 0 and i % 4 == 3:
                        n, q = 32 * p + i, i // 4
                        act.wait_ge(e_av, n + 1)
                        copy(ctx_lat_t[:, 2 * (q % 4):2 * (q % 4) + 2, (q // 4) * S:(q // 4 + 1) * S],
                             bank[5 + q % 2][:].rearrange("p (a n) -> p a n", a=2)).then_inc(e_ctx, 1)

            def gate(p):
                act.wait_ge(gap_ready, p + 1)
                g = gap[:, TPP * p:TPP * (p + 1)]
                act.activation(g, g, ACT.Exp).then_inc(gap_exp, 1)

            def expert_in(e, p):
                for mc in range(2):
                    n = (2 * e + p) * 2 + mc
                    act.wait_ge(m_h, n + 1)
                    if n >= 2:
                        act.wait_ge(m_g, n - 1)
                    act.activation(silu_m[:, n % 2, :], bank[n % 2][:], ACT.Silu).then_inc(m_silu, 1)

            stage_a(0)
            stage_a(1)
            linear_out(0)
            linear_out(1)
            stage_b()
            norm_moves(1, 0)
            stage_c(0)
            norm_moves(1, 1)
            turn_context()
            stage_c(1)
            fold_outputs()
            norm_moves(2, 0)
            stage_d(0)
            norm_moves(2, 1)
            stage_d(1)
            norm_moves(3, 0)
            stage_e(0)
            norm_moves(3, 1)
            stage_e(1)
            norm_moves(4, 0)
            gate(0)
            expert_in(0, 0)
            norm_moves(4, 1)
            gate(1)
            for e, p in [(e, p) for e in range(NE) for p in range(NPAIR)][1:]:
                expert_in(e, p)

        @block.vector
        def _(dve):
            links = [0]

            def link(ins):
                links[0] += 1
                ins.then_inc(dve_link, 1)
                dve.wait_ge(dve_link, links[0])

            def gat_weights():
                dve.wait_ge(ld["ga"], 16)
                dve.wait_ge(ld["wg0"], 16)
                dve.wait_ge(ld["wg1"], 16)
                for step, (w, rows, first) in enumerate(((wg0[:, :], CTX, 0), (wg1[:, 0, :], P, 2), (wg1[:, 1, :], P, 2))):
                    for k in range(2):
                        t = prod_tmp[0:rows, :]
                        link(dve.tensor_tensor(t, w[:, 0:GH * GO], a_bc[0:rows, first + k, :], ALU.mult))
                        for o in (GH * GO,) if k == 0 else (GF, GF + 32):
                            last = dve.tensor_reduce(w[:, o:o + GH], t.rearrange("p (h o) -> p h o", h=GH), AX.X, ALU.add)
                        link(last)
                    if rows == CTX or step == 2:
                        dve.sem_inc(wg_done, 1)

            def norm_stats(L, p):
                if L:
                    dve.wait_ge(x_ready, (L - 1) * TILES + TPP * (p + 1))
                for tt in range(TPP):
                    T = TPP * p + tt
                    n = L * TILES + T
                    if L < 5:
                        dve.wait_ge(y_ready, n - tt % 2 + 2)
                        b_ = {0: (6, 7), 1: (6, 7), 2: (4, 5), 3: (3, 4), 4: (3, 4)}[L][tt // 2]
                        y = bank[b_][:, (tt % 2) * D:(tt % 2 + 1) * D]
                        if L == 2:
                            dve.scalar_tensor_tensor(R[:, T, :], y, out_scale[:], X[:, T, :], ALU.mult, ALU.add)\
                               .then_inc(r_done, 1)
                            continue
                        dve.tensor_tensor(R[:, T, :], y, X[:, T, :], ALU.add).then_inc(r_done, 1)
                if L < 5:
                    dve.wait_ge(r_done, L * TILES + TPP * (p + 1))
                for tt in range(TPP):
                    last = dve.bn_stats(stat6[:, TPP * p + tt, :], R[:, TPP * p + tt, :])
                link(last)
                for tt in range(TPP):
                    last = dve.bn_aggr(mean_var[:, TPP * p + tt, :], stat6[:, TPP * p + tt, :])
                last.then_inc(stats_ready, 1)

            def norm_scale(L, p):
                dve.wait_ge(rstd_ready, 2 * L + p + 1)
                dve.wait_ge(stats_ready, 2 * L + p + 1)
                for tt in range(TPP):
                    T = TPP * p + tt
                    dve.tensor_scalar(X[:, T, :], R[:, T, :], mean_var[:, T, 0:1], rstd[:, T:T + 1],
                                      ALU.subtract, ALU.mult).then_inc(x_ready, 1)

            def norm(L, p):
                norm_stats(L, p)
                norm_scale(L, p)

            def stage_a(p):
                def source(i):
                    return bank[i][:] if i < 2 else bank[i][:, 0:D]

                for k in range(7):
                    if k < 6:
                        n = 6 * p + k
                        dve.wait_ge(q_ps if k < 2 else kv_ps, (2 * p + k + 1) if k < 2 else (TPP * p + k - 1))
                        if k >= 2:
                            dve.wait_ge(v_done, TPP * p + k - 1)
                        if n >= 3:
                            dve.wait_ge(f_done, n - 2)
                        w = 512 if k < 2 else D
                        dve.tensor_scalar(fmin[:, n % 3, 0:w], source(k), 0.0, None, ALU.min).then_inc(f_min, 1)
                    if k >= 1:
                        i = k - 1
                        n = 6 * p + i
                        dve.wait_ge(f_exp, n + 1)
                        w = 512 if i < 2 else D
                        o = qf[p][:, i, :] if i < 2 else kf[p][:, i - 2, :]
                        dve.scalar_tensor_tensor(o, source(i), 0.0, fmin[:, n % 3, 0:w], ALU.max, ALU.add)\
                           .then_inc(f_done, 1)

            def linear_attention(p):
                if p == 0:
                    dve.wait_ge(ld["block"], 16)
                else:
                    dve.wait_ge(nd_ps, TPP)
                for j in range(2):
                    dve.wait_ge(kva_ps, 2 * p + j + 1)
                    for c in range(2):
                        last = dve.tensor_tensor(kvm[:, j, c, :], bank[6 + j][:, c * NV:(c + 1) * NV],
                                                 block_mask[:], ALU.mult)
                    last.then_inc(kvm_done, 1)
                if p:
                    dve.wait_ge(a_tok_done, TPP)
                for tt in range(TPP):
                    n = TPP * p + tt
                    dve.wait_ge(nd_ps, n + 1)
                    if n >= 2:
                        dve.wait_ge(at_ps, n - 1)
                    num_den = bank[tt][:, 0:2 * NV].rearrange("p (c n) -> p c n", c=2)
                    d = a_den[:, tt, :, :]
                    link(dve.tensor_scalar(d, num_den[:, :, P:NV], 1e-6, None, ALU.add))
                    link(dve.reciprocal(d, d))
                    for c in range(2):
                        last = dve.tensor_tensor(a_tok[:, n % 2, c * P:(c + 1) * P].rearrange("p (h i) -> p h i", i=AD),
                                                 num_den[:, c, 0:P].rearrange("p (h i) -> p h i", i=AD),
                                                 d[:, c, :].unsqueeze(2).broadcast_to([P, 8, AD]), ALU.mult)
                    last.then_inc(a_tok_done, 1)

            def gat_mask(lp):
                p = lp % 2
                dve.wait_ge(x_ready, TPP * (p + 1))
                if lp >= 2:
                    dve.wait_ge(b_e, 16 * (lp - 1))
                link(dve.tensor_scalar(mask[lp % 2][:, :, :], X[:, TPP * p:TPP * (p + 1), :], 1.0, -1e10,
                                       ALU.subtract, ALU.mult))

            def split_rows(lp):
                dve.wait_ge(tr_done, lp + 1)
                rest = trow[lp % 2][32:TR, :]
                dve.scalar_tensor_tensor(rest, bank[6][32:TR, :], -1.0, rest.bitcast(F32), ALU.mult, ALU.subtract)\
                   .then_inc(trow_done, 1)

            def stage_b():
                split_rows(0)
                for k in range(GN + 9):
                    if k % 16 == 13 and k // 16 < 3:
                        split_rows(k // 16 + 1)
                    n = k - 2
                    if 0 <= n < GN:
                        dve.wait_ge(b_exp, n + 1)
                        dve.reciprocal(sum_b[:, n % 4, :], sum_b[:, n % 4, :]).then_inc(b_rec, 1)
                    if k < GN and k % 16 == 0:
                        gat_mask(k // 16)
                    if k < GN:
                        n, lp, h, j = k, k // 16, k // 2, k % 2
                        if k == 0:
                            dve.wait_ge(ft_done, TPP)
                        dve.wait_ge(b_tc, h + 1)
                        dve.wait_ge(b_a2, n + 1)
                        if n >= 2:
                            dve.wait_ge(b_e, n - 1)
                        for s in range(2):
                            last = dve.scalar_tensor_tensor(
                                nl[:, n % 2, s * S:(s + 1) * S], tneg[:, h % 2, j * S:(j + 1) * S],
                                sneg[lp % 2][:, 2 * j + s, h % GH:h % GH + 1], a2[:, n % 2, s * S:(s + 1) * S],
                                ALU.add, ALU.min)
                        last.then_inc(b_lr, 1)
                        dve.wait_ge(b_lr, n + 1)
                        if n >= 2:
                            dve.wait_ge(b_exp, n - 1)
                        for s in range(2):
                            last = dve.tensor_tensor_reduce(eb[:, n % 2, s * S:(s + 1) * S], nl[:, n % 2, s * S:(s + 1) * S],
                                                            mask[lp % 2][:, 2 * j + s, :], 1.0, BIG, ALU.add, ALU.min,
                                                            nmax_b[:, n % 4, s:s + 1])
                        last.then_inc(b_e, 1)
                    n = k - 4
                    if 0 <= n < GN and n % 2 == 0:
                        dve.wait_ge(b_pt, n + 1)
                        if n >= 2:
                            dve.wait_ge(b_av, n - 1)
                        dve.tensor_copy(ptb[:, n % 2, :], bank[2 + n % 2][:]).then_inc(b_evd, 1)
                    n = k - 6
                    if 0 <= n < GN and n // 2 % 4 == 3:
                        lp, g, j = n // 16, n // 8 % 2, n % 2
                        f = 4 * lp + 2 * g + j
                        dve.wait_ge(b_av, n + 1)
                        if f >= 2:
                            dve.wait_ge(b_h, f - 1)
                        ps = bank[4 + 2 * g + j][:, 0:S]
                        bias = gbias[:, 2 * (lp // 2) + g:2 * (lp // 2) + g + 1]
                        dve.tensor_scalar(g_v[:, j, :], ps, bias, 0.0, ALU.add, ALU.max)
                        dve.tensor_scalar(g_m[:, j, :], ps, bias, 0.0, ALU.add, ALU.min).then_inc(b_m, 1)
                    n = k - 8
                    if 0 <= n < GN and n // 2 % 4 == 3:
                        lp, g, j = n // 16, n // 8 % 2, n % 2
                        f = 4 * lp + 2 * g + j
                        dve.wait_ge(b_em, f + 1)
                        dve.wait_ge(b_m, f + 1)
                        dve.scalar_tensor_tensor(ht[lp % 2][:, g, j * S:(j + 1) * S], g_m[:, j, :], -1.0, g_v[:, j, :],
                                                 ALU.add, ALU.add).then_inc(b_h, 1)
                    if k == 20:
                        context_rope()
                    if k == 48 + 11:
                        norm_stats(1, 0)
                    if k == 48 + 14:
                        norm_scale(1, 0)

            def weight_abs():
                for i, (w, what) in enumerate(zip(raw, ("ffn1", "ffn3", "ffn2"))):
                    dve.wait_ge(ld[what], 16)
                    dve.tensor_reduce(abs_sum[:, i:i + 1], w, AX.X, ALU.add,
                                      apply_absolute_value=True).then_inc(abs_done, 1)

            def weight_scales():
                dve.wait_ge(sum_ps, 1)
                for dst, f in ((half_scale, 0.5), (neg_half, -0.5), (full_scale, 1.0)):
                    last = dve.tensor_scalar(dst[:], bank[5][:, 0:3], f / (HID * D), None, ALU.mult)
                last.then_inc(sums_done, 1)

            def ternary_weights():
                dve.wait_ge(sums_done, 1)
                dve.tensor_tensor(out_scale[:], full_scale[:, 1:2], full_scale[:, 2:3], ALU.mult)
                for i, w in enumerate(raw):
                    if i:
                        dve.wait_ge(quant, i)
                    n = w.shape[1]
                    link(dve.tensor_scalar(below[:, 0:n], w, neg_half[:, i:i + 1], None, ALU.is_lt))
                    dve.scalar_tensor_tensor(carve(ternary, 2 * HP * i, n), w, half_scale[:, i:i + 1],
                                             below[:, 0:n], ALU.is_gt, ALU.subtract).then_inc(quant, 1)
                dve.wait_ge(quant, 3)

            def context_rope():
                dve.wait_ge(ld["ctxr"], 16)
                dve.wait_ge(ld["mrope"], 16)
                kv, hf = KVR[:, :, 0, :], CTX // 2
                dve.wait_ge(y_ready, TILES)
                for s in range(2):
                    dve.tensor_tensor(kv_cos[:, s::2, :], kv[:, s::2, :],
                                      mrope[:, 0, s, :].unsqueeze(1).broadcast_to([P, B, CTX]), ALU.mult)
                    for a in range(2):
                        last = dve.tensor_tensor(kv_sin[:, s::2, a * hf:(a + 1) * hf], kv[:, s::2, (1 - a) * hf:(2 - a) * hf],
                                                 mrope[:, 1, s, a * hf:(a + 1) * hf].unsqueeze(1).broadcast_to([P, B, hf]),
                                                 ALU.mult)
                link(last)
                for a in range(2):
                    last = dve.tensor_tensor(KVR[:, :, a, :], kv_cos[:, :, :], kv_sin[:, :, :], ALU.add)
                last.then_inc(kvr_done, 1)

            def x_rest(p):
                for c in range(2):
                    dve.wait_ge(xt_ready, 2 * p + c + 1)
                    dve.tensor_tensor(xl[p][:, c, :], bank[6 + c][:], xh[p][:, c, :].bitcast(F32), ALU.subtract)\
                       .then_inc(xl_ready, 1)

            def stage_c(p):
                if p == 0:
                    dve.wait_ge(y_ready, 2 * TILES)
                else:
                    dve.wait_ge(y_ready, 2 * TILES + TPP)
                for k in range(HC + 1):
                    n = HC * p + k
                    if k < HC:
                        dve.wait_ge(c_silu, n + 1)
                        if n >= 2:
                            dve.wait_ge(c_lo, n - 1)
                        dve.tensor_tensor(hg[:, n % 2, :], silu_c[:, n % 2, :], bank[2 + n % 2][:], ALU.mult)\
                           .then_inc(c_g, 1)
                    if k:
                        dve.wait_ge(c_hi, n)
                        dve.wait_ge(c_g, n)
                        dve.tensor_tensor(hg_lo[:, k - 1, :], hg[:, (n - 1) % 2, :], hg_hi[:, k - 1, :].bitcast(F32),
                                          ALU.subtract).then_inc(c_lo, 1)

            def stage_d(p):
                if p == 0:
                    dve.wait_ge(d_zero, 1)
                    dve.wait_ge(ld["tri"], 16)
                    dve.wait_ge(ld["rope"], 16)
                def rest(n):
                    dve.wait_ge(d_hi, n + 1)
                    v = roped[:, n % 2, :].rearrange("p (a h i) -> p a h i", a=2, h=AH)
                    slots = rp[:, n % 2, :].rearrange("p (a h d i) -> p a h d i", a=2, h=AH, d=4)
                    for a, hi, lo in ((0, slice(0, 2), slice(2, 4)), (1, slice(0, 4, 2), slice(1, 4, 2))):
                        last = dve.tensor_tensor(slots[:, a, :, lo, :], v[:, a, :, :].unsqueeze(2).broadcast_to([P, AH, 2, AD]),
                                                 slots[:, a, :, hi, :], ALU.subtract)
                    last.then_inc(d_lo, 1)

                for tt in range(TPP):
                    n, s = TPP * p + tt, tt % 2
                    dve.wait_ge(qkv_ps, n + 1)

                    def heads(v):
                        return v.rearrange("p (a h i) -> p a h i", a=2, h=AH)

                    def table(cs, lo, hi):
                        return rope[:, cs, s, :, lo:hi].unsqueeze(2).broadcast_to([P, 2, AH, hi - lo])
                    qk, hf = heads(bank[n % 2][:]), AD // 2
                    if n:
                        dve.wait_ge(d_rope, n)
                    dve.tensor_tensor(heads(t1), qk, table(0, 0, AD), ALU.mult)
                    for a in range(2):
                        last = dve.tensor_tensor(heads(t2)[:, :, :, a * hf:(a + 1) * hf],
                                                 qk[:, :, :, (1 - a) * hf:(2 - a) * hf],
                                                 table(1, a * hf, (a + 1) * hf), ALU.mult)
                    last.then_inc(d_t1, 1)
                    dve.wait_ge(d_t1, n + 1)
                    if n >= 2:
                        dve.wait_ge(d_hi, n - 1)
                        dve.wait_ge(d_lo, n - 1)
                    dve.tensor_tensor(roped[:, n % 2, :], t1, t2, ALU.add).then_inc(d_rope, 1)
                    if tt:
                        if n >= 3:
                            dve.wait_ge(rp_ps, 4 * (n - 2))
                        rest(n - 1)
                dve.wait_ge(rp_ps, 4 * (TPP * (p + 1) - 2))
                rest(TPP * (p + 1) - 1)
                for k in range(38):
                    i = k - 2
                    if 0 <= i < 32:
                        n = 32 * p + i
                        dve.wait_ge(d_exp, n + 1)
                        dve.reciprocal(sum_d[:, n % 4, :], sum_d[:, n % 4, :]).then_inc(d_rec, 1)
                    if k < 32:
                        n = 32 * p + k
                        dve.wait_ge(d_s, n + 1)
                        if n >= 3:
                            dve.wait_ge(d_exp, n - 2)
                        for s in range(2):
                            o, w = (0, P) if s == 0 else (P, 2 * P)
                            last = dve.tensor_tensor_reduce(ns_d[:, n % 3, o:o + w], bank[k % 3][:, s * S:s * S + w],
                                                            tri[:, 2 * P - w:2 * P], 1.0, BIG, ALU.add, ALU.min,
                                                            nmin_d[:, n % 4, s:s + 1])
                        last.then_inc(d_max, 1)
                    i = k - 4
                    if 0 <= i < 32 and i % 2 == 0:
                        n = 32 * p + i
                        dve.wait_ge(d_pt, n + 1)
                        if n >= 2:
                            dve.wait_ge(d_av, n - 1)
                        dve.tensor_copy(ptd[:, i % 2, :], bank[3 + i % 2][:, 0:384]).then_inc(d_evd, 1)
                    i = k - 6
                    if i >= 0 and i % 4 == 3:
                        n, q = 32 * p + i, i // 4
                        dve.wait_ge(d_av, n + 1)
                        dve.tensor_copy(atd[:, q % 4, (q // 4) * S:(q // 4 + 1) * S], bank[5 + q % 2][:, 0:S])\
                           .then_inc(d_fin, 1)

            def stage_e(p):
                for k in range(37):
                    i = k - 2
                    if 0 <= i < 32:
                        n = 32 * p + i
                        dve.wait_ge(e_exp, n + 1)
                        dve.reciprocal(sum_e[:, n % 4, :], sum_e[:, n % 4, :]).then_inc(e_rec, 1)
                    if k < 32:
                        n = 32 * p + k
                        dve.wait_ge(e_s, n + 1)
                        if n >= 4:
                            dve.wait_ge(e_exp, n - 3)
                        dve.tensor_reduce(nmax_e[:, n % 4, :], bank[k % 3][:].rearrange("p (s n) -> p s n", s=2),
                                          AX.X, ALU.max, negate=True).then_inc(e_max, 1)
                    i = k - 4
                    if 0 <= i < 32 and i % 2 == 0:
                        n = 32 * p + i
                        dve.wait_ge(e_pt, n + 1)
                        if n >= 2:
                            dve.wait_ge(e_av, n - 1)
                        dve.tensor_copy(pte[:, i % 2, :], bank[3 + i % 2][:]).then_inc(e_evd, 1)

            def gate(p):
                a, b = TPP * p, TPP * (p + 1)
                dve.wait_ge(lg_ps, p + 1)
                dve.tensor_copy(logits[:, a:b, :], bank[4][:, 0:TPP * NE].rearrange("p (t e) -> p t e", e=NE))\
                   .then_inc(gap_done, 1)
                dve.wait_ge(gap_done, p + 1)
                for T in range(a, b):
                    last = dve.max(top8[:, T, :], logits[:, T, :])
                link(last)
                dve.tensor_tensor(gap[:, a:b], top8[:, a:b, 1], top8[:, a:b, 0], ALU.subtract).then_inc(gap_ready, 1)
                for T in range(a, b):
                    last = dve.max_index(top_i[:, T, :].bitcast(U32), top8[:, T, :], logits[:, T, :])
                link(last)
                link(dve.tensor_copy(top_f[:, a:b, :], top_i[:, a:b, :].bitcast(U32)))
                dve.wait_ge(gap_exp, p + 1)
                link(dve.tensor_scalar(w_first[:, a:b], gap[:, a:b], 1.0, None, ALU.add))
                link(dve.reciprocal(w_first[:, a:b], w_first[:, a:b]))
                link(dve.tensor_tensor(w_second[:, a:b], w_first[:, a:b], gap[:, a:b], ALU.mult))
                if p == 0:
                    dve.wait_ge(ld["iota"], 16)
                for T in range(a, b):
                    dve.tensor_scalar(pick1[:, T, :], iota8[:], top_f[:, T, 0:1], w_first[:, T:T + 1], ALU.is_equal, ALU.mult)
                    last = dve.tensor_scalar(pick2[:, T, :], iota8[:], top_f[:, T, 1:2], w_second[:, T:T + 1],
                                             ALU.is_equal, ALU.mult)
                link(last)
                link(dve.tensor_tensor(combine[:, a:b, :], pick1[:, a:b, :], pick2[:, a:b, :], ALU.add))

            def expert_gates(e, p):
                g = 2 * e + p
                for mc in range(2):
                    n = 2 * g + mc
                    dve.wait_ge(m_silu, n + 1)
                    if g >= 2:
                        dve.wait_ge(m_y, 2 * (g - 1))
                    dve.tensor_tensor(gm[:, n % 4, :], silu_m[:, n % 2, :], bank[2 + n % 2][:], ALU.mult)\
                       .then_inc(m_g, 1)

            def expert_sum(e, p):
                g = 2 * e + p
                for tt in range(TPP):
                    T, n = TPP * p + tt, TPP * g + tt
                    dve.wait_ge(m_y, 2 * g + tt // 2 + 1)
                    if e:
                        dve.wait_ge(m_acc, n - TILES + 1)
                    else:
                        dve.wait_ge(x_ready, 4 * TILES + T + 1)
                    dve.scalar_tensor_tensor(R[:, T, :], bank[4 + 2 * (g % 2) + tt // 2][:, (tt % 2) * D:(tt % 2 + 1) * D],
                                             combine[:, T, e:e + 1], (R if e else X)[:, T, :], ALU.mult, ALU.add)\
                       .then_inc(m_acc, 1)

            dve.wait_ge(ld["ident"], 16)
            dve.wait_ge(ld["sel"], 16)
            dve.tensor_copy(sel_r[:], sel[:]).then_inc(casts_ready, 1)
            dve.wait_ge(consts_ready, 1)
            gat_weights()
            stage_a(0)
            stage_a(1)
            linear_attention(0)
            weight_abs()
            dve.wait_ge(ld["x"], 16)
            norm_stats(0, 0)
            weight_scales()
            linear_attention(1)
            norm_scale(0, 0)
            norm(0, 1)
            ternary_weights()
            dve.wait_ge(ld["gb"], 16)
            stage_b()
            norm_stats(1, 1)
            x_rest(0)
            norm_scale(1, 1)
            stage_c(0)
            x_rest(1)
            norm(2, 0)
            stage_c(1)
            norm(2, 1)
            stage_d(0)
            norm(3, 0)
            stage_d(1)
            norm(3, 1)
            stage_e(0)
            norm(4, 0)
            stage_e(1)
            norm(4, 1)
            gate(0)
            expert_gates(0, 0)
            gate(1)
            units = [(e, p) for e in range(NE) for p in range(NPAIR)]
            for u in range(1, len(units)):
                expert_gates(*units[u])
                expert_sum(*units[u - 1])
                if units[u] == (NE - 1, 1):
                    dve.wait_ge(m_acc, TPP * (2 * NE - 1))
                    norm(5, 0)
            expert_sum(*units[-1])
            dve.wait_ge(m_acc, TPP * 2 * NE)
            norm(5, 1)

        @block.gpsimd
        def _(pool):
            links = [0]

            def link(ins):
                links[0] += 1
                ins.then_inc(pool_link, 1)
                pool.wait_ge(pool_link, links[0])

            def inverse_std(L, p):
                a, b = TPP * p, TPP * (p + 1)
                pool.wait_ge(stats_ready, 2 * L + p + 1)
                if L:
                    pool.wait_ge(rstd_ready, 2 * (L - 1) + p + 1)
                link(pool.tensor_scalar(veps[:, a:b], mean_var[:, a:b, 1], LN_EPS, None, ALU.add))
                pool.tensor_tensor(rstd[:, a:b], veps[:, a:b], minus_half[:], ALU.pow).then_inc(rstd_ready, 1)

            for p in range(NPAIR):
                pool.memset(vo[p][:, :, :, P:NV], 1.0)
            pool.memset(minus_half[:], -0.5)
            pool.memset(wg0[:, GF + GH:GF + 32], 0.0)
            pool.memset(wg1[:, :, GF + GH:GF + 32], 0.0)
            pool.memset(ones[:], 1.0).then_inc(consts_ready, 1)
            inverse_std(0, 0)
            inverse_std(0, 1)

            def fifth(n):
                h, j = n // 2, n % 2
                pool.wait_ge(b_tc, h + 1)
                if n >= 2:
                    pool.wait_ge(b_lr, n - 1)
                for s in range(2):
                    last = pool.tensor_scalar(a2[:, n % 2, s * S:(s + 1) * S], tneg[:, h % 2, j * S:(j + 1) * S],
                                              sneg[n // 16 % 2][:, 2 * j + s, h % GH:h % GH + 1], 0.2, ALU.add, ALU.mult)
                last.then_inc(b_a2, 1)

            fifth(0)
            for k in range(GN + 3):
                if k + 1 < GN:
                    fifth(k + 1)
                n = k - 2
                if 0 <= n < GN:
                    pool.wait_ge(b_rec, n + 1)
                    for s in range(2):
                        w = pb[:, n % 3, s * S:(s + 1) * S]
                        last = pool.tensor_scalar(w, w, sum_b[:, n % 4, s:s + 1], 1.0, ALU.mult, ALU.mult)
                    last.then_inc(b_norm, 1)
                if k == 48 + 11:
                    inverse_std(1, 0)
            inverse_std(1, 1)
            pool.wait_ge(y_ready, 2 * TILES)
            pool.memset(vp, 0.0).then_inc(d_zero, 1)
            inverse_std(2, 0)
            inverse_std(2, 1)

            def divide(p, reciprocals, divided, probs, sums, spans):
                for i in range(32):
                    n = 32 * p + i
                    pool.wait_ge(reciprocals, n + 1)
                    for s, (a, b) in enumerate(spans):
                        w = probs[:, n % 4, a:b]
                        last = pool.tensor_scalar(w, w, sums[:, n % 4, s:s + 1], 1.0, ALU.mult, ALU.mult)
                    last.then_inc(divided, 1)

            for p in range(NPAIR):
                divide(p, d_rec, d_norm, pd, sum_d, ((0, P), (P, 3 * P)))
                inverse_std(3, p)
            for p in range(NPAIR):
                divide(p, e_rec, e_norm, pe_, sum_e, ((0, S), (S, 2 * S)))
                inverse_std(4, p)
            for p in range(NPAIR):
                inverse_std(5, p)


INPUTS = ("x x_t ctx_rows ctx_t wa gat_w0 gat_w1 gat_a gat_b ffn1 ffn3 ffn2 wd_qkv wd_o m_q m_kcq m_qr m_kr "
          "m_kckv m_o gate_w moe c_ident c_block c_tri c_rope c_mrope c_sel c_iota").split()


def constants():
    ident = np.eye(P, dtype=np.float32)
    blocks = np.kron(np.eye(P // AD), np.ones((AD, AD))).astype(np.float32)
    tri = np.where(np.triu(np.ones((P, P)), 1) > 0, np.float32(-NEG), np.float32(0)).astype(np.float32)
    tri = np.concatenate([np.zeros((P, P), np.float32), tri], 1)
    inv = (1.0 / 10000.0 ** (np.arange(0, AD, 2, dtype=np.float32) / AD)).astype(np.float32)
    f = np.einsum("i,j->ij", np.arange(S, dtype=np.float32), inv)
    f = np.concatenate((f, f), axis=-1)
    sign = np.where(np.arange(AD) < AD // 2, -1.0, 1.0).astype(np.float32)
    cs = np.stack([np.cos(f), np.sin(f) * sign]).astype(np.float32).reshape(2, 2, P, AD)
    rope = np.stack([cs * np.float32(-AD ** -0.5), cs], axis=3).transpose(2, 0, 1, 3, 4)
    inv = (1.0 / 10000.0 ** (np.arange(0, CTX, 2, dtype=np.float32) / CTX)).astype(np.float32)
    f = (np.arange(S, dtype=np.float32)[:, None] * inv[None, :]).astype(np.float32)
    sign = np.where(np.arange(CTX) < CTX // 2, -1.0, 1.0).astype(np.float32)
    cs = np.stack([np.repeat(np.cos(f), 2, -1), np.repeat(np.sin(f), 2, -1) * sign]).astype(np.float32)
    mrope = cs.reshape(2, 2, P, CTX).transpose(2, 0, 1, 3)
    sel = np.zeros((TR, GH, P), np.float32)
    for h in range(GH):
        sel[h, h, :] = sel[32 + h, h, :] = 1.0
    iota = np.broadcast_to(np.arange(NE, dtype=np.float32), (P, NE))
    return dict(c_ident=ident, c_block=np.concatenate([blocks, blocks[:, ::AD]], 1), c_tri=tri, c_rope=rope,
                c_mrope=mrope, c_sel=sel, c_iota=iota)


def lay_out(i):
    def chunks(w, rows=P):
        return w.reshape(-1, rows, w.shape[-1]).transpose(1, 0, 2)

    def zeros_like_rows(n, w):
        return np.zeros((n, w.shape[-1]), w.dtype)
    x = i["x"].reshape(B * S, D)
    c = i["ctx_512"].reshape(B * S, CTX)
    a = dict(x=chunks(x), x_t=chunks(x.T), ctx_rows=chunks(c), ctx_t=c.T)
    a["wa"] = np.concatenate([chunks(i["L0_attn_Wq"].T).reshape(P, -1),
                              chunks(np.concatenate([i["L0_attn_Wk"].T, i["L0_attn_Wv"].T], 1)).reshape(P, -1),
                              chunks(i["L0_attn_Wo"].T).reshape(P, -1)], 1)
    a["gat_w0"] = i["L0_xattn_W0"].transpose(1, 0, 2).reshape(CTX, GH * GO)
    a["gat_w1"] = chunks(i["L0_xattn_W1"].transpose(1, 0, 2).reshape(D, GH * GO))
    a["gat_a"] = np.stack([i["L0_xattn_" + n].reshape(-1) for n in ("a_self0", "a_neigh0", "a_self1", "a_neigh1")])
    a["gat_b"] = np.concatenate([i["L0_xattn_b0"].reshape(2, P).T, i["L0_xattn_b1"].reshape(2, P).T], 1)
    for n in (1, 3):
        w = i[f"L0_ffn_w{n}"]
        a[f"ffn{n}"] = chunks(np.concatenate([w, zeros_like_rows(HP - HID, w)], 0).T).reshape(P, -1)
    w2 = i["L0_ffn_w2"].T
    a["ffn2"] = chunks(np.concatenate([w2, zeros_like_rows(HP - HID, w2)], 0)).reshape(P, -1)
    a["wd_qkv"] = chunks(np.concatenate([i["L1_attn_" + n].T for n in ("Wq", "Wk", "Wv")], 1)).reshape(P, -1)
    wo = i["L1_attn_Wo"].T.reshape(AH, AD, D)
    wo = np.concatenate([wo, np.zeros((AH, 32 - AD, D), wo.dtype)], 1)
    a["wd_o"] = chunks(wo.reshape(AH * 32, D)).reshape(P, -1)
    a["m_q"] = i["L1_xattn_Wq"].reshape(MH, MK, D).transpose(1, 0, 2).reshape(MK, MH * D)
    a["m_kcq"] = i["L1_xattn_w_kc_q"].transpose(2, 0, 1).reshape(2, QCH, MH, MK).transpose(1, 0, 2, 3)
    a["m_qr"] = i["L1_xattn_W_qr"].transpose(2, 0, 1)
    a["m_kr"] = i["L1_xattn_W_kr"].transpose(2, 0, 1)
    a["m_kckv"] = i["L1_xattn_w_kc_kv"].transpose(1, 0, 2)
    a["m_o"] = i["L1_xattn_Wo"].T.reshape(MH, MK, D).transpose(1, 0, 2)
    a["gate_w"] = chunks(i["L1_ffn_gate_kernel"])
    a["moe"] = np.concatenate([i["L1_ffn_" + n].reshape(NE, 2, P, D).transpose(2, 0, 1, 3).reshape(P, NE, 2 * D)
                               for n in ("wi_0", "wi_1", "wo")], 2)
    return a


def kernel(**inputs):
    import concourse.bacc as _bacc
    from concourse.bass_utils import run_bass_kernel_spmd as _run

    given = {k: np.asarray(v) for k, v in inputs.items()}
    arrays = {**lay_out(given), **constants()}
    nc = _bacc.Bacc("TRN2", target_bir_lowering=False, num_devices=1)
    feed, args = {}, []
    for name in INPUTS:
        a = np.ascontiguousarray(arrays[name])
        feed[name + "_dram"] = a
        args.append(nc.dram_tensor(name + "_dram", a.shape, mybir.dt.from_np(a.dtype), kind="ExternalInput").ap())
    out = nc.dram_tensor("out_dram", (P, TILES, D), F32, kind="ExternalOutput").ap()
    build_decoder(nc, *args, out)
    r = _run(nc, [feed], core_ids=[0])
    y = r.results[0]["out_dram"]
    return y.transpose(1, 0, 2).reshape(B, S, D)
```

```python
from contextlib import ExitStack

import numpy as np

import concourse.bass as bass
from concourse import mybir

F32 = mybir.dt.float32
F32R = mybir.dt.float32r
U32 = mybir.dt.uint32
ALU = mybir.AluOpType
ACT = mybir.ActivationFunctionType
AX = mybir.AxisListType

P = 128
B, S, D = 4, 256, 256
NPAIR = 2
TILES = B * S // P
TPP = TILES // NPAIR
PT = TPP * P
CTX = 64
GH, GO = 8, 32
HID = 682
HC = 6
HP = HC * P
AH, AD = 16, 16
MH, MK, MCQ, MR = 16, 128, 192, 64
QCH = MCQ // 2
NE = 8
TR = 32 + GH
QUERY_STEPS = {8: (0, 1), 9: (2, 3), 10: (4, 5), 14: (6, 7)}
UNITS = [(0, 0), (1, 0), (0, 1), (1, 1)] + [(e, p) for e in range(2, NE) for p in range(NPAIR)]
GN = 2 * NPAIR * GH * 2
LN_EPS = 1e-5
FOLDS = {22: (0, "g", 0, 6), 23: (0, "g", 1, 7), 30: (0, "b", 0, 4), 31: (0, "b", 1, 4), 32: (0, "b", 2, 4),
         33: (0, "b", 3, 4), 35: (0, "c", 0, 5), 36: (0, "c", 1, 5), 38: (0, "c", 2, 6), 39: (0, "c", 3, 6),
         46: (1, "g", 0, 4), 47: (1, "g", 1, 5), 48: (1, "b", 0, 4), 49: (1, "b", 1, 4), 50: (1, "b", 2, 4),
         51: (1, "b", 3, 4), 54: (1, "c", 0, 7), 55: (1, "c", 1, 7), 56: (1, "c", 2, 6), 57: (1, "c", 3, 6)}
NEG = -1e30
BIG = 3e38


def build_decoder(nc, x, x_t, ctx_rows, ctx_t, wa, gat_w0, gat_w1, gat_a, gat_b, ffn1, ffn3, ffn2,
                  wd_qkv, wd_o, m_q, m_kcq, m_qr, m_kr, m_kckv, m_o, gate_w, moe, c_ident, c_block,
                  c_tri, c_rope, c_mrope, c_sel, c_iota, out):
    ctx = ExitStack()
    with ctx:
        def sb(name, shape, dt=F32):
            return ctx.enter_context(nc.sbuf_tensor(name, shape, dt))

        def sem(name):
            return ctx.enter_context(nc.semaphore(name))

        def over(*regions):
            at = []
            for name, floats, *dt in regions[1:]:
                with nc.sbuf_tensor(name, [P, floats], *(dt or [F32])) as t:
                    at.append(t)
            return [sb(regions[0][0], [P, regions[0][1]], *(regions[0][2:] or [F32]))] + at

        def carve(region, at, *dims, rows=P):
            n = int(np.prod(dims))
            v = region[0:rows, at:at + n]
            if len(dims) == 2:
                v = v.rearrange("p (a b) -> p a b", a=dims[0])
            elif len(dims) == 3:
                v = v.rearrange("p (a b c) -> p a b c", a=dims[0], b=dims[1])
            return v

        X = sb("X", [P, TILES, D])
        XT = sb("XT", [P, 2, NPAIR * PT])
        R = sb("R", [P, TILES, D])
        stat6 = sb("stat6", [P, TILES, 6])
        mean_var = sb("mean_var", [P, TILES, 2])
        veps = sb("veps", [P, TILES])
        rstd = sb("rstd", [P, TILES])
        ident = sb("ident", [P, P])
        tri = sb("tri", [P, 2 * P])
        ones = sb("ones", [P, P])
        block_mask = sb("block_mask", [P, P + GH])
        rope = sb("rope", [P, 2, 2, 2, AD])
        mrope = sb("mrope", [P, 2, 2, CTX])
        sel_r = sb("sel_r", [TR, GH, P], F32R)
        iota8 = sb("iota8", [P, NE])
        minus_half = sb("minus_half", [P, TPP])
        WA = sb("WA", [P, 2560])
        wa_q, wa_kv, wa_o = carve(WA, 0, 2, D), carve(WA, 512, 2, 2 * D), carve(WA, 1536, 2, D)
        wd_in, wd_out = carve(WA, 0, 2, 3 * D), carve(WA, 1536, 4, D)
        GF = GH * GO + GH
        GW = GF + TR
        wg0 = sb("wg0", [CTX, GW])
        wg1 = sb("wg1", [P, 2, GW])
        gbias = sb("gbias", [P, 4])
        ternary, E1 = over(("ternary", 2 * 2 * HP + HC * D, F32R), ("E1", 8 * PT))
        w1t, w3t = carve(ternary, 0, 2, HP), carve(ternary, 2 * HP, 2, HP)
        w2t = carve(ternary, 4 * HP, HC, D)
        ctx_lat_t = carve(E1, 0, 2, 8, S)
        abs_sum = sb("abs_sum", [P, 3])
        half_scale = sb("half_scale", [P, 3])
        neg_half = sb("neg_half", [P, 3])
        full_scale = sb("full_scale", [P, 3])
        out_scale = sb("out_scale", [P, 1])
        MW = sb("MW", [P, 6144])
        mq, mkcq = carve(MW, 0, 8, D), carve(MW, 2048, 2, 8, P, rows=QCH)
        mqr, mkr = carve(MW, 4096, 8, MCQ, rows=MR), carve(MW, 5632, 8, MR, rows=MR)
        raw = [carve(MW, a, b) for a, b in ((0, 2 * HP), (2 * HP, 2 * HP), (4 * HP, HC * D))]
        mkckv, mo = carve(MW, 0, MH, CTX), carve(MW, 1024, MH, D)
        WC = sb("WC", [P, 2, MH * CTX])
        WE = sb("WE", [P, MH // 2, D])
        below = (WC.rearrange("p a b -> p (a b)"), WE.rearrange("p a b -> p (a b)"))
        sel = WE[0:TR, 0:4, :].rearrange("p a (b n) -> p (a b) n", b=2)
        gate_sb = sb("gate_sb", [P, 2, NE])
        CT = sb("CT", [CTX, NPAIR * PT])
        KVR = sb("KVR", [P, TILES, 2, CTX])
        KVT = sb("KVT", [P, NPAIR * PT])
        Q0, R1 = over(("Q0", 8 * S), ("R1", 1024, F32R))
        A0, R0, RD, RG = over(("A0", 16 * PT), ("R0", 4096, F32R), ("RD", 16 * PT, F32R), ("RG", 8 * PT, F32R))
        NV = P + GH
        kf = [carve(A0, 1024 * p, TPP, D) for p in range(NPAIR)]
        qf = [carve(A0, 2048 + 1024 * p, 2, PT) for p in range(NPAIR)]
        vo = [carve(A0, 4096 + 1088 * p, TPP, 2, NV) for p in range(NPAIR)]
        kvm = carve(A0, 6272, 2, 2, NV)
        ht = [carve(A0, 4096, 2, PT), carve(A0, 5120, 2, PT)]
        prod_tmp = carve(A0, 6912, D)
        xh, xl = ([carve(R0, 2048 * p + 1024 * i, 2, PT) for p in range(NPAIR)] for i in range(2))
        silu_c = carve(A0, 6144, 2, PT)
        qc, pe_, pte = [carve(Q0, 0, 8, S), carve(A0, 0, 8, S)], carve(A0, 4096, 4, 512), carve(A0, 6144, 2, 512)
        sum_e, nmax_e = carve(A0, 7168, 4, 2), carve(A0, 7176, 4, 2)
        A1, RA, RF = over(("A1", 12416), ("RA", 4096 + 2 * HC * PT, F32R), ("RF", 10240, F32R))
        ft = [carve(A1, 1024 * i, TPP, D) for i in range(2)]
        mask = [carve(A1, 2048 + 1024 * i, TPP, D) for i in range(2)]
        sneg = [carve(A1, 4096 + 32 * i, TPP, GH) for i in range(2)]
        tneg, a2, nl = carve(A1, 4160, 2, 512), carve(A1, 5184, 2, 512), carve(A1, 6208, 2, 512)
        eb, pb, ptb = carve(A1, 7232, 2, 512), carve(A1, 8256, 4, 512), carve(A1, 10304, 2, 512)
        g_v, g_m = carve(A1, 11328, 2, D), carve(A1, 11840, 2, D)
        nmax_b, sum_b = carve(A1, 12352, 4, 2), carve(A1, 12360, 4, 2)
        trow = [carve(R1, 512 * i, PT, rows=TR) for i in range(2)]
        abs_w = carve(MW, 4608, HC * D)
        hg_hi, hg_lo = carve(RA, 4096, HC, PT), carve(RA, 4096 + HC * PT, HC, PT)
        hg = carve(A1, 4096 + 2 * HC * PT, 2, PT)
        fmin, a_tok, at0 = carve(A1, 8256, 3, 512), carve(A1, 9792, 2, D), carve(A1, 10816, 2, PT)
        a_den = carve(A1, 11856, TPP, 2, 8)
        a_bc = carve(A1, 0, 4, D)
        vp, t1, t2 = carve(A1, 0, 6, 512), carve(A1, 3072, 512), carve(A1, 3584, 512)
        roped, rp = carve(A1, 4096, 2, 512), carve(A1, 5120, 2, 2048)
        pd, ns_d = carve(A1, 9216, 5, 384), carve(A1, 11136, 3, 384)
        qkt, atd, ptd = carve(RD, 0, 32, S), carve(E1, 0, 8, S), carve(E1, 2048, 2, 384)
        nmin_d, sum_d = sb("nmin_d", [P, 5, 2]), sb("sum_d", [P, 5, 2])
        w_hi, w_lo = ([carve(RF, 3072 * i + 1536 * u, 3, 2, D) for u in range(2)] + [carve(ternary, 1536 * i, 3, 2, D)]
                      for i in range(2))
        x_hi, x_lo = ([carve(RF, 6144 + 1024 * (2 * p + i), 2, PT) for p in range(NPAIR)] for i in range(2))
        g_hi, g_lo = carve(RG, 0, 4, PT), carve(RG, 4 * PT, 4, PT)
        gm, silu_m = carve(A0, 4096, 2, PT), carve(A0, 5120, 2, PT)
        logits, top8, top_i = (carve(A1, 10240 + 64 * i, TILES, NE) for i in range(3))
        top_f = carve(A1, 10432, TILES, 8)
        gap, w_first, w_second = (carve(A1, 10496 + 8 * i, TILES) for i in range(3))
        pick1, pick2, combine = (carve(A1, 10520 + 64 * i, TILES, NE) for i in range(3))
        fold_g, fold_b = carve(A0, 0, 2, 512, rows=QCH), carve(A0, 1024, 512)
        kv_cos, kv_sin = carve(E1, 2816, TILES, CTX), carve(E1, 3328, TILES, CTX)

        bank = [ctx.enter_context(nc.psum_tensor(f"bank{i}", [P, 512], F32)) for i in range(8)]

        names = ("xt0 xt1 x wa ident block wg0 wg1 ga gb ctxt ctxr sel tri rope mrope iota ffn1 ffn3 ffn2 "
                 "wd fold_r0 fold_b0 fold_q0 fold_r1 fold_b1 fold_q1 fold2 gate").split()
        ld = {n: sem("ld_" + n) for n in names}
        slot_ld = [sem(f"ld_slot{i}") for i in range(4)]
        stored = sem("stored")
        consts_ready, casts_ready = sem("consts"), sem("casts")
        pool_link, dve_link = sem("pool_link"), sem("dve_link")
        y_ready, r_done, stats_ready, rstd_ready = sem("y_ready"), sem("r_done"), sem("stats"), sem("rstd_s")
        x_ready, xt_ps, xt_ready, xl_ready = sem("x_ready"), sem("xt_ps"), sem("xt_ready"), sem("xl_ready")
        q_ps, kv_ps, f_min, f_exp, f_done, v_done = (sem("a_" + n) for n in "q_ps kv_ps min exp feat v".split())
        kva_ps, kvm_done, nd_ps, a_tok_done, at_ps, at_done = (sem("a_" + n) for n in "kva_ps kvm nd_ps tok at_ps at".split())
        wg_done, ft_ps, ft_done, tr_ps, tr_done, trow_done, tb_ps = (
            sem("b_" + n) for n in "wg ft_ps ft tr_ps tr trow tb".split())
        b_tc, b_a2, b_lr, b_e, b_exp, b_rec, b_norm = (sem("b_" + n) for n in "tc a2 lr e exp rec norm".split())
        b_pt, b_ev, b_av, b_m, b_em, b_h = (sem("b_" + n) for n in "pt ev av m em h".split())
        sum_ps, sums_done, abs_done, below_done, quant = (sem("c_" + n) for n in "sum_ps sums abs below quant".split())
        h1_ps, c_silu, c_g, c_hi, c_lo = (sem("c_" + n) for n in "h_ps silu g hi lo".split())
        d_zero, d_hi, d_lo, d_rec, d_norm = sem("d_zero"), sem("d_hi"), sem("d_lo"), sem("d_rec"), sem("d_norm")
        d_v_ps = sem("d_v_ps")
        d_qk_ps, d_rope, d_v, rp_ps, d_qkt = (sem("d_" + n) for n in "qk_ps rope v rp_ps qkt".split())
        d_t1, d_s, d_max, d_exp, d_pt, d_evd, d_eva, d_av, d_fin = (
            sem("d_" + n) for n in "t1 s max exp pt evd eva av fin".split())
        fo_g, fo_gs, fo_b, fo_bs, fo_c, fo_cs, fo_e, fo_es = (
            sem("fo_" + n) for n in "g gs b bs c cs e es".split())
        kvr_done, kvt_ps, kvt_done, qc_ps, qc_done = (sem("e_" + n) for n in "kvr kvt_ps kvt qc_ps qc".split())
        e_s, e_max, e_exp, e_rec, e_norm, e_pt, e_evd, e_eva, e_av, e_ctx = (
            sem("e_" + n) for n in "s max exp rec norm pt evd eva av ctx".split())
        lg_ps, gap_done, gap_ready, gap_exp = (sem("f_" + n) for n in "lg_ps lg gap gap_exp".split())
        m_h, m_silu, m_g, m_y, m_acc = (sem("m_" + n) for n in "h silu g y acc".split())
        m_w_hi, m_w_lo, m_x_hi, m_x_lo, m_g_hi, m_g_lo = (sem("m_" + n) for n in "w_hi w_lo x_hi x_lo g_hi g_lo".split())

        block = ctx.enter_context(nc.Block())

        def wait_moved(eng, by_dve, by_act, n):
            eng.wait_ge(by_act if n % 2 else by_dve, n // 2 + 1)

        def moved(by_dve, by_act, n):
            return (by_act if n % 2 else by_dve), n // 2 + 1

        @block.sync
        def _(sp):
            def load(dst, src, what):
                sp.dma_start(dst, src).then_inc(ld[what], 16)

            load(XT[:, :, 0:PT], x_t[:, :, 0:PT], "xt0")
            load(WA[:, 0:2048], wa, "wa")
            load(XT[:, :, PT:2 * PT], x_t[:, :, PT:2 * PT], "xt1")
            load(block_mask[:], c_block, "block")
            load(ident[:], c_ident, "ident")
            load(X[:], x, "x")
            for src, dst, what in zip((ffn1, ffn3, ffn2), raw, ("ffn1", "ffn3", "ffn2")):
                load(dst, src, what)
            load(wg0[:, 0:GH * GO], gat_w0, "wg0")
            load(CT[:], ctx_t, "ctxt")
            load(a_bc, gat_a.partition_broadcast(P), "ga")
            load(wg1[:, :, 0:GH * GO], gat_w1, "wg1")
            load(sel[:], c_sel, "sel")
            load(gbias[:], gat_b, "gb")
            load(tri[:], c_tri, "tri")
            load(rope[:], c_rope, "rope")
            load(mrope[:], c_mrope, "mrope")
            load(KVR[:, :, 0, :], ctx_rows, "ctxr")
            load(iota8[:], c_iota, "iota")
            load(gate_sb[:], gate_w, "gate")
            sp.wait_ge(quant, 3)
            load(mqr, m_qr[:, 0:8, :], "fold_r0")
            load(mkr, m_kr[:, 0:8, :], "fold_r0")
            load(mkcq, m_kcq[:, :, 0:8, :], "fold_b0")
            load(MW[:, 0:2048], m_q[:, 0:2048], "fold_q0")
            sp.wait_ge(y_ready, TILES)
            sp.dma_start(WA[:, 0:1536], wd_qkv).then_inc(ld["wd"], 16)
            sp.dma_start(WA[:, 1536:2560], wd_o).then_inc(ld["wd"], 16)
            sp.wait_ge(fo_g, 2)
            load(mqr, m_qr[:, 8:16, :], "fold_r1")
            load(mkr, m_kr[:, 8:16, :], "fold_r1")
            sp.wait_ge(fo_b, 1)
            load(mkcq, m_kcq[:, :, 8:16, :], "fold_b1")
            sp.wait_ge(fo_c, 2)
            load(MW[:, 0:2048], m_q[:, 2048:4096], "fold_q1")
            sp.wait_ge(fo_c, 4)
            load(mkckv, m_kckv, "fold2")
            load(mo, m_o, "fold2")
            sp.wait_ge(fo_e, 4)
            for e in range(NE):
                if e >= 4:
                    sp.wait_ge(m_w_lo, e - 3)
                sp.dma_start(MW[:, (e % 4) * 1536:(e % 4 + 1) * 1536], moe[:, e, :]).then_inc(slot_ld[e % 4], 16)
            for p in range(NPAIR):
                sp.wait_ge(x_ready, 5 * TILES + TPP * (p + 1))
                sp.dma_start(out[:, TPP * p:TPP * (p + 1), :], X[:, TPP * p:TPP * (p + 1), :]).then_inc(stored, 16)
            sp.wait_ge(stored, 16 * NPAIR)

        @block.tensor
        def _(pe):
            freed = [()] * 8

            def claim(b, *freed_by):
                for s_, v_ in freed[b]:
                    pe.wait_ge(s_, v_)
                freed[b] = freed_by
                return bank[b]

            def transpose(dst, src):
                return pe.transpose(dst, src, ident[:])

            def norm_transposes(L, p, chunks=(0, 1), banks=(6, 7)):
                pe.wait_ge(x_ready, L * TILES + TPP * (p + 1))
                for c in chunks:
                    n = (2 * (L - 1) + p) * 2 + c
                    ps = claim(banks[c], (xl_ready, n + 1) if L == 1 else (xt_ready, n + 1))
                    for tt in range(TPP):
                        last = transpose(ps[:, tt * P:(tt + 1) * P], X[:, TPP * p + tt, c * P:(c + 1) * P])
                    last.then_inc(xt_ps, 1)

            def project_out(L, p, banks, lhs, rhs, chunks):
                for tt in range(TPP):
                    n = L * TILES + TPP * p + tt
                    if tt % 2 == 0:
                        ps = claim(banks[tt // 2], (r_done, n + 2))
                    for k in range(chunks):
                        last = pe.matmul(ps[:, (tt % 2) * D:(tt % 2 + 1) * D], lhs(k, tt), rhs(k),
                                         start=(k == 0), stop=(k == chunks - 1))
                    last.then_inc(y_ready, 1)

            def project_piece(L, b, piece, lhs, rhs, chunks):
                s, half = piece // 2, piece % 2
                n = L * TILES + 2 * b + s
                if piece == 0:
                    claim(6, (r_done, n + 2))
                for k in range(half * chunks // 2, (half + 1) * chunks // 2):
                    last = pe.matmul(bank[6][:, s * D:(s + 1) * D], lhs(k, s), rhs(k),
                                     start=(k == 0), stop=(k == chunks - 1))
                if half:
                    last.then_inc(y_ready, 1)

            def project_in(p):
                pe.wait_ge(ld[f"xt{p}"], 16)
                if p == 0:
                    pe.wait_ge(ld["wa"], 16)
                for oc in range(2):
                    ps = claim(oc, (f_done, 6 * p + oc + 1))
                    for c in range(2):
                        last = pe.matmul(ps[:], wa_q[:, c, oc * P:(oc + 1) * P], XT[:, c, p * PT:(p + 1) * PT],
                                         start=(c == 0), stop=(c == 1))
                    last.then_inc(q_ps, 1)
                for tt in range(TPP):
                    ps = claim(2 + tt, (f_done, 6 * p + tt + 3), (v_done, TPP * p + tt + 1))
                    for c in range(2):
                        last = pe.matmul(ps[:], XT[:, c, (TPP * p + tt) * P:(TPP * p + tt + 1) * P], wa_kv[:, c, :],
                                         start=(c == 0), stop=(c == 1))
                    last.then_inc(kv_ps, 1)

            def linear_attention(p):
                for j in range(2):
                    ps = claim(6 + j, (kvm_done, 2 * p + j + 1))
                    pe.wait_ge(f_done, 6 * p + 2 * j + 4)
                    pe.wait_ge(v_done, TPP * p + 2 * j + 2)
                    for c in range(2):
                        for s in range(2):
                            tt = 2 * j + s
                            last = pe.matmul(ps[:, c * NV:(c + 1) * NV], kf[p][:, tt, c * P:(c + 1) * P],
                                             vo[p][:, tt, c, :], start=(s == 0), stop=(s == 1))
                    last.then_inc(kva_ps, 1)
                for tt in range(TPP):
                    ps = claim(tt, (a_tok_done, TPP * p + tt + 1))
                    if tt % 2 == 0:
                        pe.wait_ge(kvm_done, 2 * p + tt // 2 + 1)
                    for c in range(2):
                        last = pe.matmul(ps[:, c * NV:(c + 1) * NV], qf[p][:, c, tt * P:(tt + 1) * P],
                                         kvm[:, tt // 2, c, :], start=True, stop=True)
                    last.then_inc(nd_ps, 1)

            def linear_out(p):
                ps = [claim(4 + c, (at_done, 2 * p + c + 1)) for c in range(2)]
                for tt in range(TPP):
                    pe.wait_ge(a_tok_done, TPP * p + tt + 1)
                    for c in range(2):
                        last = transpose(ps[c][:, tt * P:(tt + 1) * P], a_tok[:, tt % 2, c * P:(c + 1) * P])
                    last.then_inc(at_ps, 1)
                pe.wait_ge(at_done, 2 * p + 2)
                project_out(0, p, (6, 7), lambda k, tt: at0[:, k, tt * P:(tt + 1) * P], lambda k: wa_o[:, k, :], 2)

            def node_features(lp, step):
                l, p = lp // 2, lp % 2
                if step:
                    pass
                elif l == 0:
                    pe.wait_ge(ld["ctxt"], 16)
                    pe.wait_ge(wg_done, 1)
                else:
                    pe.wait_ge(b_h, 4 * p + 4)
                    pe.wait_ge(wg_done, 2)
                nch = 1 if l == 0 else 2

                def weights(c, a, b):
                    return wg0[:, a:b] if l == 0 else wg1[:, c, a:b]

                def nodes(c, a, b):
                    return CT[:, p * PT + a:p * PT + b] if l == 0 else ht[p][:, c, a:b]

                if step < TPP:
                    ps = claim(6 + step % 2, (ft_done, TPP * lp + step + 1))
                    for c in range(nch):
                        last = pe.matmul(ps[:, 0:GF], nodes(c, step * P, (step + 1) * P), weights(c, 0, GF),
                                         start=(c == 0), stop=(c == nch - 1))
                    last.then_inc(ft_ps, 1)
                    return
                ps = claim(6, (trow_done, lp + 1))
                for c in range(nch):
                    last = pe.matmul(ps[0:TR, :], weights(c, GF, GW), nodes(c, 0, PT),
                                     start=(c == 0), stop=(c == nch - 1))
                last.then_inc(tr_ps, 1)

            def neighbour_rows(hh):
                lp, h = hh // GH, hh % GH
                if h == 0:
                    pe.wait_ge(trow_done, lp + 1)
                ps = claim(h % 2, (b_tc, hh + 1))
                pe.matmul(ps[:], sel_r[:, h, :], trow[lp % 2], start=True, stop=True).then_inc(tb_ps, 1)

            def gat_turn(n):
                pe.wait_ge(b_norm, n + 1)
                ps = claim(2 + n % 2, (b_ev, n + 1))
                for mt in range(2):
                    for s in range(2):
                        last = transpose(ps[:, mt * S + s * P:mt * S + (s + 1) * P],
                                         pb[:, n % 4, s * S + mt * P:s * S + (mt + 1) * P])
                last.then_inc(b_pt, 1)

            def gat_mix(n):
                lp, i = n // 16, n % 16
                h, j = i // 2, i % 2
                b_ = 4 + 2 * (h // 4) + j
                if h % 4 == 0:
                    claim(b_, (b_m, 4 * lp + 2 * (h // 4) + j + 1))
                pe.wait_ge(b_ev, n + 1)
                q = 32 * (h % 4)
                for mt in range(2):
                    last = pe.matmul(bank[b_][q:q + GO, 0:S], ft[lp % 2][:, 2 * j + mt, h * GO:(h + 1) * GO],
                                     ptb[:, n % 2, mt * S:(mt + 1) * S], start=(mt == 0), stop=(mt == 1))
                last.then_inc(b_av, 1)

            def gat_out(p):
                pe.wait_ge(b_h, 8 + 4 * p + 4)
                for tt in range(TPP):
                    n = TILES + TPP * p + tt
                    if tt % 2 == 0:
                        ps = claim(6 + tt // 2, (r_done, n + 2))
                    for c in range(2):
                        last = transpose(ps[:, (tt % 2) * D + c * P:(tt % 2) * D + (c + 1) * P],
                                         ht[p][:, c, tt * P:(tt + 1) * P])
                    last.then_inc(y_ready, 1)

            def stage_b():
                neighbour_rows(1)
                for k in range(GN + 6):
                    if k % 2 and k // 2 + 2 < GN // 2:
                        neighbour_rows(k // 2 + 2)
                    if 3 <= k < GN + 3:
                        gat_turn(k - 3)
                    if 5 <= k < GN + 5:
                        gat_mix(k - 5)
                    if 8 <= k % 16 < 13 and k // 16 < 3:
                        node_features(k // 16 + 1, k % 16 - 8)
                    if k in FOLDS:
                        fold_queries(*FOLDS[k])
                    if k == 48 + 10:
                        gat_out(0)
                    if k == GN + 1:
                        norm_transposes(1, 0, banks=(4, 5))
                swiglu_in(0, range(2))
                gat_out(1)

            def weight_sums():
                pe.wait_ge(abs_done, 3)
                ps = claim(5, (sums_done, 1))
                pe.matmul(ps[:, 0:3], ones[:], abs_sum[:], start=True, stop=True).then_inc(sum_ps, 1)

            def swiglu_in(p, chunks):
                pe.wait_ge(quant, 3)
                pe.wait_ge(xl_ready, 2 * (p + 1))
                for k in chunks:
                    n = HC * p + k
                    for part, w in enumerate((w1t, w3t)):
                        ps = claim(2 * part + n % 2, (c_g, n + 1))
                        for i, (c, x_) in enumerate((c, x_) for c in range(2) for x_ in (xl[p], xh[p])):
                            last = pe.matmul(ps[:], w[:, c, k * P:(k + 1) * P], x_[:, c, :], start=(i == 0), stop=(i == 3))
                    last.then_inc(h1_ps, 1)

            def stage_c(p):
                swiglu_in(p, range(0 if p else 2, HC))
                norm_transposes(1 + p, 1 - p)
                for tt in range(TPP):
                    n = 2 * TILES + TPP * p + tt
                    if tt % 2 == 0:
                        ps = claim(4 + tt // 2, (r_done, n + 2))
                    for i, (k, g_) in enumerate((k, g_) for k in range(HC) for g_ in (hg_lo, hg_hi)):
                        if tt == 0:
                            pe.wait_ge(c_lo, HC * p + k + 1)
                        last = pe.matmul(ps[:, (tt % 2) * D:(tt % 2 + 1) * D], g_[:, k, tt * P:(tt + 1) * P],
                                         w2t[:, k, :], start=(i == 0), stop=(i == 2 * HC - 1))
                    last.then_inc(y_ready, 1)

            def fold_queries(w, product, i, b_):
                if product == "g":
                    if i == 0:
                        pe.wait_ge(ld[f"fold_r{w}"], 32)
                    ps = claim(b_, (fo_gs, 2 * w + i + 1))
                    for h in range(4 * i, 4 * i + 4):
                        for q in range(2):
                            at = (h % 4) * P + q * MR
                            last = pe.matmul(ps[0:QCH, at:at + MR], mqr[:, h, q * QCH:(q + 1) * QCH],
                                             mkr[:, h, :], start=True, stop=True)
                    last.then_inc(fo_g, 1)
                elif product == "b":
                    ps = bank[b_]
                    if i == 0:
                        pe.wait_ge(fo_gs, 2 * w + 2)
                        pe.wait_ge(ld[f"fold_b{w}"], 16)
                        claim(b_, (fo_bs, w + 1))
                    for h in (2 * i, 2 * i + 1):
                        for q in range(2):
                            last = pe.matmul(ps[:, h * MR:(h + 1) * MR], mkcq[:, q, h, :],
                                             fold_g[:, h // 4, (h % 4) * P + q * MR:(h % 4) * P + (q + 1) * MR],
                                             start=(q == 0), stop=(q == 1))
                    if i == 3:
                        last.then_inc(fo_b, 1)
                else:
                    c, ps = i // 2, bank[b_]
                    if i % 2 == 0:
                        pe.wait_ge(fo_bs, w + 1)
                        pe.wait_ge(ld[f"fold_q{w}"], 16)
                        claim(b_, (fo_cs, 2 * w + c + 1))
                    for h in range(4 * (i % 2), 4 * (i % 2) + 4):
                        last = pe.matmul(ps[:, h * MR:(h + 1) * MR], mq[:, h, c * P:(c + 1) * P],
                                         fold_b[:, h * MR:(h + 1) * MR], start=True, stop=True)
                    if i % 2:
                        last.then_inc(fo_c, 1)

            def fold_outputs():
                pe.wait_ge(ld["fold2"], 32)
                for q in range(4):
                    ps = claim(4 + q % 2, (fo_es, q + 1))
                    for h in range(4 * q, 4 * q + 4):
                        last = pe.matmul(ps[64 * (h % 2):64 * (h % 2) + 64, (h // 2 % 2) * D:(h // 2 % 2 + 1) * D],
                                         mkckv[:, h, :], mo[:, h, :], start=True, stop=True)
                    last.then_inc(fo_e, 1)

            def queries_keys(T, b_):
                if T % TPP == 0:
                    pe.wait_ge(xt_ready, 4 + 2 * (T // TPP + 1))
                ps = claim(b_, (d_t1, T + 1))
                for c in range(2):
                    last = pe.matmul(ps[:], XT[:, c, T * P:(T + 1) * P], wd_in[:, c, 0:512], start=(c == 0), stop=(c == 1))
                last.then_inc(d_qk_ps, 1)

            def values(T, b_):
                ps = claim(b_, (d_v, T + 1))
                for c in range(2):
                    last = pe.matmul(ps[:, 0:D], XT[:, c, T * P:(T + 1) * P], wd_in[:, c, 512:768],
                                     start=(c == 0), stop=(c == 1))
                last.then_inc(d_v_ps, 1)

            def turn_heads(T, i):
                if i == 0:
                    pe.wait_ge(d_hi, T + 1)
                    pe.wait_ge(d_lo, T + 1)
                ps = claim(6 + i % 2, (d_qkt, 4 * T + i + 1))
                at = 8 * (i % 2) + 4 * (i // 2)
                for c in range(4):
                    last = transpose(ps[:, c * P:(c + 1) * P], rp[:, T % 2, (at + c) * P:(at + c + 1) * P])
                last.then_inc(rp_ps, 1)

            def stage_d():
                pe.wait_ge(ld["wd"], 32)
                for T in range(2):
                    queries_keys(T, T)
                    values(T, 2 + T)
                fold_outputs()
                for T in range(2):
                    for i in range(4):
                        turn_heads(T, i)

                def scores(n):
                    b, h = n // AH, n % AH
                    if h == 0:
                        pe.wait_ge(d_v, 2 * b + 2)
                    if h % 8 == 0:
                        pe.wait_ge(d_qkt, 4 * (2 * b + 1) + 2 + h // 4)
                    ps = claim(n % 2, (d_max, n + 1))
                    q, c = 64 * (h % 2), 16 * (b % 2) + h // 2
                    for s in range(2):
                        last = pe.matmul(ps[:, s * S:(s + 1) * S], qkt[q:q + 64, c, s * P:(s + 1) * P],
                                         qkt[q:q + 64, 8 + c, :], start=True, stop=True)
                    last.then_inc(d_s, 1)

                def turn(n):
                    pe.wait_ge(d_norm, n + 1)
                    ps = claim(2 + n % 2, moved(d_evd, d_eva, n))
                    for at in (0, P, 2 * P):
                        last = transpose(ps[:, at:at + P], pd[:, n % 5, at:at + P])
                    last.then_inc(d_pt, 1)

                def mix(n):
                    b, h, g = n // AH, n % AH, n // 4
                    b_ = 4 + g % 2
                    if h % 4 == 0:
                        claim(b_, (d_fin, g + 1))
                    wait_moved(pe, d_evd, d_eva, n)
                    q = 32 * (h % 4)
                    for kt in range(2):
                        last = pe.matmul(bank[b_][q:q + 32, kt * P:S], vp[:, (2 * b + kt) % 6, h * 32:(h + 1) * 32],
                                         ptd[:, n % 2, kt * S:kt * P + S], start=(kt == 0), stop=(kt == 1),
                                         skip_group_check=True)
                    last.then_inc(d_av, 1)

                def out_pieces(b, pieces):
                    pe.wait_ge(d_fin, 4 * (b + 1))
                    for piece in pieces:
                        project_piece(3, b, piece, lambda k, s: atd[:, 4 * (b % 2) + k, s * P:(s + 1) * P],
                                      lambda k: wd_out[:, k, :], 4)

                scores(0)
                for k in range(AH * B + 6):
                    b, i = k // AH, k % AH
                    if k + 1 < AH * B:
                        scores(k + 1)
                    if 4 <= k < AH * B + 4:
                        turn(k - 4)
                    if k >= 6:
                        mix(k - 6)
                    T = 2 * b + 2
                    if i == 0 and 1 <= b < B:
                        turn_heads(T - 1, 2)
                        turn_heads(T - 1, 3)
                    if T < TILES:
                        if i == 2:
                            queries_keys(T, 6)
                            values(T, 7)
                        if i in (6, 8):
                            turn_heads(T, i - 6)
                            turn_heads(T, i - 5)
                        if i == 10:
                            queries_keys(T + 1, 7)
                        if i == 12:
                            values(T + 1, 7)
                        if i == 14:
                            turn_heads(T + 1, 0)
                            turn_heads(T + 1, 1)
                    if i in (11, 12) and 1 <= b < B:
                        out_pieces(b - 1, (0, 1) if i == 11 else (2, 3))
                    if k == 4:
                        norm_transposes(2, 1)
                    if k == 3 * AH + 4:
                        norm_transposes(3, 0)
                    if k == 3 * AH + 6:
                        turn_context()
                    for m in QUERY_STEPS.get(k - 3 * AH, ()):
                        latent_queries(0, m, 6 + m % 2)
                out_pieces(B - 1, range(4))

            def turn_context():
                pe.wait_ge(kvr_done, 1)
                for p in range(NPAIR):
                    ps = claim(6 + p, (kvt_done, p + 1))
                    for tt in range(TPP):
                        last = transpose(ps[:, tt * P:(tt + 1) * P],
                                         KVR[:, TPP * p + tt, :, :].rearrange("p a b -> p (a b)"))
                    last.then_inc(kvt_ps, 1)

            def latent_queries(b, m, b_):
                if m == 0:
                    pe.wait_ge(xt_ready, 8 + 2 * (b // 2 + 1))
                ps = claim(b_, (qc_done, 8 * b + m + 1))
                for c in range(2):
                    last = pe.matmul(ps[:, 0:S], WC[:, c, m * P:(m + 1) * P], XT[:, c, b * S:(b + 1) * S],
                                     start=(c == 0), stop=(c == 1))
                last.then_inc(qc_ps, 1)

            def stage_e():
                pe.wait_ge(fo_cs, 4)
                pe.wait_ge(fo_es, 4)
                pe.wait_ge(kvt_done, 2)

                def scores(n):
                    b, h = n // MH, n % MH
                    pe.wait_ge(qc_done, 8 * b + h // 2 + 1)
                    ps = claim(n % 2, (e_exp, n + 1))
                    q = 64 * (h % 2)
                    for s in range(2):
                        last = pe.matmul(ps[:, s * S:(s + 1) * S], qc[b % 2][q:q + 64, h // 2, s * P:(s + 1) * P],
                                         KVT[q:q + 64, b * S:(b + 1) * S], start=True, stop=True)
                    last.then_inc(e_s, 1)

                def turn(n):
                    pe.wait_ge(e_norm, n + 1)
                    ps = claim(2 + n % 2, moved(e_evd, e_eva, n))
                    for lt in range(2):
                        for s in range(2):
                            last = transpose(ps[:, lt * S + s * P:lt * S + (s + 1) * P],
                                             pe_[:, n % 4, s * S + lt * P:s * S + (lt + 1) * P])
                    last.then_inc(e_pt, 1)

                def mix(n):
                    b, h, g = n // MH, n % MH, n // 4
                    b_ = 4 + g % 2
                    if h % 4 == 0:
                        claim(b_, (e_ctx, g + 1))
                    wait_moved(pe, e_evd, e_eva, n)
                    q = 64 * (h % 2)
                    for lt in range(2):
                        last = pe.matmul(bank[b_][q:q + 64, (h // 2 % 2) * S:(h // 2 % 2 + 1) * S],
                                         KVR[:, 2 * b + lt, 0, :], pte[:, n % 2, lt * S:(lt + 1) * S],
                                         start=(lt == 0), stop=(lt == 1))
                    last.then_inc(e_av, 1)

                def out_piece(b, piece):
                    if piece == 0:
                        pe.wait_ge(e_ctx, 4 * (b + 1))
                    project_piece(4, b, piece, lambda k, s: ctx_lat_t[:, b % 2, k, s * P:(s + 1) * P],
                                  lambda k: WE[:, k, :], 8)

                scores(0)
                for k in range(MH * B + 5):
                    b, i = k // MH, k % MH
                    if k + 1 < MH * B:
                        scores(k + 1)
                    if 3 <= k < MH * B + 3:
                        turn(k - 3)
                    if k >= 5:
                        mix(k - 5)
                    if i % 2 and b + 1 < B:
                        latent_queries(b + 1, i // 2, 7)
                    if i in (8, 10, 12, 14) and 1 <= b < B:
                        out_piece(b - 1, (i - 8) // 2)
                    if k in (4, 6):
                        norm_transposes(3, 1, (k // 2 - 2,), (6, 6))
                    if k == 3 * MH + 6:
                        norm_transposes(4, 0)
                gate(0)
                for piece in range(4):
                    out_piece(B - 1, piece)

            def gate(p):
                pe.wait_ge(xt_ready, 12 + 2 * (p + 1))
                pe.wait_ge(ld["gate"], 16)
                ps = claim(4, (gap_done, p + 1))
                for tt in range(TPP):
                    t = (TPP * p + tt) * P
                    for c in range(2):
                        last = pe.matmul(ps[:, tt * NE:(tt + 1) * NE], XT[:, c, t:t + P], gate_sb[:, c, :],
                                         start=(c == 0), stop=(c == 1))
                last.then_inc(lg_ps, 1)

            def expert_in(u):
                e, p = UNITS[u]
                pe.wait_ge(m_w_lo, e + 1)
                pe.wait_ge(m_x_lo, 2 * (p + 1))
                for mc in range(2):
                    n = 2 * u + mc
                    for part in range(2):
                        ps = claim(2 * part + n % 2, (m_g, n + 1))
                        products = [(w_, x_, c) for c in range(2) for w_, x_ in
                                    ((w_lo[e % 3], x_hi[p]), (w_hi[e % 3], x_lo[p]), (w_hi[e % 3], x_hi[p]))]
                        for i, (w_, x_, c) in enumerate(products):
                            last = pe.matmul(ps[:], w_[:, part, c, mc * P:(mc + 1) * P], x_[:, c, :],
                                             start=(i == 0), stop=(i == 5))
                    last.then_inc(m_h, 1)

            def expert_out(u):
                e = UNITS[u][0]
                pe.wait_ge(m_g_lo, 2 * u + 2)
                for tp in range(2):
                    ps = claim(4 + 2 * (u % 2) + tp, (m_acc, TPP * u + 2 * tp + 2))
                    for tt in range(2 * tp, 2 * tp + 2):
                        products = [(g_, w_, mc) for mc in range(2) for g_, w_ in
                                    ((g_lo, w_hi[e % 3]), (g_hi, w_lo[e % 3]), (g_hi, w_hi[e % 3]))]
                        for i, (g_, w_, mc) in enumerate(products):
                            last = pe.matmul(ps[:, (tt % 2) * D:(tt % 2 + 1) * D],
                                             g_[:, (2 * u + mc) % 4, tt * P:(tt + 1) * P], w_[:, 2, mc, :],
                                             start=(i == 0), stop=(i == 5))
                    last.then_inc(m_y, 1)

            pe.wait_ge(consts_ready, 1)
            project_in(0)
            project_in(1)
            linear_attention(0)
            pe.wait_ge(ld["ident"], 16)
            linear_out(0)
            weight_sums()
            for step in range(TPP + 1):
                node_features(0, step)
            pe.wait_ge(casts_ready, 1)
            neighbour_rows(0)
            linear_attention(1)
            linear_out(1)
            stage_b()
            stage_c(0)
            stage_c(1)
            stage_d()
            stage_e()
            expert_in(0)
            norm_transposes(4, 1)
            expert_in(1)
            expert_out(0)
            for u in range(2, len(UNITS)):
                expert_in(u)
                if u == 2:
                    gate(1)
                expert_out(u - 1)
            expert_out(len(UNITS) - 1)

        @block.scalar
        def _(act):
            def copy(dst, src, scale=1.0):
                return act.activation(dst, src, ACT.Copy, scale=scale)

            def norm_moves(L, p, chunks=(0, 1), banks=(6, 7)):
                for c in chunks:
                    n = (2 * (L - 1) + p) * 2 + c
                    act.wait_ge(xt_ps, n + 1)
                    if L == 1:
                        copy(xh[p][:, c, :], bank[banks[c]][:]).then_inc(xt_ready, 1)
                        continue
                    if L == 4:
                        copy(x_hi[p][:, c, :], bank[6 + c][:]).then_inc(m_x_hi, 1)
                    copy(XT[:, c, p * PT:(p + 1) * PT], bank[banks[c]][:]).then_inc(xt_ready, 1)

            def stage_a(p):
                for i in range(6):
                    n = 6 * p + i
                    if i < TPP:
                        act.wait_ge(kv_ps, TPP * p + i + 1)
                        copy(vo[p][:, i, :, 0:P], bank[2 + i][:, D:2 * D].rearrange("p (c n) -> p c n", c=2))\
                            .then_inc(v_done, 1)
                    act.wait_ge(f_min, n + 1)
                    w = 512 if i < 2 else D
                    act.activation(fmin[:, n % 3, 0:w], fmin[:, n % 3, 0:w], ACT.Exp).then_inc(f_exp, 1)

            def weight_abs():
                for i, (w, what) in enumerate(zip(raw, ("ffn1", "ffn3", "ffn2"))):
                    act.wait_ge(ld[what], 16)
                    if i:
                        act.wait_ge(abs_done, i)
                    act.activation(abs_w[:, 0:w.shape[1]], w, ACT.Abs, accum_out=abs_sum[:, i:i + 1]).then_inc(abs_done, 1)

            def linear_out(p):
                act.wait_ge(at_ps, TPP * (p + 1))
                for c in range(2):
                    copy(at0[:, c, :], bank[4 + c][:]).then_inc(at_done, 1)

            def node_features(lp, step):
                u = lp % 2
                if lp >= 2 and step == 0:
                    act.wait_ge(b_e, 16 * (lp - 1))
                    act.wait_ge(b_a2, 16 * (lp - 1))
                if step < TPP:
                    act.wait_ge(ft_ps, TPP * lp + step + 1)
                    copy(ft[u][:, step, :], bank[6 + step % 2][:, 0:GH * GO])
                    copy(sneg[u][:, step, :], bank[6 + step % 2][:, GH * GO:GH * GO + GH], -1.0).then_inc(ft_done, 1)
                else:
                    act.wait_ge(tr_ps, lp + 1)
                    copy(trow[u], bank[6][0:TR, :], -1.0).then_inc(tr_done, 1)

            def neighbour_rows(hh):
                act.wait_ge(tb_ps, hh + 1)
                if hh >= 2:
                    act.wait_ge(b_a2, 2 * hh - 2)
                    act.wait_ge(b_lr, 2 * hh - 2)
                copy(tneg[:, hh % 2, :], bank[hh % 2][:]).then_inc(b_tc, 1)

            def stage_b():
                for k in range(GN + 8):
                    if k % 2 == 0 and k // 2 + 1 < GN // 2:
                        neighbour_rows(k // 2 + 1)
                    if 1 <= k <= GN:
                        n = k - 1
                        act.wait_ge(b_e, n + 1)
                        if n >= 4:
                            act.wait_ge(b_pt, n - 3)
                        for s in range(2):
                            last = act.activation(pb[:, n % 4, s * S:(s + 1) * S], eb[:, n % 2, s * S:(s + 1) * S],
                                                  ACT.Exp, bias=nmax_b[:, n % 4, s:s + 1], scale=-1.0,
                                                  accum_out=sum_b[:, n % 4, s:s + 1])
                        last.then_inc(b_exp, 1)
                    n = k - 4
                    if 0 <= n < GN:
                        act.wait_ge(b_pt, n + 1)
                        if n >= 2:
                            act.wait_ge(b_av, n - 1)
                        copy(ptb[:, n % 2, :], bank[2 + n % 2][:]).then_inc(b_ev, 1)
                    n = k - 7
                    if 0 <= n < GN and n // 2 % 4 == 3:
                        f = n // 8 * 2 + n % 2
                        act.wait_ge(b_m, f + 1)
                        act.activation(g_m[:, f % 2, :], g_m[:, f % 2, :], ACT.Exp).then_inc(b_em, 1)
                    if k - 1 in FOLDS:
                        fold_queries(*FOLDS[k - 1])
                    if k == GN + 2:
                        norm_moves(1, 0, banks=(4, 5))
                    if 8 <= k % 16 < 13 and k // 16 < 3:
                        node_features(k // 16 + 1, k % 16 - 8)

            def fold_queries(w, product, i, b_):
                if product == "g":
                    act.wait_ge(fo_g, 2 * w + i + 1)
                    copy(fold_g[:, i, :], bank[b_][0:QCH, :]).then_inc(fo_gs, 1)
                elif product == "b" and i == 3:
                    act.wait_ge(fo_b, w + 1)
                    copy(fold_b, bank[b_][:]).then_inc(fo_bs, 1)
                elif product == "c" and i % 2:
                    c = i // 2
                    act.wait_ge(fo_c, 2 * w + c + 1)
                    copy(WC[:, c, w * 512:(w + 1) * 512], bank[b_][:]).then_inc(fo_cs, 1)

            def fold_outputs(quarters):
                for q in quarters:
                    act.wait_ge(fo_e, q + 1)
                    copy(WE[:, 2 * q:2 * q + 2, :], bank[4 + q % 2][:].rearrange("p (a n) -> p a n", a=2)).then_inc(fo_es, 1)

            def stage_c(p):
                if p:
                    act.wait_ge(y_ready, 2 * TILES + TPP)
                for k in range(HC + 1):
                    n = HC * p + k
                    if k < HC:
                        act.wait_ge(h1_ps, n + 1)
                        if n >= 2:
                            act.wait_ge(c_g, n - 1)
                        act.activation(silu_c[:, n % 2, :], bank[n % 2][:], ACT.Silu, scale=full_scale[:, 0:1])\
                           .then_inc(c_silu, 1)
                    if k:
                        act.wait_ge(c_g, n)
                        copy(hg_hi[:, k - 1, :], hg[:, (n - 1) % 2, :]).then_inc(c_hi, 1)

            def turn_context():
                for p in range(NPAIR):
                    act.wait_ge(kvt_ps, p + 1)
                    copy(KVT[:, p * PT:(p + 1) * PT], bank[6 + p][:]).then_inc(kvt_done, 1)

            def values(T, b_):
                act.wait_ge(d_v_ps, T + 1)
                copy(vp[:, T % 6, :].rearrange("p (h i) -> p h i", h=AH)[:, :, 0:AD],
                     bank[b_][:, 0:D].rearrange("p (h i) -> p h i", h=AH)).then_inc(d_v, 1)

            def rounded(T):
                act.wait_ge(d_rope, T + 1)
                if T >= 2:
                    act.wait_ge(rp_ps, 4 * (T - 1))
                slots = rp[:, T % 2, :].bitcast(F32R).rearrange("p (a h d i) -> p a h d i", a=2, h=AH, d=4)
                v = roped[:, T % 2, :].rearrange("p (a h i) -> p a h i", a=2, h=AH)
                for a, to in enumerate((slots[:, 0, :, 0:2, :], slots[:, 1, :, 0::2, :])):
                    last = copy(to, v[:, a, :, :].unsqueeze(2).broadcast_to([P, AH, 2, AD]))
                last.then_inc(d_hi, 1)

            def move_heads(T, i):
                act.wait_ge(rp_ps, 4 * T + i + 1)
                at = 16 * (T // 2 % 2) + 8 * (i % 2) + 4 * (i // 2)
                copy(qkt[:, at:at + 4, (T % 2) * P:(T % 2 + 1) * P],
                     bank[6 + i % 2][:].rearrange("p (c n) -> p c n", c=4)).then_inc(d_qkt, 1)

            def stage_d():
                act.wait_ge(d_zero, 1)
                values(0, 2)
                values(1, 3)
                fold_outputs((0, 1))
                rounded(0)
                fold_outputs((2, 3))
                rounded(1)
                for T in range(2):
                    for i in range(4):
                        move_heads(T, i)
                for k in range(AH * B + 5):
                    b, i = k // AH, k % AH
                    n = k - 5
                    if n >= 0 and n % 2:
                        act.wait_ge(d_pt, n + 1)
                        if n >= 2:
                            act.wait_ge(d_av, n - 1)
                        copy(ptd[:, n % 2, :], bank[2 + n % 2][:, 0:384]).then_inc(d_eva, 1)
                    if k < AH * B:
                        n = k
                        act.wait_ge(d_max, n + 1)
                        if n >= 5:
                            act.wait_ge(d_pt, n - 4)
                        for s in range(2):
                            o, w = (0, P) if s == 0 else (P, 2 * P)
                            last = act.activation(pd[:, n % 5, o:o + w], ns_d[:, n % 3, o:o + w], ACT.Exp,
                                                  bias=nmin_d[:, n % 5, s:s + 1], scale=-1.0,
                                                  accum_out=sum_d[:, n % 5, s:s + 1])
                        last.then_inc(d_exp, 1)
                    T = 2 * b + 2
                    if i == 1 and 1 <= b < B:
                        move_heads(T - 1, 2)
                        move_heads(T - 1, 3)
                    if T < TILES:
                        if i == 3:
                            values(T, 7)
                        if i == 4:
                            rounded(T)
                        if i in (7, 9):
                            move_heads(T, i - 7)
                            move_heads(T, i - 6)
                        if i == 12:
                            rounded(T + 1)
                        if i == 13:
                            values(T + 1, 7)
                        if i == 15:
                            move_heads(T + 1, 0)
                            move_heads(T + 1, 1)
                    if k == 5:
                        norm_moves(2, 1)
                    if k == 3 * AH + 5:
                        norm_moves(3, 0)
                    if k == 3 * AH + 7:
                        turn_context()
                    for m in QUERY_STEPS.get(k - 1 - 3 * AH, ()):
                        latent_queries(0, m, 6 + m % 2)

            def latent_queries(b, m, b_):
                act.wait_ge(qc_ps, 8 * b + m + 1)
                copy(qc[b % 2][:, m, :], bank[b_][:, 0:S]).then_inc(qc_done, 1)

            def stage_e():
                for k in range(MH * B + 7):
                    n = k - 4
                    if 0 <= n < MH * B and n % 2:
                        act.wait_ge(e_pt, n + 1)
                        if n >= 2:
                            act.wait_ge(e_av, n - 1)
                        copy(pte[:, n % 2, :], bank[2 + n % 2][:]).then_inc(e_eva, 1)
                    if k < MH * B:
                        n = k
                        act.wait_ge(e_max, n + 1)
                        if n >= 4:
                            act.wait_ge(e_pt, n - 3)
                        for s in range(2):
                            last = act.activation(pe_[:, n % 4, s * S:(s + 1) * S], bank[n % 2][:, s * S:(s + 1) * S],
                                                  ACT.Exp, bias=nmax_e[:, n % 4, s:s + 1],
                                                  accum_out=sum_e[:, n % 4, s:s + 1])
                        last.then_inc(e_exp, 1)
                    b, i = (k - 1) // MH, (k - 1) % MH
                    if k and i % 2 and b + 1 < B:
                        latent_queries(b + 1, i // 2, 7)
                    n = k - 6
                    if 0 <= n < MH * B and n % 4 == 3:
                        g = n // 4
                        act.wait_ge(e_av, n + 1)
                        if g >= 8:
                            act.wait_ge(y_ready, 4 * TILES + 2 * (g // 4 - 1))
                        copy(ctx_lat_t[:, g // 4 % 2, 2 * (g % 4):2 * (g % 4) + 2, :],
                             bank[4 + g % 2][:].rearrange("p (a n) -> p a n", a=2)).then_inc(e_ctx, 1)
                    if k in (5, 7):
                        norm_moves(3, 1, (k // 2 - 2,), (6, 6))
                    if k == MH + 3:
                        act.wait_ge(y_ready, 4 * TILES)
                        expert_weights(0)
                    if k == 3 * MH + 7:
                        norm_moves(4, 0)
                expert_weights(1)

            def expert_weights(e):
                act.wait_ge(slot_ld[e % 4], 16 * (e // 4 + 1))
                if e == 2:
                    act.wait_ge(y_ready, 5 * TILES)
                if e >= 3:
                    act.wait_ge(m_y, 2 * (UNITS.index((e - 3, 1)) + 1))
                copy(w_hi[e % 3].rearrange("p a b n -> p (a b n)"), MW[:, (e % 4) * 1536:(e % 4 + 1) * 1536])\
                    .then_inc(m_w_hi, 1)

            def gate(p):
                act.wait_ge(gap_ready, p + 1)
                g = gap[:, TPP * p:TPP * (p + 1)]
                act.activation(g, g, ACT.Exp).then_inc(gap_exp, 1)

            def expert_in(u):
                e, p = UNITS[u]
                for mc in range(2):
                    n = 2 * u + mc
                    act.wait_ge(m_h, n + 1)
                    if n >= 2:
                        act.wait_ge(m_g, n - 1)
                    act.activation(silu_m[:, n % 2, :], bank[n % 2][:], ACT.Silu).then_inc(m_silu, 1)
                if u >= 2:
                    act.wait_ge(m_y, 2 * (u - 1))
                for mc in range(2):
                    n = 2 * u + mc
                    act.wait_ge(m_g, n + 1)
                    copy(g_hi[:, n % 4, :], gm[:, n % 2, :]).then_inc(m_g_hi, 1)
                if u in (1, 3) or u >= 4 and p == 0 and e + 2 < NE:
                    expert_weights(e + 2 if u >= 4 else 2 + u // 2)

            stage_a(0)
            stage_a(1)
            weight_abs()
            linear_out(0)
            for step in range(TPP + 1):
                node_features(0, step)
            neighbour_rows(0)
            linear_out(1)
            stage_b()
            stage_c(0)
            norm_moves(1, 1)
            stage_c(1)
            norm_moves(2, 0)
            stage_d()
            stage_e()
            expert_in(0)
            norm_moves(4, 1)
            gate(0)
            expert_in(1)
            for u in range(2, len(UNITS)):
                expert_in(u)
                if u == 2:
                    gate(1)

        @block.vector
        def _(dve):
            links = [0]

            def link(ins):
                links[0] += 1
                ins.then_inc(dve_link, 1)
                dve.wait_ge(dve_link, links[0])

            def gat_weights():
                dve.wait_ge(ld["ga"], 16)
                dve.wait_ge(ld["wg0"], 16)
                dve.wait_ge(ld["wg1"], 16)
                for step, (w, rows, first) in enumerate(((wg0[:, :], CTX, 0), (wg1[:, 0, :], P, 2), (wg1[:, 1, :], P, 2))):
                    for k in range(2):
                        t = prod_tmp[0:rows, :]
                        link(dve.tensor_tensor(t, w[:, 0:GH * GO], a_bc[0:rows, first + k, :], ALU.mult))
                        for o in (GH * GO,) if k == 0 else (GF, GF + 32):
                            last = dve.tensor_reduce(w[:, o:o + GH], t.rearrange("p (h o) -> p h o", h=GH), AX.X, ALU.add)
                        link(last)
                    if rows == CTX or step == 2:
                        dve.sem_inc(wg_done, 1)

            def residual(L, p, half):
                if L and half == 0:
                    dve.wait_ge(x_ready, (L - 1) * TILES + TPP * (p + 1))
                for tt in (2 * half, 2 * half + 1):
                    T = TPP * p + tt
                    dve.wait_ge(y_ready, L * TILES + T - tt % 2 + 2)
                    b_ = {0: (6, 7), 1: (6, 7), 2: (4, 5), 3: (6, 6), 4: (6, 6)}[L][half]
                    y = bank[b_][:, (tt % 2) * D:(tt % 2 + 1) * D]
                    if L == 2:
                        dve.scalar_tensor_tensor(R[:, T, :], y, out_scale[:], X[:, T, :], ALU.mult, ALU.add)\
                           .then_inc(r_done, 1)
                    else:
                        dve.tensor_tensor(R[:, T, :], y, X[:, T, :], ALU.add).then_inc(r_done, 1)

            def statistics(L, p):
                if L < 5:
                    dve.wait_ge(r_done, L * TILES + TPP * (p + 1))
                for tt in range(TPP):
                    last = dve.bn_stats(stat6[:, TPP * p + tt, :], R[:, TPP * p + tt, :])
                link(last)
                for tt in range(TPP):
                    last = dve.bn_aggr(mean_var[:, TPP * p + tt, :], stat6[:, TPP * p + tt, :])
                last.then_inc(stats_ready, 1)

            def norm_stats(L, p):
                if L < 5:
                    residual(L, p, 0)
                    residual(L, p, 1)
                statistics(L, p)

            def norm_scale(L, p):
                dve.wait_ge(rstd_ready, 2 * L + p + 1)
                dve.wait_ge(stats_ready, 2 * L + p + 1)
                for tt in range(TPP):
                    T = TPP * p + tt
                    dve.tensor_scalar(X[:, T, :], R[:, T, :], mean_var[:, T, 0:1], rstd[:, T:T + 1],
                                      ALU.subtract, ALU.mult).then_inc(x_ready, 1)

            def norm(L, p):
                norm_stats(L, p)
                norm_scale(L, p)

            def stage_a(p):
                def source(i):
                    return bank[i][:] if i < 2 else bank[i][:, 0:D]

                for k in range(7):
                    if k < 6:
                        n = 6 * p + k
                        dve.wait_ge(q_ps if k < 2 else kv_ps, (2 * p + k + 1) if k < 2 else (TPP * p + k - 1))
                        if k >= 2:
                            dve.wait_ge(v_done, TPP * p + k - 1)
                        if n >= 3:
                            dve.wait_ge(f_done, n - 2)
                        w = 512 if k < 2 else D
                        dve.tensor_scalar(fmin[:, n % 3, 0:w], source(k), 0.0, None, ALU.min).then_inc(f_min, 1)
                    if k >= 1:
                        i = k - 1
                        n = 6 * p + i
                        dve.wait_ge(f_exp, n + 1)
                        w = 512 if i < 2 else D
                        o = qf[p][:, i, :] if i < 2 else kf[p][:, i - 2, :]
                        dve.scalar_tensor_tensor(o, source(i), 0.0, fmin[:, n % 3, 0:w], ALU.max, ALU.add)\
                           .then_inc(f_done, 1)

            def linear_attention(p):
                if p == 0:
                    dve.wait_ge(ld["block"], 16)
                else:
                    dve.wait_ge(nd_ps, TPP)
                for j in range(2):
                    dve.wait_ge(kva_ps, 2 * p + j + 1)
                    for c in range(2):
                        last = dve.tensor_tensor(kvm[:, j, c, :], bank[6 + j][:, c * NV:(c + 1) * NV],
                                                 block_mask[:], ALU.mult)
                    last.then_inc(kvm_done, 1)
                if p:
                    dve.wait_ge(a_tok_done, TPP)
                for tt in range(TPP):
                    n = TPP * p + tt
                    dve.wait_ge(nd_ps, n + 1)
                    if n >= 2:
                        dve.wait_ge(at_ps, n - 1)
                    num_den = bank[tt][:, 0:2 * NV].rearrange("p (c n) -> p c n", c=2)
                    d = a_den[:, tt, :, :]
                    link(dve.tensor_scalar(d, num_den[:, :, P:NV], 1e-6, None, ALU.add))
                    link(dve.reciprocal(d, d))
                    for c in range(2):
                        last = dve.tensor_tensor(a_tok[:, n % 2, c * P:(c + 1) * P].rearrange("p (h i) -> p h i", i=AD),
                                                 num_den[:, c, 0:P].rearrange("p (h i) -> p h i", i=AD),
                                                 d[:, c, :].unsqueeze(2).broadcast_to([P, 8, AD]), ALU.mult)
                    last.then_inc(a_tok_done, 1)

            def gat_mask(lp):
                p = lp % 2
                dve.wait_ge(x_ready, TPP * (p + 1))
                if lp >= 2:
                    dve.wait_ge(b_e, 16 * (lp - 1))
                link(dve.tensor_scalar(mask[lp % 2][:, :, :], X[:, TPP * p:TPP * (p + 1), :], 1.0, -1e10,
                                       ALU.subtract, ALU.mult))

            def split_rows(lp):
                dve.wait_ge(tr_done, lp + 1)
                rest = trow[lp % 2][32:TR, :]
                dve.scalar_tensor_tensor(rest, bank[6][32:TR, :], -1.0, rest.bitcast(F32), ALU.mult, ALU.subtract)\
                   .then_inc(trow_done, 1)

            def stage_b():
                for k in range(GN + 9):
                    if k % 16 == 13 and k // 16 < 3:
                        split_rows(k // 16 + 1)
                    n = k - 2
                    if 0 <= n < GN:
                        dve.wait_ge(b_exp, n + 1)
                        dve.reciprocal(sum_b[:, n % 4, :], sum_b[:, n % 4, :]).then_inc(b_rec, 1)
                    if k < GN and k % 16 == 0:
                        gat_mask(k // 16)
                    if k < GN:
                        n, lp, h, j = k, k // 16, k // 2, k % 2
                        if k == 0:
                            dve.wait_ge(ft_done, TPP)
                        dve.wait_ge(b_tc, h + 1)
                        dve.wait_ge(b_a2, n + 1)
                        if n >= 2:
                            dve.wait_ge(b_e, n - 1)
                        for s in range(2):
                            last = dve.scalar_tensor_tensor(
                                nl[:, n % 2, s * S:(s + 1) * S], tneg[:, h % 2, j * S:(j + 1) * S],
                                sneg[lp % 2][:, 2 * j + s, h % GH:h % GH + 1], a2[:, n % 2, s * S:(s + 1) * S],
                                ALU.add, ALU.min)
                        last.then_inc(b_lr, 1)
                        dve.wait_ge(b_lr, n + 1)
                        if n >= 2:
                            dve.wait_ge(b_exp, n - 1)
                        for s in range(2):
                            last = dve.tensor_tensor_reduce(eb[:, n % 2, s * S:(s + 1) * S], nl[:, n % 2, s * S:(s + 1) * S],
                                                            mask[lp % 2][:, 2 * j + s, :], 1.0, BIG, ALU.add, ALU.min,
                                                            nmax_b[:, n % 4, s:s + 1])
                        last.then_inc(b_e, 1)
                    n = k - 6
                    if 0 <= n < GN and n // 2 % 4 == 3:
                        lp, g, j = n // 16, n // 8 % 2, n % 2
                        f = 4 * lp + 2 * g + j
                        dve.wait_ge(b_av, n + 1)
                        if f >= 2:
                            dve.wait_ge(b_h, f - 1)
                        ps = bank[4 + 2 * g + j][:, 0:S]
                        bias = gbias[:, 2 * (lp // 2) + g:2 * (lp // 2) + g + 1]
                        dve.tensor_scalar(g_v[:, j, :], ps, bias, 0.0, ALU.add, ALU.max)
                        dve.tensor_scalar(g_m[:, j, :], ps, bias, 0.0, ALU.add, ALU.min).then_inc(b_m, 1)
                    n = k - 8
                    if 0 <= n < GN and n // 2 % 4 == 3:
                        lp, g, j = n // 16, n // 8 % 2, n % 2
                        f = 4 * lp + 2 * g + j
                        dve.wait_ge(b_em, f + 1)
                        dve.wait_ge(b_m, f + 1)
                        dve.scalar_tensor_tensor(ht[lp % 2][:, g, j * S:(j + 1) * S], g_m[:, j, :], -1.0, g_v[:, j, :],
                                                 ALU.add, ALU.add).then_inc(b_h, 1)
                    if k == GN + 3:
                        x_rest(0, (4, 5))
                    if k == 2:
                        norm_stats(0, 1)
                    if k == 5:
                        norm_scale(0, 1)
                    if k in (4, 7, 9):
                        ternary_weights((4, 7, 9).index(k))
                    if k == 48 + 11:
                        norm_stats(1, 0)
                    if k == 48 + 14:
                        norm_scale(1, 0)

            def weight_scales():
                dve.wait_ge(sum_ps, 1)
                for dst, f in ((half_scale, 0.5), (neg_half, -0.5), (full_scale, 1.0)):
                    last = dve.tensor_scalar(dst[:], bank[5][:, 0:3], f / (HID * D), None, ALU.mult)
                last.then_inc(sums_done, 1)

            def ternary_weights(i):
                w, n = raw[i], raw[i].shape[1]
                if i == 0:
                    dve.wait_ge(sums_done, 1)
                    dve.tensor_tensor(out_scale[:], full_scale[:, 1:2], full_scale[:, 2:3], ALU.mult)
                if i == 2:
                    dve.wait_ge(quant, 1)
                    link(dve.tensor_scalar(below[i % 2][:, 0:n], w, neg_half[:, i:i + 1], None, ALU.is_lt))
                else:
                    dve.wait_ge(below_done, i + 1)
                dve.scalar_tensor_tensor(carve(ternary, 2 * HP * i, n), w, half_scale[:, i:i + 1],
                                         below[i % 2][:, 0:n], ALU.is_gt, ALU.subtract).then_inc(quant, 1)

            def context_rope():
                dve.wait_ge(ld["ctxr"], 16)
                dve.wait_ge(ld["mrope"], 16)
                kv, hf = KVR[:, :, 0, :], CTX // 2
                dve.wait_ge(y_ready, 3 * TILES)
                for s in range(2):
                    dve.tensor_tensor(kv_cos[:, s::2, :], kv[:, s::2, :],
                                      mrope[:, 0, s, :].unsqueeze(1).broadcast_to([P, B, CTX]), ALU.mult)
                    for a in range(2):
                        last = dve.tensor_tensor(kv_sin[:, s::2, a * hf:(a + 1) * hf], kv[:, s::2, (1 - a) * hf:(2 - a) * hf],
                                                 mrope[:, 1, s, a * hf:(a + 1) * hf].unsqueeze(1).broadcast_to([P, B, hf]),
                                                 ALU.mult)
                link(last)
                for a in range(2):
                    last = dve.tensor_tensor(KVR[:, :, a, :], kv_cos[:, :, :], kv_sin[:, :, :], ALU.add)
                last.then_inc(kvr_done, 1)

            def x_rest(p, banks=(6, 7)):
                for c in range(2):
                    dve.wait_ge(xt_ready, 2 * p + c + 1)
                    dve.tensor_tensor(xl[p][:, c, :], bank[banks[c]][:], xh[p][:, c, :].bitcast(F32), ALU.subtract)\
                       .then_inc(xl_ready, 1)

            def stage_c(p):
                if p == 0:
                    dve.wait_ge(y_ready, 2 * TILES)
                else:
                    dve.wait_ge(y_ready, 2 * TILES + TPP)
                for k in range(HC + 1):
                    n = HC * p + k
                    if k < HC:
                        dve.wait_ge(c_silu, n + 1)
                        if n >= 2:
                            dve.wait_ge(c_lo, n - 1)
                        dve.tensor_tensor(hg[:, n % 2, :], silu_c[:, n % 2, :], bank[2 + n % 2][:], ALU.mult)\
                           .then_inc(c_g, 1)
                    if p == 0 and k == 1:
                        norm_scale(1, 1)
                    if p == 1 and k == 2:
                        statistics(2, 0)
                    if p == 1 and k == 5:
                        norm_scale(2, 0)
                    if k:
                        dve.wait_ge(c_hi, n)
                        dve.wait_ge(c_g, n)
                        dve.tensor_tensor(hg_lo[:, k - 1, :], hg[:, (n - 1) % 2, :], hg_hi[:, k - 1, :].bitcast(F32),
                                          ALU.subtract).then_inc(c_lo, 1)

            def rotate(T, b_):
                def heads(v):
                    return v.rearrange("p (a h i) -> p a h i", a=2, h=AH)

                def table(cs, lo, hi):
                    return rope[:, cs, T % 2, :, lo:hi].unsqueeze(2).broadcast_to([P, 2, AH, hi - lo])
                qk, hf = heads(bank[b_][:]), AD // 2
                dve.wait_ge(d_qk_ps, T + 1)
                if T:
                    dve.wait_ge(d_rope, T)
                dve.tensor_tensor(heads(t1), qk, table(0, 0, AD), ALU.mult)
                for a in range(2):
                    last = dve.tensor_tensor(heads(t2)[:, :, :, a * hf:(a + 1) * hf],
                                             qk[:, :, :, (1 - a) * hf:(2 - a) * hf],
                                             table(1, a * hf, (a + 1) * hf), ALU.mult)
                last.then_inc(d_t1, 1)
                dve.wait_ge(d_t1, T + 1)
                if T >= 2:
                    dve.wait_ge(d_hi, T - 1)
                    dve.wait_ge(d_lo, T - 1)
                dve.tensor_tensor(roped[:, T % 2, :], t1, t2, ALU.add).then_inc(d_rope, 1)

            def rest(T):
                dve.wait_ge(d_hi, T + 1)
                v = roped[:, T % 2, :].rearrange("p (a h i) -> p a h i", a=2, h=AH)
                slots = rp[:, T % 2, :].rearrange("p (a h d i) -> p a h d i", a=2, h=AH, d=4)
                for a, hi, lo in ((0, slice(0, 2), slice(2, 4)), (1, slice(0, 4, 2), slice(1, 4, 2))):
                    last = dve.tensor_tensor(slots[:, a, :, lo, :], v[:, a, :, :].unsqueeze(2).broadcast_to([P, AH, 2, AD]),
                                             slots[:, a, :, hi, :], ALU.subtract)
                last.then_inc(d_lo, 1)

            def stage_d():
                dve.wait_ge(ld["tri"], 16)
                dve.wait_ge(ld["rope"], 16)
                for T in range(2):
                    rotate(T, T)
                norm_scale(2, 1)
                for T in range(2):
                    rest(T)
                for k in range(AH * B + 7):
                    b, i = k // AH, k % AH
                    n = k - 2
                    if 0 <= n < AH * B:
                        dve.wait_ge(d_exp, n + 1)
                        dve.reciprocal(sum_d[:, n % 5, :], sum_d[:, n % 5, :]).then_inc(d_rec, 1)
                    if k < AH * B:
                        n = k
                        dve.wait_ge(d_s, n + 1)
                        if n >= 3:
                            dve.wait_ge(d_exp, n - 2)
                        for s in range(2):
                            o, w = (0, P) if s == 0 else (P, 2 * P)
                            last = dve.tensor_tensor_reduce(ns_d[:, n % 3, o:o + w], bank[n % 2][:, s * S:s * S + w],
                                                            tri[:, 2 * P - w:2 * P], 1.0, BIG, ALU.add, ALU.min,
                                                            nmin_d[:, n % 5, s:s + 1])
                        last.then_inc(d_max, 1)
                    n = k - 5
                    if 0 <= n < AH * B and n % 2 == 0:
                        dve.wait_ge(d_pt, n + 1)
                        if n >= 2:
                            dve.wait_ge(d_av, n - 1)
                        dve.tensor_copy(ptd[:, n % 2, :], bank[2 + n % 2][:, 0:384]).then_inc(d_evd, 1)
                    n = k - 7
                    if n >= 0 and n % 4 == 3:
                        g = n // 4
                        dve.wait_ge(d_av, n + 1)
                        if g >= 8:
                            dve.wait_ge(y_ready, 3 * TILES + 2 * (g // 4 - 1))
                        dve.tensor_copy(atd[:, g % 8, :], bank[4 + g % 2][:, 0:S]).then_inc(d_fin, 1)
                    T = 2 * b + 2
                    if T < TILES:
                        if i == 3:
                            rotate(T, 6)
                        if i == 5:
                            rest(T)
                        if i == 11:
                            rotate(T + 1, 7)
                        if i == 13:
                            rest(T + 1)
                    if i == 13 and 1 <= b < B:
                        residual(3, (b - 1) // 2, (b - 1) % 2)
                    if k == AH + 8:
                        context_rope()
                    if k == 2 * AH + 14:
                        statistics(3, 0)
                    if k == 3 * AH + 1:
                        norm_scale(3, 0)
            def stage_e():
                for k in range(MH * B + 6):
                    n = k - 2
                    if 0 <= n < MH * B:
                        dve.wait_ge(e_exp, n + 1)
                        dve.reciprocal(sum_e[:, n % 4, :], sum_e[:, n % 4, :]).then_inc(e_rec, 1)
                    if k < MH * B:
                        n = k
                        dve.wait_ge(e_s, n + 1)
                        if n >= 4:
                            dve.wait_ge(e_exp, n - 3)
                        dve.tensor_reduce(nmax_e[:, n % 4, :], bank[n % 2][:].rearrange("p (s n) -> p s n", s=2),
                                          AX.X, ALU.max, negate=True).then_inc(e_max, 1)
                    n = k - 4
                    if 0 <= n < MH * B and n % 2 == 0:
                        dve.wait_ge(e_pt, n + 1)
                        if n >= 2:
                            dve.wait_ge(e_av, n - 1)
                        dve.tensor_copy(pte[:, n % 2, :], bank[2 + n % 2][:]).then_inc(e_evd, 1)
                    if k % MH == MH - 1 and 1 <= k // MH < B:
                        b = k // MH - 1
                        residual(4, b // 2, b % 2)
                    if k == 0:
                        residual(3, 1, 1)
                        statistics(3, 1)
                    if k == 3:
                        norm_scale(3, 1)
                    if k == 3 * MH:
                        statistics(4, 0)
                    if k == 3 * MH + 3:
                        norm_scale(4, 0)
                    if k == 3 * MH + 9:
                        token_rest(0)
                residual(4, 1, 1)
                statistics(4, 1)

            def gate(p):
                a, b = TPP * p, TPP * (p + 1)
                dve.wait_ge(lg_ps, p + 1)
                dve.tensor_copy(logits[:, a:b, :], bank[4][:, 0:TPP * NE].rearrange("p (t e) -> p t e", e=NE))\
                   .then_inc(gap_done, 1)
                dve.wait_ge(gap_done, p + 1)
                for T in range(a, b):
                    last = dve.max(top8[:, T, :], logits[:, T, :])
                link(last)
                dve.tensor_tensor(gap[:, a:b], top8[:, a:b, 1], top8[:, a:b, 0], ALU.subtract).then_inc(gap_ready, 1)
                for T in range(a, b):
                    last = dve.max_index(top_i[:, T, :].bitcast(U32), top8[:, T, :], logits[:, T, :])
                link(last)
                link(dve.tensor_copy(top_f[:, a:b, :], top_i[:, a:b, :].bitcast(U32)))
                dve.wait_ge(gap_exp, p + 1)
                link(dve.tensor_scalar(w_first[:, a:b], gap[:, a:b], 1.0, None, ALU.add))
                link(dve.reciprocal(w_first[:, a:b], w_first[:, a:b]))
                link(dve.tensor_tensor(w_second[:, a:b], w_first[:, a:b], gap[:, a:b], ALU.mult))
                if p == 0:
                    dve.wait_ge(ld["iota"], 16)
                for T in range(a, b):
                    dve.tensor_scalar(pick1[:, T, :], iota8[:], top_f[:, T, 0:1], w_first[:, T:T + 1], ALU.is_equal, ALU.mult)
                    last = dve.tensor_scalar(pick2[:, T, :], iota8[:], top_f[:, T, 1:2], w_second[:, T:T + 1],
                                             ALU.is_equal, ALU.mult)
                link(last)
                link(dve.tensor_tensor(combine[:, a:b, :], pick1[:, a:b, :], pick2[:, a:b, :], ALU.add))

            def expert_gates(u):
                if u >= 2:
                    dve.wait_ge(m_y, 2 * (u - 1))
                for mc in range(2):
                    n = 2 * u + mc
                    dve.wait_ge(m_silu, n + 1)
                    if n >= 2:
                        dve.wait_ge(m_g_lo, n - 1)
                    dve.tensor_tensor(gm[:, n % 2, :], silu_m[:, n % 2, :], bank[2 + n % 2][:], ALU.mult).then_inc(m_g, 1)
                for mc in range(2):
                    n = 2 * u + mc
                    dve.wait_ge(m_g_hi, n + 1)
                    dve.wait_ge(m_g, n + 1)
                    dve.tensor_tensor(g_lo[:, n % 4, :], gm[:, n % 2, :], g_hi[:, n % 4, :].bitcast(F32), ALU.subtract)\
                       .then_inc(m_g_lo, 1)

            def token_rest(p):
                for c in range(2):
                    dve.wait_ge(m_x_hi, 2 * p + c + 1)
                    dve.wait_ge(xt_ready, 12 + 2 * p + c + 1)
                    dve.tensor_tensor(x_lo[p][:, c, :], XT[:, c, p * PT:(p + 1) * PT], x_hi[p][:, c, :].bitcast(F32),
                                      ALU.subtract).then_inc(m_x_lo, 1)

            def expert_sum(u):
                e, p = UNITS[u]
                for tt in range(TPP):
                    T, n = TPP * p + tt, TPP * u + tt
                    dve.wait_ge(m_y, 2 * u + tt // 2 + 1)
                    if e:
                        dve.wait_ge(m_acc, TPP * UNITS.index((e - 1, p)) + tt + 1)
                    else:
                        dve.wait_ge(x_ready, 4 * TILES + T + 1)
                    dve.scalar_tensor_tensor(R[:, T, :], bank[4 + 2 * (u % 2) + tt // 2][:, (tt % 2) * D:(tt % 2 + 1) * D],
                                             combine[:, T, e:e + 1], (R if e else X)[:, T, :], ALU.mult, ALU.add)\
                       .then_inc(m_acc, 1)

            stage_a(0)
            dve.wait_ge(ld["sel"], 16)
            dve.tensor_copy(sel_r[:], sel[:]).then_inc(casts_ready, 1)
            dve.wait_ge(consts_ready, 1)
            gat_weights()
            stage_a(1)
            linear_attention(0)
            dve.wait_ge(ld["x"], 16)
            norm_stats(0, 0)
            weight_scales()
            split_rows(0)
            linear_attention(1)
            norm_scale(0, 0)
            dve.wait_ge(ld["gb"], 16)
            stage_b()
            norm_stats(1, 1)
            stage_c(0)
            x_rest(1)
            residual(2, 0, 0)
            residual(2, 0, 1)
            stage_c(1)
            norm_stats(2, 1)
            stage_d()
            stage_e()
            norm_scale(4, 1)
            expert_gates(0)
            token_rest(1)
            gate(0)
            expert_gates(1)
            expert_sum(0)
            for u in range(2, len(UNITS)):
                expert_gates(u)
                if u == 2:
                    gate(1)
                expert_sum(u - 1)
                if u == len(UNITS) - 1:
                    dve.wait_ge(m_acc, TPP * u)
                    norm(5, 0)
            expert_sum(len(UNITS) - 1)
            dve.wait_ge(m_acc, TPP * len(UNITS))
            norm(5, 1)

        @block.gpsimd
        def _(pool):
            links = [0]

            def link(ins):
                links[0] += 1
                ins.then_inc(pool_link, 1)
                pool.wait_ge(pool_link, links[0])

            def inverse_std(L, p):
                a, b = TPP * p, TPP * (p + 1)
                pool.wait_ge(stats_ready, 2 * L + p + 1)
                if L:
                    pool.wait_ge(rstd_ready, 2 * (L - 1) + p + 1)
                link(pool.tensor_scalar(veps[:, a:b], mean_var[:, a:b, 1], LN_EPS, None, ALU.add))
                pool.tensor_tensor(rstd[:, a:b], veps[:, a:b], minus_half[:], ALU.pow).then_inc(rstd_ready, 1)

            for p in range(NPAIR):
                pool.memset(vo[p][:, :, :, P:NV], 1.0)
            pool.memset(minus_half[:], -0.5)
            pool.memset(wg0[:, GF + GH:GF + 32], 0.0)
            pool.memset(wg1[:, :, GF + GH:GF + 32], 0.0)
            pool.memset(ones[:], 1.0).then_inc(consts_ready, 1)
            inverse_std(0, 0)
            pool.wait_ge(sums_done, 1)
            for i, w in enumerate(raw[0:2]):
                pool.tensor_scalar(below[i % 2][:, 0:w.shape[1]], w, neg_half[:, i:i + 1], 1.0, ALU.is_lt, ALU.mult)\
                    .then_inc(below_done, 1)

            def fifth(n):
                h, j = n // 2, n % 2
                pool.wait_ge(b_tc, h + 1)
                if n >= 2:
                    pool.wait_ge(b_lr, n - 1)
                for s in range(2):
                    last = pool.tensor_scalar(a2[:, n % 2, s * S:(s + 1) * S], tneg[:, h % 2, j * S:(j + 1) * S],
                                              sneg[n // 16 % 2][:, 2 * j + s, h % GH:h % GH + 1], 0.2, ALU.add, ALU.mult)
                last.then_inc(b_a2, 1)

            fifth(0)
            for k in range(GN + 3):
                if k + 1 < GN:
                    fifth(k + 1)
                n = k - 2
                if 0 <= n < GN:
                    pool.wait_ge(b_rec, n + 1)
                    for s in range(2):
                        w = pb[:, n % 4, s * S:(s + 1) * S]
                        last = pool.tensor_scalar(w, w, sum_b[:, n % 4, s:s + 1], 1.0, ALU.mult, ALU.mult)
                    last.then_inc(b_norm, 1)
                if k == 3:
                    inverse_std(0, 1)
                if k == 48 + 11:
                    inverse_std(1, 0)
            inverse_std(1, 1)
            pool.wait_ge(y_ready, 2 * TILES)
            pool.memset(vp, 0.0).then_inc(d_zero, 1)
            inverse_std(2, 0)
            inverse_std(2, 1)

            def divide(first, end, reciprocals, divided, probs, sums, ring, spans):
                for n in range(first, end):
                    pool.wait_ge(reciprocals, n + 1)
                    for s, (a, b) in enumerate(spans):
                        w = probs[:, n % ring, a:b]
                        last = pool.tensor_scalar(w, w, sums[:, n % ring, s:s + 1], 1.0, ALU.mult, ALU.mult)
                    last.then_inc(divided, 1)

            def expert_weights(e, part=0, parts=1):
                pool.wait_ge(m_w_hi, e + 1)
                n = 1536 // parts
                a, b, at = part * n, (part + 1) * n, (e % 4) * 1536
                last = pool.tensor_tensor(w_lo[e % 3].rearrange("p a b n -> p (a b n)")[:, a:b], MW[:, at + a:at + b],
                                          w_hi[e % 3].rearrange("p a b n -> p (a b n)")[:, a:b].bitcast(F32), ALU.subtract)
                if part == parts - 1:
                    last.then_inc(m_w_lo, 1)

            divide(0, 3 * AH - 2, d_rec, d_norm, pd, sum_d, 5, ((0, P), (P, 3 * P)))
            inverse_std(3, 0)
            divide(3 * AH - 2, B * AH, d_rec, d_norm, pd, sum_d, 5, ((0, P), (P, 3 * P)))
            inverse_std(3, 1)
            first = 0
            for part in range(3):
                end = MH + 7 + 3 * part
                divide(first, end, e_rec, e_norm, pe_, sum_e, 4, ((0, S), (S, 2 * S)))
                expert_weights(0, part, 3)
                first = end
            divide(first, 3 * MH, e_rec, e_norm, pe_, sum_e, 4, ((0, S), (S, 2 * S)))
            inverse_std(4, 0)
            divide(3 * MH, B * MH, e_rec, e_norm, pe_, sum_e, 4, ((0, S), (S, 2 * S)))
            expert_weights(1)
            inverse_std(4, 1)
            for e in range(2, NE):
                expert_weights(e)
            for p in range(NPAIR):
                inverse_std(5, p)


INPUTS = ("x x_t ctx_rows ctx_t wa gat_w0 gat_w1 gat_a gat_b ffn1 ffn3 ffn2 wd_qkv wd_o m_q m_kcq m_qr m_kr "
          "m_kckv m_o gate_w moe c_ident c_block c_tri c_rope c_mrope c_sel c_iota").split()


def constants():
    ident = np.eye(P, dtype=np.float32)
    blocks = np.kron(np.eye(P // AD), np.ones((AD, AD))).astype(np.float32)
    tri = np.where(np.triu(np.ones((P, P)), 1) > 0, np.float32(-NEG), np.float32(0)).astype(np.float32)
    tri = np.concatenate([np.zeros((P, P), np.float32), tri], 1)
    inv = (1.0 / 10000.0 ** (np.arange(0, AD, 2, dtype=np.float32) / AD)).astype(np.float32)
    f = np.einsum("i,j->ij", np.arange(S, dtype=np.float32), inv)
    f = np.concatenate((f, f), axis=-1)
    sign = np.where(np.arange(AD) < AD // 2, -1.0, 1.0).astype(np.float32)
    cs = np.stack([np.cos(f), np.sin(f) * sign]).astype(np.float32).reshape(2, 2, P, AD)
    rope = np.stack([cs * np.float32(-AD ** -0.5), cs], axis=3).transpose(2, 0, 1, 3, 4)
    inv = (1.0 / 10000.0 ** (np.arange(0, CTX, 2, dtype=np.float32) / CTX)).astype(np.float32)
    f = (np.arange(S, dtype=np.float32)[:, None] * inv[None, :]).astype(np.float32)
    sign = np.where(np.arange(CTX) < CTX // 2, -1.0, 1.0).astype(np.float32)
    cs = np.stack([np.repeat(np.cos(f), 2, -1), np.repeat(np.sin(f), 2, -1) * sign]).astype(np.float32)
    mrope = cs.reshape(2, 2, P, CTX).transpose(2, 0, 1, 3)
    sel = np.zeros((TR, GH, P), np.float32)
    for h in range(GH):
        sel[h, h, :] = sel[32 + h, h, :] = 1.0
    iota = np.broadcast_to(np.arange(NE, dtype=np.float32), (P, NE))
    return dict(c_ident=ident, c_block=np.concatenate([blocks, blocks[:, ::AD]], 1), c_tri=tri, c_rope=rope,
                c_mrope=mrope, c_sel=sel, c_iota=iota)


def lay_out(i):
    def chunks(w, rows=P):
        return w.reshape(-1, rows, w.shape[-1]).transpose(1, 0, 2)

    def zeros_like_rows(n, w):
        return np.zeros((n, w.shape[-1]), w.dtype)
    x = i["x"].reshape(B * S, D)
    c = i["ctx_512"].reshape(B * S, CTX)
    a = dict(x=chunks(x), x_t=chunks(x.T), ctx_rows=chunks(c), ctx_t=c.T)
    a["wa"] = np.concatenate([chunks(i["L0_attn_Wq"].T).reshape(P, -1),
                              chunks(np.concatenate([i["L0_attn_Wk"].T, i["L0_attn_Wv"].T], 1)).reshape(P, -1),
                              chunks(i["L0_attn_Wo"].T).reshape(P, -1)], 1)
    a["gat_w0"] = i["L0_xattn_W0"].transpose(1, 0, 2).reshape(CTX, GH * GO)
    a["gat_w1"] = chunks(i["L0_xattn_W1"].transpose(1, 0, 2).reshape(D, GH * GO))
    a["gat_a"] = np.stack([i["L0_xattn_" + n].reshape(-1) for n in ("a_self0", "a_neigh0", "a_self1", "a_neigh1")])
    a["gat_b"] = np.concatenate([i["L0_xattn_b0"].reshape(2, P).T, i["L0_xattn_b1"].reshape(2, P).T], 1)
    for n in (1, 3):
        w = i[f"L0_ffn_w{n}"]
        a[f"ffn{n}"] = chunks(np.concatenate([w, zeros_like_rows(HP - HID, w)], 0).T).reshape(P, -1)
    w2 = i["L0_ffn_w2"].T
    a["ffn2"] = chunks(np.concatenate([w2, zeros_like_rows(HP - HID, w2)], 0)).reshape(P, -1)
    a["wd_qkv"] = chunks(np.concatenate([i["L1_attn_" + n].T for n in ("Wq", "Wk", "Wv")], 1)).reshape(P, -1)
    wo = i["L1_attn_Wo"].T.reshape(AH, AD, D)
    wo = np.concatenate([wo, np.zeros((AH, 32 - AD, D), wo.dtype)], 1)
    a["wd_o"] = chunks(wo.reshape(AH * 32, D)).reshape(P, -1)
    a["m_q"] = i["L1_xattn_Wq"].reshape(MH, MK, D).transpose(1, 0, 2).reshape(MK, MH * D)
    a["m_kcq"] = i["L1_xattn_w_kc_q"].transpose(2, 0, 1).reshape(2, QCH, MH, MK).transpose(1, 0, 2, 3)
    a["m_qr"] = i["L1_xattn_W_qr"].transpose(2, 0, 1)
    a["m_kr"] = i["L1_xattn_W_kr"].transpose(2, 0, 1)
    a["m_kckv"] = i["L1_xattn_w_kc_kv"].transpose(1, 0, 2)
    a["m_o"] = i["L1_xattn_Wo"].T.reshape(MH, MK, D).transpose(1, 0, 2)
    a["gate_w"] = chunks(i["L1_ffn_gate_kernel"])
    a["moe"] = np.concatenate([i["L1_ffn_" + n].reshape(NE, 2, P, D).transpose(2, 0, 1, 3).reshape(P, NE, 2 * D)
                               for n in ("wi_0", "wi_1", "wo")], 2)
    return a


def kernel(**inputs):
    import concourse.bacc as _bacc
    from concourse.bass_utils import run_bass_kernel_spmd as _run

    given = {k: np.asarray(v) for k, v in inputs.items()}
    arrays = {**lay_out(given), **constants()}
    nc = _bacc.Bacc("TRN2", target_bir_lowering=False, num_devices=1)
    feed, args = {}, []
    for name in INPUTS:
        a = np.ascontiguousarray(arrays[name])
        feed[name + "_dram"] = a
        args.append(nc.dram_tensor(name + "_dram", a.shape, mybir.dt.from_np(a.dtype), kind="ExternalInput").ap())
    out = nc.dram_tensor("out_dram", (P, TILES, D), F32, kind="ExternalOutput").ap()
    build_decoder(nc, *args, out)
    r = _run(nc, [feed], core_ids=[0])
    y = r.results[0]["out_dram"]
    return y.transpose(1, 0, 2).reshape(B, S, D)
```
